# Optimizing a Trainium2 kernel written in Bass

```python
import numpy as np
import jax
import jax.numpy as jnp

def _softmax(x, axis=-1):
    return jax.nn.softmax(x, axis=axis)

def _gelu(x):
    return jax.nn.gelu(x, approximate=True)

def _silu(x):
    return jax.nn.silu(x)

def _sigmoid(x):
    return jax.nn.sigmoid(x)

def _layernorm(x, axis=-1, eps=1e-05):
    m = jnp.mean(x, axis=axis, keepdims=True)
    v = jnp.var(x, axis=axis, keepdims=True)
    return (x - m) / jnp.sqrt(v + eps)

def _scatter_add(tgt, idx, src, axis=0):
    return tgt.at[idx].add(src)

def _segment_sum(src, seg, n):
    return jax.ops.segment_sum(src, seg, n)
kernel_name = 'mk_adaln_d1_jaxref_r8_d1f5a4'

def setup_inputs(seed: int=0):
    np.random.seed(seed)
    _w = jnp.asarray

    def _L0_attn_setup():
        import jax, jax.numpy as jnp
        import numpy as np
        B, S, E = (2, 256, 256)
        NQ, NKV, HD = (16, 4, 128)
        WINDOW = 64
        ROPE_BASE = 10000.0

        def _rope(x):
            half = HD // 2
            freqs = 1.0 / ROPE_BASE ** (2.0 * jnp.arange(half, dtype=jnp.float32) / HD)
            pos = jnp.arange(x.shape[2], dtype=jnp.float32)
            ang = pos[:, None] * freqs[None, :]
            cos = jnp.cos(ang)[None, None].astype(x.dtype)
            sin = jnp.sin(ang)[None, None].astype(x.dtype)
            xe = x[..., 0::2]
            xo = x[..., 1::2]
            re = xe * cos - xo * sin
            ro = xe * sin + xo * cos
            return jnp.stack([re, ro], axis=-1).reshape(x.shape)
        key = jax.random.key(seed)
        ks = jax.random.split(key, 9)
        s_in = 1.0 / np.sqrt(E)
        s_out = 1.0 / np.sqrt(NQ * HD)
        return {'x': jax.random.normal(ks[0], (B, S, E), jnp.float32), 'Wq': jax.random.normal(ks[1], (E, NQ * HD), jnp.float32) * s_in, 'bq': jax.random.normal(ks[2], (NQ * HD,), jnp.float32) * 0.01, 'Wk': jax.random.normal(ks[3], (E, NKV * HD), jnp.float32) * s_in, 'bk': jax.random.normal(ks[4], (NKV * HD,), jnp.float32) * 0.01, 'Wv': jax.random.normal(ks[5], (E, NKV * HD), jnp.float32) * s_in, 'bv': jax.random.normal(ks[6], (NKV * HD,), jnp.float32) * 0.01, 'Wo': jax.random.normal(ks[7], (NQ * HD, E), jnp.float32) * s_out, 'bo': jax.random.normal(ks[8], (E,), jnp.float32) * 0.01}
    _L0_attn_in = _L0_attn_setup()

    def _L0_ffn_setup():
        import jax, jax.numpy as jnp
        import numpy as np
        E, TOPK, H, I = (8, 2, 256, 512)
        SOFTCAP = 30.0
        key = jax.random.key(seed)
        ks = jax.random.split(key, 5)
        s = 1.0 / np.sqrt(H)
        si = 1.0 / np.sqrt(I)
        return {'hidden_states': jax.random.normal(ks[0], (4, 256, H), jnp.float32), 'w_gate': jax.random.normal(ks[1], (H, E), jnp.float32) * s, 'w1': jax.random.normal(ks[2], (E, H, I), jnp.float32) * s, 'w3': jax.random.normal(ks[3], (E, H, I), jnp.float32) * s, 'w2': jax.random.normal(ks[4], (E, I, H), jnp.float32) * si}
    _L0_ffn_in = _L0_ffn_setup()
    _L0_c = _w((lambda *s: np.random.randn(*s).astype(np.float32) * 0.05)(2, 256))
    _L0_wmod = _w((lambda *s: np.random.randn(*s).astype(np.float32) * 0.05)(256, 6 * 256) * 256 ** (-0.5))
    _d = {'L0_attn_x': _L0_attn_in['x'], 'L0_attn_Wq': _L0_attn_in['Wq'], 'L0_attn_bq': _L0_attn_in['bq'], 'L0_attn_Wk': _L0_attn_in['Wk'], 'L0_attn_bk': _L0_attn_in['bk'], 'L0_attn_Wv': _L0_attn_in['Wv'], 'L0_attn_bv': _L0_attn_in['bv'], 'L0_attn_Wo': _L0_attn_in['Wo'], 'L0_attn_bo': _L0_attn_in['bo'], 'L0_ffn_w_gate': _L0_ffn_in['w_gate'], 'L0_ffn_w1': _L0_ffn_in['w1'], 'L0_ffn_w3': _L0_ffn_in['w3'], 'L0_ffn_w2': _L0_ffn_in['w2'], 'L0_c': _L0_c, 'L0_wmod': _L0_wmod}
    _x0 = _d['L0_attn_x']
    _d['L0_attn_x'] = jax.random.normal(jax.random.fold_in(jax.random.key(seed), 1), (2, 1024, 256), dtype=_x0.dtype)
    del _x0
    return _d

def reference(L0_attn_x, L0_attn_Wq, L0_attn_bq, L0_attn_Wk, L0_attn_bk, L0_attn_Wv, L0_attn_bv, L0_attn_Wo, L0_attn_bo, L0_ffn_w_gate, L0_ffn_w1, L0_ffn_w3, L0_ffn_w2, L0_c, L0_wmod):

    def _L0_attn_ref(x, Wq, bq, Wk, bk, Wv, bv, Wo, bo):
        import jax, jax.numpy as jnp
        import numpy as np
        B, S, E = (2, 256, 256)
        NQ, NKV, HD = (16, 4, 128)
        WINDOW = 64
        ROPE_BASE = 10000.0

        def _rope(x):
            half = HD // 2
            freqs = 1.0 / ROPE_BASE ** (2.0 * jnp.arange(half, dtype=jnp.float32) / HD)
            pos = jnp.arange(x.shape[2], dtype=jnp.float32)
            ang = pos[:, None] * freqs[None, :]
            cos = jnp.cos(ang)[None, None].astype(x.dtype)
            sin = jnp.sin(ang)[None, None].astype(x.dtype)
            xe = x[..., 0::2]
            xo = x[..., 1::2]
            re = xe * cos - xo * sin
            ro = xe * sin + xo * cos
            return jnp.stack([re, ro], axis=-1).reshape(x.shape)
        b, s, _ = x.shape
        q = (x @ Wq + bq).reshape(b, s, NQ, HD).transpose(0, 2, 1, 3)
        k = (x @ Wk + bk).reshape(b, s, NKV, HD).transpose(0, 2, 1, 3)
        v = (x @ Wv + bv).reshape(b, s, NKV, HD).transpose(0, 2, 1, 3)
        q = _rope(q)
        k = _rope(k)
        rep = NQ // NKV
        k = jnp.repeat(k, rep, axis=1)
        v = jnp.repeat(v, rep, axis=1)
        scores = jnp.einsum('bhqd,bhkd->bhqk', q, k) / np.sqrt(HD)
        i = jnp.arange(s)[:, None]
        j = jnp.arange(s)[None, :]
        allowed = (j <= i) & (i - j <= WINDOW)
        scores = jnp.where(allowed[None, None], scores, -jnp.inf)
        weights = jax.nn.softmax(scores, axis=-1)
        out = jnp.einsum('bhqk,bhkd->bhqd', weights, v)
        out = out.transpose(0, 2, 1, 3).reshape(b, s, NQ * HD)
        return out @ Wo + bo

    def _L0_ffn_ref(hidden_states, w_gate, w1, w3, w2):
        import jax, jax.numpy as jnp
        import numpy as np
        E, TOPK, H, I = (8, 2, 256, 512)
        SOFTCAP = 30.0
        orig_shape = hidden_states.shape
        x = hidden_states.reshape(-1, H)
        logits = x @ w_gate
        logits = SOFTCAP * jnp.tanh(logits / SOFTCAP)
        probs = jax.nn.softmax(logits, axis=-1)
        _, idx = jax.lax.top_k(probs, TOPK)
        mask = jax.nn.one_hot(idx, E, dtype=probs.dtype).sum(-2)
        weights = probs * mask
        out = jnp.zeros_like(x)
        for e in range(E):
            h = jax.nn.silu(x @ w1[e]) * (x @ w3[e])
            out = out + h @ w2[e] * weights[:, e:e + 1]
        return out.reshape(orig_shape)
    x = L0_attn_x
    mod = (_silu(L0_c) @ L0_wmod).reshape(L0_c.shape[0], 6, 1, -1)
    sa, ca, ga, sb, cb, gb = (mod[:, 0], mod[:, 1], mod[:, 2], mod[:, 3], mod[:, 4], mod[:, 5])
    ga = (2 * (ga >= 0) - 1) * jnp.maximum(jnp.abs(ga), 0.25)
    gb = (2 * (gb >= 0) - 1) * jnp.maximum(jnp.abs(gb), 0.25)
    h = _layernorm(x, axis=-1) * (1 + ca) + sa
    x = x + ga * _L0_attn_ref(h, L0_attn_Wq, L0_attn_bq, L0_attn_Wk, L0_attn_bk, L0_attn_Wv, L0_attn_bv, L0_attn_Wo, L0_attn_bo)
    h = _layernorm(x, axis=-1) * (1 + cb) + sb
    x = x + gb * _L0_ffn_ref(h, L0_ffn_w_gate, L0_ffn_w1, L0_ffn_w3, L0_ffn_w2)
    return x

_drawn_inputs = setup_inputs


def setup_inputs(seed=0):
    import zlib

    import numpy as np

    out = dict(_drawn_inputs(seed))
    spreads = {}
    factors = {'L0_attn_bq': 64.0, 'L0_attn_bk': 64.0, 'L0_attn_bv': 8.0, 'L0_attn_bo': 22.808}
    for name, (base, spread) in spreads.items():
        noise = np.random.default_rng([zlib.crc32(name.encode()), seed]).standard_normal(out[name].shape)
        drawn = base * np.exp(spread * noise) if base else spread * noise
        out[name] = jnp.asarray(drawn.astype(out[name].dtype))
    for name, factor in factors.items():
        out[name] = (out[name] * factor).astype(out[name].dtype)
    return out
```

```python
import math
from contextlib import ExitStack

import numpy as np

import concourse.bass as bass
from concourse import mybir
from concourse.alu_op_type import AluOpType as ALU

B, S, E = 2, 1024, 256
NQ, NKV, HD = 16, 4, 128
HG = NQ // NKV
WINDOW = 64
NX, TOPK, INNER = 8, 2, 512
SOFTCAP, EPS = 30.0, 1e-5
P = 128
EC = E // P
TILES = S // P
ALL = B * TILES
TOKENS = B * S
HALF = TILES // 2
W_SCALE = 64.0
P_SCALE = 64.0
K_SCALE = 1.0 / math.sqrt(HD)
MASKED = -1e30

REGION = TOKENS + P
ROWS = NX * REGION + P
UNUSED_ROW = NX * REGION
SLOTS = 40
ROW = 2 * E + 2
SKIP = TOPK * TOKENS

UNITS = TILES * NKV
FIRST_SLOT, LAST_SLOT = -11, 50
Q_AHEAD = 6


def ring_entries():
    at = {}
    for i, pair in enumerate([[("ln", 0, 0), ("ln", 0, 1)]]
                             + [[("k", 0, 2 * i), ("k", 0, 2 * i + 1)] for i in range(2)]
                             + [[("v", 0, 2 * i), ("v", 0, 2 * i + 1)] for i in range(2)]
                             + [[("q", 2 * i, 0), ("q", 2 * i + 1, 0)] for i in range(3)]):
        at[i - 9 if i else -10] = pair
    for k in range(UNITS - Q_AHEAD):
        at[k] = [("q", k + Q_AHEAD, 0)]
    for c in range(EC):
        at[3 + c].append(("ln", 1, c))
    for i in range(4):
        at[8 + i].append(("k", 1, i))
        at[12 + i].append(("v", 1, i))
    for h in range(2):
        for d, e in ((23, ("lt", h, 0)), (24, ("lt", h, 1)), (26, ("lg", h, 0)), (29, ("rk", h, 0))):
            at.setdefault(16 * h + d, []).append(e)
    return at


RING = ring_entries()
ORDER = [e for k in sorted(RING) for e in RING[k]]
ENTRIES = len(ORDER)
NTH = {e: n for n, e in enumerate(ORDER)}
ROPED = [e for e in ORDER if e[0] in "qk"]
SPLIT = [e for e in ORDER if e[0] in ("q", "k", "ln")]
NROPED, NSPLIT = len(ROPED), len(SPLIT)
NZ, NA = 3, 4

SMALL_IN = 16 * 17
POOL_READY = 7
STEPS_BATCH = 58


def layer_kernel(nc, x, wq, bq, wk, bk, wv, bv, wo, bo, w_gate, w1, w3, w2, c_t, wmod,
                 cos_t, sin_t, mask_t, ident, ident16, identb, lower, tokens, bases, reverse, slot_nos, out):
    f32, f16, b16, i32, u32, u16 = (mybir.dt.float32, mybir.dt.float16, mybir.dt.bfloat16,
                                    mybir.dt.int32, mybir.dt.uint32, mybir.dt.uint16)
    ACT = mybir.ActivationFunctionType
    X = mybir.AxisListType.X
    routed = nc.dram_tensor("routed", [ROWS, ROW], f16).ap()
    results = nc.dram_tensor("results", [TOPK * TOKENS, E], f32).ap()

    with ExitStack() as ctx:
        def sb(name, shape, dt):
            return ctx.enter_context(nc.sbuf_tensor(name, shape, dt))

        def sem(name):
            return ctx.enter_context(nc.semaphore(name))

        PER_X = 6 * 1024
        region = sb("region", [P, NX * PER_X], f16)
        taken = [0]

        def carve(cols):
            at = taken[0]
            taken[0] += cols
            assert taken[0] <= NX * PER_X
            return region[:, at:at + cols]

        wq_s = carve(2 * EC * NQ * HD).rearrange("p (s c n) -> p s c n", s=2, c=EC)
        wk_s = carve(2 * EC * NKV * HD).rearrange("p (s c n) -> p s c n", s=2, c=EC)
        wv_s = carve(2 * EC * NKV * HD).rearrange("p (s c n) -> p s c n", s=2, c=EC)
        wo_s = carve(2 * NQ * E).rearrange("p (s h n) -> p s h n", s=2, h=NQ)
        KEYS = WINDOW + S
        keys_at = taken[0]
        keys = carve(NKV * 2 * KEYS).rearrange("p (g s n) -> p g s n", g=NKV, s=2)
        vals_flat = carve(2 * TILES * NKV * HD)
        vals = vals_flat.rearrange("p (s t n) -> p s t n", s=2, t=TILES)
        valx_flat = carve(2 * TILES * NKV * HD)
        valx = valx_flat.rearrange("p (s t n) -> p s t n", s=2, t=TILES)
        cos_s = carve(2 * S).bitcast(f32)
        masks = carve(2 * 512).bitcast(b16).rearrange("p (a n) -> p a n", a=2)
        wq_f = valx_flat.bitcast(f32).rearrange("p (c n) -> p c n", c=EC)
        wk_f = vals_flat[:, 0:2048].bitcast(f32).rearrange("p (c n) -> p c n", c=EC)
        wv_f = vals_flat[:, 2048:4096].bitcast(f32).rearrange("p (c n) -> p c n", c=EC)

        x_s = sb("x_s", [P, ALL, E], f32)
        hT = sb("hT", [P, 2, EC, S], f16)
        q_s = sb("q_s", [P, 2, 2, TILES, HG, 64], f16)
        att = sb("att", [P, 2, 2, HG, P], f16)
        exps = sb("exps", [P, 2, 4, P], f32)
        probs = sb("probs", [P, 2, 4, P], f32)
        pT = sb("pT", [P, 2, 2, 512], f16)
        zrot = sb("zrot", [P, NZ, 512], f32)
        arot = sb("arot", [P, NA, 512], f32)
        sin_s = sb("sin_s", [P, S], f32)
        ident_f = sb("ident_f", [P, P], f32)
        ident_b = sb("ident_b", [P, P], b16)
        ident_h = sb("ident_h", [P, P], f16)
        lower_h = sb("lower_h", [P, P], f16)
        ones_h = sb("ones_h", [P, P], f16)
        stage = sb("stage", [P, 2, 1024], f32)
        xn = sb("xn", [P, HALF, E], f32)
        h2T = sb("h2T", [P, 2, 512], f32)
        pay = sb("pay", [P, HALF, ROW], f16)
        pad = sb("pad", [P, ROW], f16)
        gates = sb("gates", [P, 4, B, E], f32)
        ga_bo = sb("ga_bo", [P, B, E], f32)
        mod_c = sb("mod_c", [P, 4, B], f32)
        bias_c = sb("bias_c", [P, NQ + 2 * NKV], f32)
        c_s = sb("c_s", [P, EC, B], f32)
        silu_c = sb("silu_c", [P, EC, B], f32)
        stats = sb("stats", [P, HALF, 6], f32)
        mean_var = sb("mean_var", [P, HALF, 2], f32)
        var_eps = sb("var_eps", [P, HALF], f32)
        power = sb("power", [P, HALF], f32)
        rstd = sb("rstd", [P, HALF], f32)
        neg_max = sb("neg_max", [P, 2, 4], f32)
        row_sum = sb("row_sum", [P, 2, 4], f32)
        inv_sum = sb("inv_sum", [P, 2, 4], f32)
        wg_s = sb("wg_s", [P, EC, NX], f32)
        G = [P, HALF, NX]
        logit, capped, shifted, eg, key, one1, one2, tmp, place = (
            sb(n, G, f32) for n in ("logit", "capped", "shifted", "eg", "key", "one1", "one2", "tmp", "place"))
        best, gsum, ginv, gw, gplace = (
            sb(n, [P, HALF], f32) for n in ("best", "gsum", "ginv", "gw", "gplace"))
        chosen = sb("chosen", [P, HALF + 1, NX], f16)
        used_rows = sb("used_rows", [P, NX], f32)
        base_s = sb("base_s", [P, NX], f32)
        rev_s = sb("rev_s", [P, NX], f32)
        weight = sb("weight", [P, TOPK, ALL], f32)
        rows_i = sb("rows_i", [P, TOPK, HALF], i32)
        tok_s = sb("tok_s", [P, TOPK, ALL], i32)

        x_rows = arot[:, :, :].rearrange("p a n -> p (a n)").bitcast(f16)[:, 0:4 * ROW].rearrange(
            "p (a n) -> p a n", a=4)
        q_flat = q_s[:, :, :, :, :, :].rearrange("p a s t h q -> p (a s t h q)")
        xT = q_flat[:, 0:1024].rearrange("p (a n) -> p a n", a=2)
        silu_g = q_flat[:, 1024:3072].bitcast(f32).rearrange("p (a n) -> p a n", a=2)
        inner = q_flat[:, 3072:5120].bitcast(f32).rearrange("p (a n) -> p a n", a=2)
        innerT = q_flat[:, 5120:7168].rearrange("p (a s n) -> p a s n", a=2, s=2)
        y_s = q_flat[:, 7168:8192].bitcast(f32).rearrange("p (a n) -> p a n", a=2)
        xstage = hT[:, :, :, :].rearrange("p s c n -> p (s c n)").bitcast(f32)[:, 0:2048].rearrange(
            "p (a n) -> p a n", a=2)
        NST = 4

        def xst(m):
            return stage[:, m % NST, :] if m % NST < 2 else xstage[:, m % NST - 2, :]

        counts = sb("counts", [P, NX], f32)
        counts_i = sb("counts_i", [P, NX], i32)
        xtiles = sb("xtiles", [P, NX], f32)
        scan = sb("scan", [P, 4, 2 * NX], f32)
        slot_no = sb("slot_no", [P, SLOTS], f32)
        slot_i = sb("slot_i", [P, SLOTS], i32)
        after = zrot[:, 0, 0:SLOTS * NX].rearrange("p (s x) -> p s x", x=NX)
        slot_x = sb("slot_x", [P, SLOTS], f32)
        slot_row = sb("slot_row", [P, SLOTS], f32)
        slot_t = sb("slot_t", [P, SLOTS], f32)
        slot_u = sb("slot_u", [P, SLOTS], f32)
        slot_xi = sb("slot_xi", [P, SLOTS], i32)
        slot_ri = sb("slot_ri", [P, SLOTS], i32)
        tiles_i = sb("tiles_i", [P, NX], i32)
        mix = region[:, 8192:8192 + 4 * E * 2].bitcast(f32).rearrange("p (a t n) -> p a t n", a=2, t=2)
        pair = region[:, 0:2 * 2 * 2 * E * 2].bitcast(f32).rearrange("p (a k t n) -> p a k t n", a=2, k=TOPK, t=2)

        def bank(name):
            return ctx.enter_context(nc.psum_tensor(name, [P, 512], f32))

        ring = [bank("ring0"), bank("ring1")]
        score = [bank("score0"), bank("score1")]
        t_ps = bank("t_ps")
        o_ps = bank("o_ps")
        y_ps = [bank("y0"), bank("y1")]

        wmod_s = q_flat[:, 0:6144].bitcast(f32).rearrange("p (c n) -> p c n", c=EC)
        wide_c = probs[:, :, :, :].rearrange("p a j n -> p (a j n)")[:, 0:EC * B * P].rearrange(
            "p (c b n) -> p c b n", c=EC, b=B) if 2 * 4 * P >= EC * B * P else None
        sign = zrot[:, 0, :]
        absol = zrot[:, 1, :]
        x_flat = x_s[:, :, :].rearrange("p t n -> p (t n)")
        gates_flat = gates[:, :, :, :].rearrange("p v b n -> p v (b n)")
        ga_bo_flat = ga_bo[:, :, :].rearrange("p b n -> p (b n)")
        weight_flat = weight[:, :, :]
        pay_place = pay[:, :, 2 * E:ROW].bitcast(i32)
        vals_of = {0: valx, 1: vals}

        s_c_in = sem("c_in")
        s_wmod_in = sem("wmod_in")
        s_small_in = sem("small_in")
        s_wkv_in = sem("wkv_in")
        s_wq_in = sem("wq_in")
        s_silu_done = sem("silu_done")
        s_wide_done = sem("wide_done")
        s_mod_cols = sem("mod_cols")
        s_mod_wide = sem("mod_wide")
        s_ready = sem("ready")
        s_gates_ready = sem("gates_ready")
        s_scaled_bias = sem("scaled_bias")
        s_wkv_hi = sem("wkv_hi")
        s_wkv_lo = sem("wkv_lo")
        s_wq_hi = sem("wq_hi")
        s_wq_lo = sem("wq_lo")
        s_wo_hi = sem("wo_hi")
        s_wo_lo = sem("wo_lo")
        s_pool_ready = sem("pool_ready")
        s_variance = sem("variance")
        s_rstd_done = sem("rstd_done")
        s_normed = sem("normed")
        s_ring_filled = sem("ring_filled")
        s_ring_freed = sem("ring_freed")
        s_swapped = sem("swapped")
        s_turned = sem("turned")
        s_rotated = sem("rotated")
        s_split_hi = sem("split_hi")
        s_split_lo = sem("split_lo")
        s_val_hi = sem("val_hi")
        s_residual = sem("residual")
        s_scored = sem("scored")
        s_maxed = sem("maxed")
        s_exped = sem("exped")
        s_summed = sem("summed")
        s_normalized = sem("normalized")
        s_probs_t = sem("probs_t")
        s_pT_hi = sem("pT_hi")
        s_pT_lo = sem("pT_lo")
        s_att_ps = sem("att_ps")
        s_att_hi = sem("att_hi")
        s_att_lo = sem("att_lo")
        s_projected = sem("projected")
        s_y_taken = sem("y_taken")
        s_y_done = sem("y_done")
        s_h2_done = sem("h2_done")
        s_pay_hi = sem("pay_hi")
        s_pay_lo = sem("pay_lo")
        s_capped_s = sem("capped_s")
        s_shifted_s = sem("shifted_s")
        s_gate_exp = sem("gate_exp")
        s_placed = sem("placed")
        s_place_set = sem("place_set")
        s_routed_rows = sem("routed_rows")
        s_rows_ready = sem("rows_ready")
        s_slots_ready = sem("slots_ready")
        s_pads_written = sem("pads_written")
        s_vector_step = sem("vector_step")
        s_pool_step = sem("pool_step")
        s_expert_hi = sem("expert_hi")
        s_expert_lo = sem("expert_lo")
        s_xT_ps = sem("xT_ps")
        s_xT_done = sem("xT_done")
        s_up_ps = sem("up_ps")
        s_gate_ps = sem("gate_ps")
        s_silu_g_done = sem("silu_g_done")
        s_inner_done = sem("inner_done")
        s_innerT_ps = sem("innerT_ps")
        s_innerT_hi = sem("innerT_hi")
        s_innerT_lo = sem("innerT_lo")
        s_down_ps = sem("down_ps")
        s_y_out = sem("y_out")
        s_first_done = sem("first_done")
        s_mixed = sem("mixed")
        s_summed_up = sem("summed_up")
        s_out_written = sem("out_written")
        s_x_in = [sem(f"x_in{i}") for i in range(4)]
        s_wo_in = [sem(f"wo_in{i}") for i in range(2)]
        s_stage_in = [sem(f"stage_in{i}") for i in range(4)]
        s_slot_in = [sem(f"slot_in{i}") for i in range(4)]
        s_y_written = [sem(f"y_written{i}") for i in range(2)]
        s_pair_in = [sem(f"pair_in{i}") for i in range(2)]
        s_vals_crossed = [sem(f"vals_crossed{i}") for i in range(2)]
        block = ctx.enter_context(nc.Block())

        def slot_list():
            return range(FIRST_SLOT, LAST_SLOT + 1)

        def batch_over(eng, b):
            eng.wait_ge(s_ring_freed, b * ENTRIES)
            eng.wait_ge(s_placed, b * 2)
            eng.wait_ge(s_gate_exp, b * 2)
            eng.wait_ge(s_routed_rows, b * 2 * 2 * HALF * 16)

        def tail_at(k, d):
            return next((h for h in range(2) if k == 16 * h + d), None)

        SPLIT_AT = {e: n for n, e in enumerate(SPLIT)}
        ROPED_AT = {e: n for n, e in enumerate(ROPED)}

        def bias_of(e):
            kind, i, j = e
            return (i % 16) // 4 * HG + i % 4 if kind == "q" else NQ + j

        def dest(e, s):
            kind, i, j = e
            src = arot[:, SPLIT_AT[e] % NA, :]
            if kind == "q":
                return (q_s[:, i // 4 % 2, s, :, i % 4, :], src.rearrange("p (t q) -> p t q", q=64))
            if kind == "k":
                return keys[:, j, s, WINDOW + 512 * i:WINDOW + 512 * (i + 1)], src
            return hT[:, s, j, 512 * i:512 * (i + 1)], src

        @block.sync
        def _(sp):
            sp.dma_start(c_s[:, :, :], c_t).then_inc(s_c_in, 16)
            x_v = x.rearrange("(t p) n -> p t n", p=P)
            sp.dma_start(x_s[:, 0:HALF, :], x_v[:, 0:HALF, :]).then_inc(s_x_in[0], 16)
            sp.dma_start(ident_f[:, :], ident).then_inc(s_small_in, 16)
            sp.dma_start(wmod_s, wmod.rearrange("(c p) n -> p c n", p=P)).then_inc(s_wmod_in, 16)
            sp.dma_start(wk_f, wk.rearrange("(c p) n -> p c n", p=P)).then_inc(s_wkv_in, 16)
            sp.dma_start(wv_f, wv.rearrange("(c p) n -> p c n", p=P)).then_inc(s_wkv_in, 16)
            sp.dma_start(wq_f, wq.rearrange("(c p) n -> p c n", p=P)).then_inc(s_wq_in, 16)
            for dst, src in ((bias_c[:, 0:NQ], bq), (bias_c[:, NQ:NQ + NKV], bk),
                             (bias_c[:, NQ + NKV:NQ + 2 * NKV], bv), (cos_s[:, :], cos_t), (sin_s[:, :], sin_t),
                             (masks[:, :, :].bitcast(u16), mask_t), (ident_h[:, :], ident16), (ident_b[:, :].bitcast(u16), identb),
                             (lower_h[:, :], lower), (tok_s[:, :, :], tokens), (base_s[:, :], bases),
                             (rev_s[:, :], reverse), (slot_no[:, :], slot_nos),
                             (wg_s[:, :, :], w_gate.rearrange("(c p) n -> p c n", p=P)),
                             (ga_bo[:, 0, :], bass.AP(bo.tensor, 0, [[0, P], [1, E]])),
                             (ga_bo[:, 1, :], bass.AP(bo.tensor, 0, [[0, P], [1, E]]))):
                sp.dma_start(dst, src).then_inc(s_small_in, 16)
            for t in range(1, ALL // HALF):
                sp.dma_start(x_s[:, t * HALF:(t + 1) * HALF, :],
                             x_v[:, t * HALF:(t + 1) * HALF, :]).then_inc(s_x_in[t], 16)
            for i in range(4):
                if i >= 2:
                    sp.wait_ge(s_wo_lo, i - 1)
                sp.dma_start(stage[:, i % 2, :].rearrange("p (h n) -> p h n", h=4),
                             wo[4 * i * HD:4 * (i + 1) * HD, :].rearrange("(h p) n -> p h n", p=P)
                             ).then_inc(s_wo_in[i % 2], 16)
            sp.wait_ge(s_pool_ready, POOL_READY)
            for b in range(B):
                for h in range(2):
                    sp.wait_ge(s_ring_freed, b * ENTRIES + NTH[("v", h, 3)] + 1)
                    lo, hi = h * HALF, (h + 1) * HALF
                    for s in range(2):
                        sp.dma_start(valx[0:64, s, lo:hi, :], vals[0:64, s, lo:hi, :]
                                     ).then_inc(s_vals_crossed[h], 16)
                        up = min(hi, TILES - 1)
                        sp.dma_start(valx[64:P, s, lo + 1:up + 1, :], vals[64:P, s, lo:up, :]
                                     ).then_inc(s_vals_crossed[h], 16)
            batch_over(sp, B)

            def load_expert(m):
                e, w = m // 3, m % 3
                if m >= NST:
                    sp.wait_ge(s_expert_lo, m - NST + 1)
                src = ((w1, w3)[w][e].rearrange("(c p) n -> p c n", p=P) if w < 2
                       else w2[e].rearrange("(c p) n -> p c n", p=P))
                sp.dma_start(xst(m).rearrange("p (c n) -> p c n", c=EC if w < 2 else INNER // P),
                             src).then_inc(s_stage_in[m % NST], 16)

            for m in range(NST):
                load_expert(m)
            sp.wait_ge(s_pool_ready, POOL_READY)
            sp.dma_start(routed[UNUSED_ROW:UNUSED_ROW + P, :], pad[:, :]).then_inc(s_pads_written, 16)
            sp.wait_ge(s_rows_ready, 1)
            for e in range(NX):
                row = nc.sync.value_load(counts_i[0:1, e:e + 1], min_val=0, max_val=ROWS - P)
                sp.dma_start(routed[bass.ds(row, P), :], pad[:, :]).then_inc(s_pads_written, 16)
            for m in range(NST, 3 * NX):
                load_expert(m)
            sp.wait_ge(s_pads_written, 16 * (NX + 1))
            sp.wait_ge(s_slots_ready, 1)

            def load_slot(i, a, first):
                row = nc.sync.value_load(slot_ri[0:1, bass.ds(i * 4 + a, 1)] if not isinstance(i, int)
                                         else slot_ri[0:1, a:a + 1], min_val=0, max_val=ROWS - P)
                if not first:
                    sp.wait_ge(s_y_written[a % 2], (i * 2 + a // 2 - 1) * 16)
                sp.dma_start(x_rows[:, a, :], routed[bass.ds(row, P), :]).then_inc(s_slot_in[a], 16)

            for a in range(4):
                load_slot(0, a, True)
            with sp.Fori(1, SLOTS // 4) as i:
                for a in range(4):
                    load_slot(i, a, False)
            for a in range(2):
                sp.wait_ge(s_y_written[a], SLOTS // 2 * 16)
            res_v = results.rearrange("(k t p) n -> p k t n", k=TOPK, p=P)
            out_v = out.rearrange("(t p) n -> p t n", p=P)
            for n in range(ALL // 2):
                if n >= 2:
                    sp.wait_ge(s_mixed, n - 1)
                for k in range(TOPK):
                    sp.dma_start(pair[:, n % 2, k, :, :], res_v[:, k, 2 * n:2 * n + 2, :]
                                 ).then_inc(s_pair_in[n % 2], 16)
                if n >= 1:
                    sp.wait_ge(s_summed_up, n)
                    sp.dma_start(out_v[:, 2 * n - 2:2 * n, :], x_s[:, 2 * n - 2:2 * n, :]
                                 ).then_inc(s_out_written, 16)
            sp.wait_ge(s_summed_up, ALL // 2)
            sp.dma_start(out_v[:, ALL - 2:ALL, :], x_s[:, ALL - 2:ALL, :]).then_inc(s_out_written, 16)
            sp.wait_ge(s_out_written, 16 * (ALL // 2))

        @block.tensor
        def _(pe):
            mm = nc.tensor.matmul

            def three(out_ap, lhs, rhs, first, last):
                mm(out_ap, lhs(0), rhs(0), start=first, stop=False)
                mm(out_ap, lhs(0), rhs(1), start=False, stop=False)
                return mm(out_ap, lhs(1), rhs(0), start=False, stop=last)

            pe.wait_ge(s_wmod_in, 16)
            pe.wait_ge(s_silu_done, 1)
            for v in range(4):
                for c in range(EC):
                    last = mm(score[0][:, B * v:B * (v + 1)], wmod_s[:, c, v * P:(v + 1) * P], silu_c[:, c, :],
                              start=(c == 0), stop=(c == EC - 1))
            last.then_inc(s_mod_cols, 1)
            pe.wait_ge(s_wide_done, 1)
            for bb in range(B):
                for half in range(2):
                    for c in range(EC):
                        last = mm((t_ps, o_ps, y_ps[0], y_ps[1])[2 * bb + half][:, :], wide_c[:, c, bb, :],
                                  wmod_s[:, c, 512 * (half + 1):512 * (half + 2)],
                                  start=(c == 0), stop=(c == EC - 1))
            last.then_inc(s_mod_wide, 1)
            pe.wait_ge(s_small_in, SMALL_IN)
            pe.wait_ge(s_wkv_lo, 2)
            pe.wait_ge(s_pool_ready, POOL_READY)

            def entry(b, e):
                kind, i, j = e
                n = NTH[e]
                bank = ring[n % 2]
                if n >= 2:
                    pe.wait_ge(s_ring_freed, b * ENTRIES + n - 1)
                if kind == "ln":
                    pe.wait_ge(s_normed, b * 4 + i + 1)
                    for t in range(HALF):
                        last = nc.tensor.transpose(bank[:, t * P:(t + 1) * P], xn[:, t, j * P:(j + 1) * P],
                                                   ident_f[:, :])
                elif kind in "kq":
                    half = i if kind == "k" else i // 16
                    cols = slice(half * 512, (half + 1) * 512)
                    if kind == "k":
                        w, at = wk_s, j * HD
                    else:
                        w, at = wq_s, ((i % 16) // 4 * HG + i % 4) * HD
                        if i == 0:
                            pe.wait_ge(s_wq_lo, 2 * EC)
                    pe.wait_ge(s_split_lo, b * NSPLIT + SPLIT_AT[("ln", half, 1)] + 1)
                    for c in range(EC):
                        last = three(bank[:, :], lambda s: w[:, s, c, at:at + HD],
                                     lambda s: hT[:, s, c, cols], c == 0, c == EC - 1)
                elif kind == "v":
                    rows = slice((i * HALF + j) * P, (i * HALF + j + 1) * P)
                    pe.wait_ge(s_split_lo, b * NSPLIT + SPLIT_AT[("ln", i, 1)] + 1)
                    for c in range(EC):
                        last = three(bank[:, :], lambda s: hT[:, s, c, rows], lambda s: wv_s[:, s, c, :],
                                     c == 0, c == EC - 1)
                elif kind == "lt":
                    pe.wait_ge(s_h2_done, b * 2 + i + 1)
                    for t in range(2):
                        for c in range(EC):
                            last = nc.tensor.transpose(bank[:, (2 * t + c) * P:(2 * t + c + 1) * P],
                                                       xn[:, 2 * j + t, c * P:(c + 1) * P], ident_f[:, :])
                elif kind == "lg":
                    pe.wait_ge(s_ring_freed, b * ENTRIES + NTH[("lt", i, 1)] + 1)
                    for t in range(HALF):
                        for c in range(EC):
                            at = (2 * (t % 2) + c) * P
                            last = mm(bank[:, t * NX:(t + 1) * NX], h2T[:, t // 2, at:at + P], wg_s[:, c, :],
                                      start=(c == 0), stop=(c == EC - 1))
                else:
                    pe.wait_ge(s_shifted_s, b * 2 + i + 1)
                    width = (HALF + 1) * NX
                    mm(bank[:, 0:width], lower_h[:, :], chosen[:, :, :].rearrange("p t n -> p (t n)"),
                       start=True, stop=False)
                    for t in range(HALF):
                        m = HALF - t
                        last = mm(bank[:, (t + 1) * NX:width].rearrange("p (t n) -> p t n", n=NX), ones_h[:, :],
                                  chosen[:, t:t + 1, :].to_broadcast([P, m, NX]), start=False, stop=(m == 1))
                last.then_inc(s_ring_filled, 1)

            def where(k):
                return k // 16, k // 4 % 4, HALF * (k // 16) + k % 4

            def scores(b, k):
                h, g, t = where(k)
                if k >= 2:
                    pe.wait_ge(s_exped, b * UNITS + k - 1)
                if k % 4 == 0:
                    need = max(SPLIT_AT[("q", k + 3, 0)], SPLIT_AT[("k", h, 3)])
                    pe.wait_ge(s_split_lo, b * NSPLIT + need + 1)
                bank = score[k % 2]
                mm(bank[:, :], ident_b[:, :], masks[:, 1 if t == 0 else 0, :], start=True, stop=False)
                for blk in range(2):
                    for hp in range(2):
                        cols = bank[:, (2 * blk + hp) * P:(2 * blk + hp + 1) * P]

                        def kk(s):
                            if blk:
                                at = WINDOW + t * P
                                return keys[:, g, s, at:at + P]
                            v = keys[:, g, s, 0:P]
                            return bass.AP(v.tensor, v.offset + WINDOW + t * P,
                                           [list(v.ap[0]), [-WINDOW, 2], [1, WINDOW]])

                        def qq(s):
                            return q_s[:, k // 4 % 2, s, 2 * (t % HALF) + blk, 2 * hp:2 * hp + 2, :].rearrange(
                                "p h q -> p (h q)")
                        mm(cols, qq(0), kk(0), start=False, stop=False)
                        mm(cols, qq(0), kk(1), start=False, stop=False)
                        last = mm(cols, qq(1), kk(0), start=False, stop=(blk == 1 and hp == 1))
                last.then_inc(s_scored, 1)

            def transposed(b, k):
                pe.wait_ge(s_normalized, b * UNITS + k + 1)
                if k >= 1:
                    pe.wait_ge(s_pT_lo, b * UNITS + k)
                for j in range(4):
                    last = nc.tensor.transpose(t_ps[:, j * P:(j + 1) * P], probs[:, k % 2, j, :], ident_f[:, :])
                last.then_inc(s_probs_t, 1)

            def attend(b, k):
                h, g, t = where(k)
                pe.wait_ge(s_pT_lo, b * UNITS + k + 1)
                if k >= 1:
                    pe.wait_ge(s_att_lo, b * UNITS + k)
                if k % 16 == 0:
                    pe.wait_ge(s_vals_crossed[h], (b + 1) * 64)
                o_v = o_ps[:, :].rearrange("p (h n) -> p h n", h=HG)
                for blk in range(2):
                    v = vals_of[blk]
                    last = three(o_v[:, :, blk * 64:(blk + 1) * 64],
                                 lambda s: v[:, s, t, g * HD:(g + 1) * HD],
                                 lambda s: pT[:, k % 2, s, blk * 256:(blk + 1) * 256].rearrange(
                                     "p (h n) -> p h n", h=HG), True, True)
                last.then_inc(s_att_ps, 1)

            def project(b, k):
                h, g, t = where(k)
                u = k % 4
                pe.wait_ge(s_att_lo, b * UNITS + k + 1)
                if h == 1 and g == 0 and u % 2 == 0:
                    pe.wait_ge(s_y_taken, b * 4 + 1 + u // 2)
                if k == 0:
                    pe.wait_ge(s_wo_lo, 4)
                cols = y_ps[u // 2][:, (u % 2) * E:(u % 2 + 1) * E]
                for n in range(HG):
                    for i, (sa, sw) in enumerate(((0, 0), (0, 1), (1, 0))):
                        last = mm(cols, att[:, k % 2, sa, n, :], wo_s[:, sw, g * HG + n, :],
                                  start=(g == 0 and n == 0 and i == 0 and u % 2 == 0),
                                  stop=(g == 3 and n == 3 and i == 2), skip_group_check=True)
                last.then_inc(s_projected, 1)

            for b in range(B):
                batch_over(pe, b)
                for k in slot_list():
                    if 0 <= k < UNITS:
                        scores(b, k)
                    for e in RING.get(k, ()):
                        entry(b, e)
                    if 0 <= k - 1 < UNITS:
                        transposed(b, k - 1)
                    if 0 <= k - 2 < UNITS:
                        attend(b, k - 2)
                    if 0 <= k - 3 < UNITS:
                        project(b, k - 3)

            batch_over(pe, B)
            pe.wait_ge(s_expert_lo, 3 * NX)
            pe.wait_ge(s_slots_ready, 1)
            x_ps, it_ps, d_ps = ring[0], t_ps, o_ps
            x_ps_h = x_ps[:, :].bitcast(f16)

            def rows_t(s, i, a, first):
                pe.wait_ge(s_slot_in[a], (i + 1) * 16)
                if not first:
                    pe.wait_ge(s_xT_done, s)
                for q in range(4):
                    last = nc.tensor.transpose(x_ps_h[:, q * P:(q + 1) * P], x_rows[:, a, q * P:(q + 1) * P],
                                               ident_h[:, :])
                last.then_inc(s_xT_ps, 1)

            def up(s, a, early):
                e = nc.tensor.value_load(slot_xi[0:1, bass.ds(s, 1)] if not isinstance(s, int)
                                         else slot_xi[0:1, s:s + 1], min_val=0, max_val=NX - 1)
                pe.wait_ge(s_xT_done, s + 1)
                if not early:
                    pe.wait_ge(s_inner_done, s - 1)
                for w, (bank, done) in enumerate(((score[a % 2], s_up_ps), (y_ps[a % 2], s_gate_ps))):
                    for c in range(EC):
                        last = three(bank[:, :], lambda q: xT[:, a % 2, (2 * q + c) * P:(2 * q + c + 1) * P],
                                     lambda q: region[:, bass.ds(e * PER_X + ((2 * w + q) * EC + c) * INNER, INNER)],
                                     c == 0, c == EC - 1)
                    last.then_inc(done, 1)

            def inner_t(s, a, first):
                pe.wait_ge(s_inner_done, s + 1)
                if not first:
                    pe.wait_ge(s_innerT_lo, s)
                for q in range(4):
                    last = nc.tensor.transpose(it_ps[:, q * P:(q + 1) * P], inner[:, a % 2, q * P:(q + 1) * P],
                                               ident_f[:, :])
                last.then_inc(s_innerT_ps, 1)

            def down(s, a, first):
                e = nc.tensor.value_load(slot_xi[0:1, bass.ds(s, 1)] if not isinstance(s, int)
                                         else slot_xi[0:1, s:s + 1], min_val=0, max_val=NX - 1)
                pe.wait_ge(s_innerT_lo, s + 1)
                if not first:
                    pe.wait_ge(s_y_out, s)
                for c in range(INNER // P):
                    last = three(d_ps[:, 0:E], lambda q: innerT[:, a % 2, q, c * P:(c + 1) * P],
                                 lambda q: region[:, bass.ds(e * PER_X + 4 * 1024 + q * 1024 + c * E, E)],
                                 c == 0, c == INNER // P - 1)
                last.then_inc(s_down_ps, 1)

            def slot(i, a, head):
                s = i * 4 + a
                rows_t(s, i, a, head and a == 0)
                if not head or a >= 2:
                    down(s - 2, a - 2, head and a == 2)
                if not head or a >= 1:
                    inner_t(s - 1, a - 1, head and a == 1)
                up(s, a, head and a < 2)

            for a in range(4):
                slot(0, a, True)
            with pe.Fori(1, SLOTS // 4) as i:
                for a in range(4):
                    slot(i, a, False)
            down(SLOTS - 2, 0, False)
            inner_t(SLOTS - 1, 1, False)
            down(SLOTS - 1, 1, False)

        @block.scalar
        def _(act):
            A = nc.scalar.activation
            act.wait_ge(s_c_in, 16)
            A(silu_c[:, :, :], c_s[:, :, :], ACT.Silu).then_inc(s_silu_done, 1)
            act.wait_ge(s_wkv_in, 32)
            A(wk_s[:, 0], wk_f, ACT.Copy, scale=W_SCALE * K_SCALE).then_inc(s_wkv_hi, 1)
            A(wv_s[:, 0], wv_f, ACT.Copy, scale=W_SCALE).then_inc(s_wkv_hi, 1)
            act.wait_ge(s_wq_in, 16)
            for c in range(EC):
                for n in range(2):
                    A(wq_s[:, 0, c, n * 1024:(n + 1) * 1024], wq_f[:, c, n * 1024:(n + 1) * 1024],
                      ACT.Copy, scale=W_SCALE).then_inc(s_wq_hi, 1)
            for i in range(4):
                act.wait_ge(s_wo_in[i % 2], 16 * (i // 2 + 1))
                A(wo_s[:, 0, 4 * i:4 * (i + 1), :], stage[:, i % 2, :].rearrange("p (h n) -> p h n", h=4),
                  ACT.Copy, scale=W_SCALE).then_inc(s_wo_hi, 1)
            act.wait_ge(s_scaled_bias, 1)

            def swap(b, e):
                r, n = ROPED_AT[e], NTH[e]
                act.wait_ge(s_ring_filled, b * ENTRIES + n + 1)
                if r >= NZ:
                    act.wait_ge(s_rotated, b * NROPED + r - NZ + 1)
                col = bias_of(e)
                z = zrot[:, r % NZ, :]
                bank = ring[n % 2]
                A(z[0:64], bank[64:P, :], ACT.Identity, bias=bias_c[64:P, col:col + 1])
                A(z[64:P], bank[0:64, :], ACT.Identity, bias=bias_c[0:64, col:col + 1]).then_inc(s_swapped, 1)

            for b in range(B):
                batch_over(act, b)
                for k in slot_list():
                    if 0 <= k - 2 < UNITS:
                        u = k - 2
                        act.wait_ge(s_probs_t, b * UNITS + u + 1)
                        if u >= 2:
                            act.wait_ge(s_att_ps, b * UNITS + u - 1)
                        A(pT[:, u % 2, 0, :], t_ps[:, :], ACT.Copy, scale=P_SCALE).then_inc(s_pT_hi, 1)
                    if 0 <= k - 3 < UNITS:
                        u = k - 3
                        g = u // 4 % 4
                        act.wait_ge(s_att_ps, b * UNITS + u + 1)
                        if u >= 2:
                            act.wait_ge(s_projected, b * UNITS + u - 1)
                        A(att[:, u % 2, 0].rearrange("p h n -> p (h n)"), o_ps[:, :], ACT.Identity,
                          bias=bias_c[:, NQ + NKV + g:NQ + NKV + g + 1]).then_inc(s_att_hi, 1)
                    if 0 <= k < UNITS:
                        act.wait_ge(s_maxed, b * UNITS + k + 1)
                        if k >= 2:
                            act.wait_ge(s_normalized, b * UNITS + k - 1)
                        for j in range(4):
                            last = A(exps[:, k % 2, j, :], score[k % 2][:, j * P:(j + 1) * P], ACT.Exp,
                                     bias=neg_max[:, k % 2, j:j + 1], accum_out=row_sum[:, k % 2, j:j + 1])
                        last.then_inc(s_exped, 1)
                    for e in RING.get(k, ()):
                        if e[0] in "qk":
                            swap(b, e)
                        elif e[0] == "v":
                            act.wait_ge(s_ring_filled, b * ENTRIES + NTH[e] + 1)
                            A(vals[:, 0, e[1] * HALF + e[2], :], ring[NTH[e] % 2][:, :], ACT.Copy,
                              scale=1 / W_SCALE).then_inc(s_val_hi, 1)
                    for e in RING.get(k - 1, ()):
                        if e in SPLIT_AT:
                            if e[0] == "ln":
                                act.wait_ge(s_ring_freed, b * ENTRIES + NTH[e] + 1)
                            else:
                                act.wait_ge(s_rotated, b * NROPED + ROPED_AT[e] + 1)
                            if e[0] == "q" and e[1] >= 8:
                                act.wait_ge(s_scored, b * UNITS + e[1] // 4 * 4 - 4)
                            dst, src = dest(e, 0)
                            A(dst, src, ACT.Copy).then_inc(s_split_hi, 1)
                    h = tail_at(k, 23)
                    if h is not None:
                        act.wait_ge(s_h2_done, b * 2 + h + 1)
                        act.wait_ge(s_routed_rows, (2 * b + h) * 128)
                        A(pay[:, :, 0:E], xn[:, :, :], ACT.Copy).then_inc(s_pay_hi, 1)
                    h = tail_at(k, 28)
                    if h is not None:
                        act.wait_ge(s_ring_freed, b * ENTRIES + NTH[("lg", h, 0)] + 1)
                        A(capped[:, :, :], logit[:, :, :], ACT.Tanh, scale=1 / SOFTCAP).then_inc(s_capped_s, 1)
                    h = tail_at(k, 29)
                    if h is not None:
                        act.wait_ge(s_shifted_s, b * 2 + h + 1)
                        A(eg[:, :, :], shifted[:, :, :], ACT.Exp, scale=SOFTCAP).then_inc(s_gate_exp, 1)

            batch_over(act, B)
            for m in range(3 * NX):
                act.wait_ge(s_stage_in[m % NST], 16 * (m // NST + 1))
                at = m // 3 * PER_X + m % 3 * 2048
                A(region[:, at:at + 1024], xst(m), ACT.Copy, scale=W_SCALE).then_inc(s_expert_hi, 1)

            def inner_hi(s, a, early):
                act.wait_ge(s_innerT_ps, s + 1)
                if not early:
                    act.wait_ge(s_down_ps, s - 1)
                A(innerT[:, a % 2, 0, :], t_ps[:, :], ACT.Copy).then_inc(s_innerT_hi, 1)

            def result(s, half, a, early):
                act.wait_ge(s_down_ps, s + 1)
                if not early:
                    act.wait_ge(s_y_written[a % 2], half * 16)
                A(y_s[:, a % 2, :], o_ps[:, 0:E], ACT.Copy, scale=1 / W_SCALE).then_inc(s_y_out, 1)

            def slot(i, a, head):
                s = i * 4 + a
                if not head or a >= 1:
                    inner_hi(s - 1, a - 1, head and a < 3)
                if not head or a >= 2:
                    result(s - 2, i * 2 + a // 2 - 1, a - 2, head)
                act.wait_ge(s_up_ps, s + 1)
                if not head or a >= 2:
                    act.wait_ge(s_inner_done, s - 1)
                A(silu_g[:, a % 2, :], score[a % 2][:, :], ACT.Silu, scale=1 / W_SCALE
                  ).then_inc(s_silu_g_done, 1)

            for a in range(4):
                slot(0, a, True)
            with act.Fori(1, SLOTS // 4) as i:
                for a in range(4):
                    slot(i, a, False)
            result(SLOTS - 2, SLOTS // 2 - 1, 0, False)
            inner_hi(SLOTS - 1, 1, False)
            result(SLOTS - 1, SLOTS // 2 - 1, 1, False)
            for n in range(ALL // 2):
                act.wait_ge(s_pair_in[n % 2], 32 * (n // 2 + 1))
                for t in range(2):
                    last = A(pair[:, n % 2, 0, t, :], pair[:, n % 2, 0, t, :], ACT.Copy,
                             scale=weight[:, 0, 2 * n + t:2 * n + t + 1])
                last.then_inc(s_first_done, 1)

        @block.vector
        def _(dve):
            V = nc.vector
            done = [0]

            def link(ins, b=0):
                done[0] += 1
                ins.then_inc(s_vector_step, 1)
                dve.wait_ge(s_vector_step, b * STEPS_BATCH + done[0])

            dve.wait_ge(s_silu_done, 1)
            for c in range(EC):
                last = V.tensor_copy(wide_c[:, c], silu_c[:, c, :].unsqueeze(2).to_broadcast([P, B, P]))
            last.then_inc(s_wide_done, 1)
            dve.wait_ge(s_small_in, SMALL_IN)
            V.tensor_scalar(bias_c[:, 0:NQ], bias_c[:, 0:NQ], W_SCALE, None, ALU.mult)
            V.tensor_scalar(bias_c[:, NQ:NQ + NKV], bias_c[:, NQ:NQ + NKV], W_SCALE * K_SCALE, None, ALU.mult)
            V.tensor_scalar(bias_c[:, NQ + NKV:NQ + 2 * NKV], bias_c[:, NQ + NKV:NQ + 2 * NKV], P_SCALE, None,
                            ALU.mult).then_inc(s_scaled_bias, 1)
            dve.wait_ge(s_mod_cols, 1)
            V.tensor_copy(mod_c[:, 0:2, :], score[0][:, 0:4].rearrange("p (c b) -> p c b", b=B))
            link(V.tensor_scalar(mod_c[:, 2:4, :], score[0][:, 4:8].rearrange("p (c b) -> p c b", b=B), 1.0, None,
                                 ALU.add))
            S_ = V.scalar_tensor_tensor
            dve.wait_ge(s_wkv_hi, 1)
            S_(wk_s[:, 1], wk_f, W_SCALE * K_SCALE, wk_s[:, 0], ALU.mult, ALU.subtract).then_inc(s_wkv_lo, 1)
            dve.wait_ge(s_wkv_hi, 2)
            S_(wv_s[:, 1], wv_f, W_SCALE, wv_s[:, 0], ALU.mult, ALU.subtract).then_inc(s_wkv_lo, 1)
            for c in range(EC):
                for n in range(2):
                    dve.wait_ge(s_wq_hi, 2 * c + n + 1)
                    S_(wq_s[:, 1, c, n * 1024:(n + 1) * 1024], wq_f[:, c, n * 1024:(n + 1) * 1024], W_SCALE,
                       wq_s[:, 0, c, n * 1024:(n + 1) * 1024], ALU.mult, ALU.subtract).then_inc(s_wq_lo, 1)
            for i in range(4):
                dve.wait_ge(s_wo_hi, i + 1)
                S_(wo_s[:, 1, 4 * i:4 * (i + 1), :], stage[:, i % 2, :].rearrange("p (h n) -> p h n", h=4), W_SCALE,
                   wo_s[:, 0, 4 * i:4 * (i + 1), :], ALU.mult, ALU.subtract).then_inc(s_wo_lo, 1)
            dve.wait_ge(s_mod_wide, 1)
            for bb in range(B):
                V.tensor_copy(gates[:, 0:2, bb, :], (t_ps, y_ps[0])[bb][:, :].rearrange("p (v n) -> p v n", v=2))
                last = V.tensor_copy(gates[:, 2:4, bb, :],
                                     (o_ps, y_ps[1])[bb][:, :].rearrange("p (v n) -> p v n", v=2))
            link(last)
            for v in (0, 3):
                gv = gates_flat[:, v, :]
                link(V.tensor_scalar(sign, gv, 0.0, 2.0, ALU.is_ge, ALU.mult))
                link(V.tensor_scalar(sign, sign, -1.0, None, ALU.add))
                link(S_(absol, gv, -1.0, gv, ALU.mult, ALU.max))
                link(S_(gv, absol, 0.25, sign, ALU.max, ALU.mult))
            link(V.tensor_tensor(ga_bo_flat, ga_bo_flat, gates_flat[:, 0, :], ALU.mult))
            V.tensor_scalar(gates_flat[:, 0, :], gates_flat[:, 0, :], 1 / (W_SCALE * P_SCALE), None, ALU.mult)
            V.tensor_copy(used_rows[:, :], base_s[:, :])
            V.tensor_scalar(gates_flat[:, 2, :], gates_flat[:, 2, :], 1.0, None, ALU.add
                            ).then_inc(s_gates_ready, 1)
            dve.wait_ge(s_gates_ready, 1)
            before = done[0]

            def xt(b, t, n=1):
                return x_flat[:, bass.ds(b * (TILES * E) + t * E, n * E)]

            for b in range(B):
                batch_over(dve, b)
                done[0] = 0

                def vlink(ins):
                    done[0] += 1
                    ins.then_inc(s_vector_step, 1)
                    dve.wait_ge(s_vector_step, b * STEPS_BATCH + (before + done[0]))

                def statistics(n, t0, come, value):
                    dve.wait_ge(come, value)
                    for i in range(HALF):
                        last = V.bn_stats(stats[:, i, :], xt(b, t0 + i))
                    vlink(last)
                    for i in range(HALF):
                        last = V.bn_aggr(mean_var[:, i, :], stats[:, i, :])
                    vlink(last)
                    V.tensor_scalar(var_eps[:, :], mean_var[:, :, 1], EPS, None, ALU.add).then_inc(s_variance, 1)

                def normalize(n, t0):
                    dve.wait_ge(s_rstd_done, b * 4 + n + 1)
                    for i in range(HALF):
                        last = V.tensor_scalar(xn[:, i, :], xt(b, t0 + i), mean_var[:, i, 0:1], rstd[:, i:i + 1],
                                               ALU.subtract, ALU.mult)
                    last.then_inc(s_normed, 1)

                def take(e):
                    kind, i, j = e
                    n = NTH[e]
                    bank = ring[n % 2]
                    if e in SPLIT_AT and SPLIT_AT[e] >= NA:
                        dve.wait_ge(s_split_lo, b * NSPLIT + SPLIT_AT[e] - NA + 1)
                    if kind in "kq":
                        col = bias_of(e)
                        half = i if kind == "k" else i // 16
                        dve.wait_ge(s_swapped, b * NROPED + ROPED_AT[e] + 1)
                        last = S_(arot[:, SPLIT_AT[e] % NA, :], bank[:, :], bias_c[:, col:col + 1],
                                  cos_s[:, half * 512:(half + 1) * 512], ALU.add, ALU.mult)
                    elif kind == "v":
                        dve.wait_ge(s_val_hi, b * 8 + i * HALF + j + 1)
                        t = i * HALF + j
                        last = S_(vals[:, 1, t, :], bank[:, :], 1 / W_SCALE, vals[:, 0, t, :],
                                  ALU.mult, ALU.subtract)
                    else:
                        dve.wait_ge(s_ring_filled, b * ENTRIES + n + 1)
                        if kind == "ln":
                            last = V.tensor_scalar(arot[:, SPLIT_AT[e] % NA, :], bank[:, :],
                                                   mod_c[:, 2 + j, bass.ds(b, 1)], mod_c[:, j, bass.ds(b, 1)],
                                                   ALU.mult, ALU.add)
                        elif kind == "lt":
                            last = V.tensor_copy(h2T[:, j, :], bank[:, :])
                        elif kind == "lg":
                            last = V.tensor_copy(logit[:, :, :].rearrange("p t n -> p (t n)"), bank[:, 0:HALF * NX])
                        else:
                            vlink(V.tensor_tensor(place[:, :, :], bank[:, 0:HALF * NX].rearrange(
                                "p (t n) -> p t n", n=NX), used_rows[:, :].unsqueeze(1).to_broadcast(G), ALU.add))
                            last = V.tensor_tensor(used_rows[:, :], bank[:, HALF * NX:(HALF + 1) * NX],
                                                   used_rows[:, :], ALU.add)
                    last.then_inc(s_ring_freed, 1)

                def rotate(e):
                    r, a = ROPED_AT[e], arot[:, SPLIT_AT[e] % NA, :]
                    dve.wait_ge(s_turned, b * NROPED + r + 1)
                    dve.wait_ge(s_ring_freed, b * ENTRIES + NTH[e] + 1)
                    V.tensor_tensor(a, a, zrot[:, r % NZ, :], ALU.add).then_inc(s_rotated, 1)

                def low(e):
                    dve.wait_ge(s_split_hi, b * NSPLIT + SPLIT_AT[e] + 1)
                    (hi, src), (lo, _) = dest(e, 0), dest(e, 1)
                    V.tensor_tensor(lo, src, hi, ALU.subtract).then_inc(s_split_lo, 1)

                def residual(pair_):
                    h = pair_ // 2
                    q = pair_ % 2
                    dve.wait_ge(s_projected, b * UNITS + 16 * h + 12 + 2 * q + 2)
                    dve.wait_ge(s_residual, b * TILES + 4 * h + 2 * q + 2)
                    ga2 = gates_flat[:, 0, bass.ds(b * E, E)].unsqueeze(1).to_broadcast([P, 2, E])
                    tmp2 = xn[:, 2 * q:2 * q + 2, :]
                    V.tensor_tensor(tmp2, y_ps[q][:, :].rearrange("p (t n) -> p t n", t=2), ga2, ALU.mult
                                    ).then_inc(s_y_taken, 1)
                    dve.wait_ge(s_y_taken, b * 4 + pair_ + 1)
                    x2 = xt(b, 4 * h + 2 * q, 2).rearrange("p (t n) -> p t n", t=2)
                    V.tensor_tensor(x2, x2, tmp2, ALU.add).then_inc(s_y_done, 1)

                def pick(one, score_ap):
                    vlink(V.tensor_reduce(best[:, :], score_ap, X, ALU.max))
                    vlink(V.tensor_tensor(key[:, :, :], score_ap, best[:, :].unsqueeze(2).to_broadcast(G),
                                          ALU.is_equal))
                    vlink(V.tensor_tensor(key[:, :, :], key[:, :, :], rev_s[:, :].unsqueeze(1).to_broadcast(G),
                                          ALU.mult))
                    vlink(V.tensor_reduce(gw[:, :], key[:, :, :], X, ALU.max))
                    vlink(V.tensor_tensor(one[:, :, :], key[:, :, :], gw[:, :].unsqueeze(2).to_broadcast(G),
                                          ALU.is_equal))

                def gate_choice(h):
                    dve.wait_ge(s_capped_s, b * 2 + h + 1)
                    pick(one1, capped[:, :, :])
                    V.tensor_tensor(shifted[:, :, :], capped[:, :, :], best[:, :].unsqueeze(2).to_broadcast(G),
                                    ALU.subtract)
                    vlink(S_(tmp[:, :, :], one1[:, :, :], -4.0, capped[:, :, :], ALU.mult, ALU.add))
                    pick(one2, tmp[:, :, :])
                    V.tensor_tensor(chosen[:, 0:HALF, :], one1[:, :, :], one2[:, :, :], ALU.add
                                    ).then_inc(s_shifted_s, 1)

                def gate_weights(h):
                    dve.wait_ge(s_gate_exp, b * 2 + h + 1)
                    vlink(V.tensor_reduce(gsum[:, :], eg[:, :, :], X, ALU.add))
                    vlink(V.reciprocal(ginv[:, :], gsum[:, :]))
                    for k, one in enumerate((one1, one2)):
                        vlink(V.tensor_tensor(tmp[:, :, :], eg[:, :, :], one[:, :, :], ALU.mult))
                        vlink(V.tensor_reduce(gw[:, :], tmp[:, :, :], X, ALU.add))
                        vlink(V.tensor_tensor(weight[:, k, bass.ds(b * TILES + h * HALF, HALF)], gw[:, :], ginv[:, :],
                                              ALU.mult))

                def placing(h):
                    dve.wait_ge(s_routed_rows, (2 * b + h) * 128)
                    for k, one in enumerate((one1, one2)):
                        vlink(V.tensor_tensor(tmp[:, :, :], place[:, :, :], one[:, :, :], ALU.mult))
                        vlink(V.tensor_reduce(gplace[:, :], tmp[:, :, :], X, ALU.add))
                        last = V.tensor_copy(rows_i[:, k, :], gplace[:, :])
                        if k == 0:
                            vlink(last)
                    last.then_inc(s_placed, 1)

                for k in slot_list():
                    for e in RING.get(k - 1, ()):
                        take(e)
                    if 0 <= k < UNITS:
                        dve.wait_ge(s_scored, b * UNITS + k + 1)
                        V.tensor_reduce(neg_max[:, k % 2, :], score[k % 2][:, :].rearrange("p (j n) -> p j n", j=4),
                                        X, ALU.max, negate=True).then_inc(s_maxed, 1)
                    if 0 <= k - 2 < UNITS:
                        u = k - 2
                        dve.wait_ge(s_pT_hi, b * UNITS + u + 1)
                        S_(pT[:, u % 2, 1, :], t_ps[:, :], P_SCALE, pT[:, u % 2, 0, :], ALU.mult, ALU.subtract
                           ).then_inc(s_pT_lo, 1)
                    if 0 <= k - 3 < UNITS:
                        u = k - 3
                        g = u // 4 % 4
                        dve.wait_ge(s_att_hi, b * UNITS + u + 1)
                        S_(att[:, u % 2, 1].rearrange("p h n -> p (h n)"), o_ps[:, :],
                           bias_c[:, NQ + NKV + g:NQ + NKV + g + 1],
                           att[:, u % 2, 0].rearrange("p h n -> p (h n)"), ALU.add, ALU.subtract
                           ).then_inc(s_att_lo, 1)
                    if 0 <= k < UNITS:
                        dve.wait_ge(s_exped, b * UNITS + k + 1)
                        V.reciprocal(inv_sum[:, k % 2, :], row_sum[:, k % 2, :]).then_inc(s_summed, 1)
                    for e in RING.get(k - 1, ()):
                        if e in ROPED_AT:
                            rotate(e)
                    for e in RING.get(k - 2, ()):
                        if e in SPLIT_AT:
                            low(e)
                    if k == FIRST_SLOT:
                        statistics(0, 0, s_x_in[2 * b], 16)
                        normalize(0, 0)
                    if k == 1:
                        statistics(1, HALF, s_x_in[2 * b + 1], 16)
                    if k == 2:
                        normalize(1, HALF)
                    if (h := tail_at(k, 17)) is not None:
                        residual(2 * h)
                    if (h := tail_at(k, 19)) is not None:
                        residual(2 * h + 1)
                    if (h := tail_at(k, 20)) is not None:
                        statistics(2 + h, HALF * h, s_y_done, b * 4 + 2 * h + 2)
                    if (h := tail_at(k, 21)) is not None:
                        normalize(2 + h, HALF * h)
                    if (h := tail_at(k, 24)) is not None:
                        dve.wait_ge(s_pay_hi, b * 2 + h + 1)
                        V.tensor_tensor(pay[:, :, E:2 * E], xn[:, :, :], pay[:, :, 0:E], ALU.subtract
                                        ).then_inc(s_pay_lo, 1)
                    if (h := tail_at(k, 28)) is not None:
                        gate_choice(h)
                    if (h := tail_at(k, 29)) is not None:
                        gate_weights(h)
                    if (h := tail_at(k, 30)) is not None:
                        placing(h)
                steps = done[0]
            assert steps == STEPS_BATCH, steps
            done[0] = before + (B - 1) * STEPS_BATCH + STEPS_BATCH

            def elink(ins):
                done[0] += 1
                ins.then_inc(s_vector_step, 1)
                dve.wait_ge(s_vector_step, done[0])

            batch_over(dve, B)
            V.tensor_copy(counts_i[:, :], used_rows[:, :]).then_inc(s_rows_ready, 1)
            elink(V.tensor_tensor(counts[:, :], used_rows[:, :], base_s[:, :], ALU.subtract))
            elink(V.tensor_scalar(counts[:, :], counts[:, :], float(P - 1), None, ALU.add))
            elink(V.tensor_copy(tiles_i[:, :], counts[:, :]))
            elink(V.tensor_scalar(tiles_i[:, :], tiles_i[:, :], 7, None, ALU.logical_shift_right))
            V.tensor_copy(xtiles[:, :], tiles_i[:, :])
            elink(V.memset(scan[:, :, 0:NX], 0.0))
            elink(V.tensor_copy(scan[:, 0, NX:], xtiles[:, :]))
            for j, d in enumerate((1, 2, 4)):
                elink(V.tensor_tensor(scan[:, j + 1, NX:], scan[:, j, NX:], scan[:, j, NX - d:2 * NX - d], ALU.add))
            SG = [P, SLOTS, NX]
            no_b = slot_no[:, :].unsqueeze(2).to_broadcast(SG)
            elink(V.tensor_tensor(after[:, :, :], no_b, scan[:, 3, NX:].unsqueeze(1).to_broadcast(SG), ALU.is_ge))
            elink(V.tensor_reduce(slot_x[:, :], after[:, :, :], X, ALU.add))
            elink(V.tensor_tensor(after[:, :, :], after[:, :, :], xtiles[:, :].unsqueeze(1).to_broadcast(SG),
                                  ALU.mult))
            elink(V.tensor_reduce(slot_t[:, :], after[:, :, :], X, ALU.add))
            elink(V.tensor_scalar(slot_u[:, :], slot_x[:, :], float(NX), None, ALU.is_lt))
            elink(V.tensor_scalar(slot_x[:, :], slot_x[:, :], float(NX - 1), None, ALU.min))
            elink(V.tensor_tensor(slot_t[:, :], slot_no[:, :], slot_t[:, :], ALU.subtract))
            elink(V.tensor_scalar(slot_t[:, :], slot_t[:, :], float(P), float(-UNUSED_ROW), ALU.mult, ALU.add))
            elink(S_(slot_row[:, :], slot_x[:, :], float(REGION), slot_t[:, :], ALU.mult, ALU.add))
            elink(V.tensor_tensor(slot_row[:, :], slot_row[:, :], slot_u[:, :], ALU.mult))
            elink(V.tensor_scalar(slot_row[:, :], slot_row[:, :], float(UNUSED_ROW), None, ALU.add))
            V.tensor_copy(slot_xi[:, :], slot_x[:, :])
            V.tensor_copy(slot_ri[:, :], slot_row[:, :]).then_inc(s_slots_ready, 1)
            for m in range(3 * NX):
                dve.wait_ge(s_expert_hi, m + 1)
                at = m // 3 * PER_X + m % 3 * 2048
                S_(region[:, at + 1024:at + 2048], xst(m), W_SCALE, region[:, at:at + 1024], ALU.mult, ALU.subtract
                   ).then_inc(s_expert_lo, 1)

            x_ps_h = ring[0][:, :].bitcast(f16)

            def inner_lo(s, a):
                dve.wait_ge(s_innerT_hi, s + 1)
                V.tensor_tensor(innerT[:, a % 2, 1, :], t_ps[:, :], innerT[:, a % 2, 0, :], ALU.subtract
                                ).then_inc(s_innerT_lo, 1)

            def slot(i, a, head):
                s = i * 4 + a
                dve.wait_ge(s_xT_ps, s + 1)
                if not head or a >= 2:
                    dve.wait_ge(s_gate_ps, s - 1)
                V.tensor_copy(xT[:, a % 2, :], x_ps_h[:, 0:512]).then_inc(s_xT_done, 1)
                if not head or a >= 1:
                    inner_lo(s - 1, a - 1)
                dve.wait_ge(s_silu_g_done, s + 1)
                dve.wait_ge(s_gate_ps, s + 1)
                if not head or a >= 2:
                    dve.wait_ge(s_innerT_ps, s - 1)
                S_(inner[:, a % 2, :], y_ps[a % 2][:, :], 1 / W_SCALE, silu_g[:, a % 2, :], ALU.mult, ALU.mult
                   ).then_inc(s_inner_done, 1)

            for a in range(4):
                slot(0, a, True)
            with dve.Fori(1, SLOTS // 4) as i:
                for a in range(4):
                    slot(i, a, False)
            inner_lo(SLOTS - 1, 1)
            for n in range(ALL // 2):
                dve.wait_ge(s_first_done, n + 1)
                for t in range(2):
                    last = S_(pair[:, n % 2, 1, t, :], pair[:, n % 2, 1, t, :],
                              weight[:, 1, 2 * n + t:2 * n + t + 1], pair[:, n % 2, 0, t, :], ALU.mult, ALU.add)
                elink(last)
                if n >= 2:
                    dve.wait_ge(s_summed_up, n - 1)
                V.tensor_tensor(mix[:, n % 2], pair[:, n % 2, 1, :, :],
                                gates[:, 3, 2 * n // TILES, :].unsqueeze(1).to_broadcast([P, 2, E]), ALU.mult
                                ).then_inc(s_mixed, 1)

        @block.gpsimd
        def _(pool):
            Q = nc.gpsimd
            Q.memset(power[:, :], -0.5).then_inc(s_pool_ready, 1)
            Q.memset(ones_h[:, :], 1.0).then_inc(s_pool_ready, 1)
            Q.memset(chosen[:, HALF, :], 0.0).then_inc(s_pool_ready, 1)
            Q.memset(keys[:, :, :, 0:WINDOW], 0.0).then_inc(s_pool_ready, 1)
            Q.memset(pad[:, :], 0.0).then_inc(s_pool_ready, 1)
            pool.wait_ge(s_pool_ready, 5)
            Q.memset(pad[:, 2 * E:ROW].bitcast(i32), SKIP).then_inc(s_pool_ready, 1)
            pool.wait_ge(s_wq_lo, 2 * EC)
            pool.wait_ge(s_pool_ready, 6)
            Q.memset(valx[:, :, 0, :], 0.0).then_inc(s_pool_ready, 1)
            pool_done = [0]

            for b in range(B):
                batch_over(pool, b)

                def rsqrt(n):
                    pool.wait_ge(s_variance, b * 4 + n + 1)
                    Q.tensor_tensor(rstd[:, :], var_eps[:, :], power[:, :], ALU.pow).then_inc(s_rstd_done, 1)

                def wide(v):
                    return gates_flat[:, v, bass.ds(b * E, E)].unsqueeze(1).to_broadcast([P, HALF, E])

                for k in slot_list():
                    if 0 <= k < UNITS:
                        pool.wait_ge(s_summed, b * UNITS + k + 1)
                        if k >= 2:
                            pool.wait_ge(s_probs_t, b * UNITS + k - 1)
                        Q.tensor_tensor(probs[:, k % 2], exps[:, k % 2],
                                        inv_sum[:, k % 2, :].unsqueeze(2).to_broadcast([P, 4, P]), ALU.mult
                                        ).then_inc(s_normalized, 1)
                    for e in RING.get(k, ()):
                        if e in ROPED_AT:
                            r = ROPED_AT[e]
                            half = e[1] if e[0] == "k" else e[1] // 16
                            z = zrot[:, r % NZ, :]
                            pool.wait_ge(s_swapped, b * NROPED + r + 1)
                            Q.tensor_tensor(z, z, sin_s[:, half * 512:(half + 1) * 512], ALU.mult
                                            ).then_inc(s_turned, 1)
                    if k == FIRST_SLOT:
                        rsqrt(0)
                    if k == 1:
                        rsqrt(1)
                    if 4 <= k < 4 + TILES:
                        t = k - 4
                        if t == 0:
                            pool.wait_ge(s_gates_ready, 1)
                            pool.wait_ge(s_normed, b * 4 + 2)
                        xx = x_flat[:, bass.ds(b * (TILES * E) + t * E, E)]
                        Q.tensor_tensor(xx, xx, ga_bo_flat[:, bass.ds(b * E, E)], ALU.add
                                        ).then_inc(s_residual, 1)
                    if (h := tail_at(k, 20)) is not None:
                        rsqrt(2 + h)
                    if (h := tail_at(k, 21)) is not None:
                        pool.wait_ge(s_normed, b * 4 + 3 + h)
                        Q.tensor_tensor(xn[:, :, :], xn[:, :, :], wide(2), ALU.mult).then_inc(s_pool_step, 1)
                    if (h := tail_at(k, 22)) is not None:
                        pool.wait_ge(s_pool_step, b * 2 + h + 1)
                        Q.tensor_tensor(xn[:, :, :], xn[:, :, :], wide(1), ALU.add).then_inc(s_h2_done, 1)
                    if (h := tail_at(k, 31)) is not None:
                        for c in range(TOPK):
                            if c:
                                pool.wait_ge(s_routed_rows, b * 256 + h * 128 + 64)
                            else:
                                pool.wait_ge(s_pay_lo, b * 2 + h + 1)
                                if h:
                                    pool.wait_ge(s_routed_rows, b * 256 + 128)
                                pool.wait_ge(s_placed, b * 2 + h + 1)
                            Q.tensor_copy(pay_place, tok_s[:, c, bass.ds(b * TILES + h * HALF, HALF)].unsqueeze(2)
                                          ).then_inc(s_place_set, 1)
                            pool.wait_ge(s_place_set, b * 4 + h * 2 + c + 1)
                            for i in range(HALF):
                                Q.indirect_dma_start(
                                    routed, bass.IndirectOffsetOnAxis(ap=rows_i[:, c, i:i + 1].bitcast(u32), axis=0),
                                    pay[:, i, :], None).then_inc(s_routed_rows, 16)

            def scatter(s, a):
                pool.wait_ge(s_y_out, s + 1)
                Q.indirect_dma_start(results,
                                     bass.IndirectOffsetOnAxis(ap=x_rows[:, a, 2 * E:ROW].bitcast(u32), axis=0),
                                     y_s[:, a % 2, :], None, bounds_check=TOPK * TOKENS - 1, oob_is_err=False
                                     ).then_inc(s_y_written[s % 2], 16)

            for s in range(SLOTS):
                scatter(s, s % 4)
            for n in range(ALL // 2):
                pool.wait_ge(s_mixed, n + 1)
                x2 = x_s[:, 2 * n:2 * n + 2, :]
                Q.tensor_tensor(x2, x2, mix[:, n % 2], ALU.add).then_inc(s_summed_up, 1)


def _pairs_last(a, heads):
    n = a.shape[-1]
    return a.reshape(a.shape[:-1] + (heads, HD // 2, 2)).swapaxes(-1, -2).reshape(a.shape[:-1] + (n,))


def _constants():
    bf16_bits = lambda v: (np.ascontiguousarray(v, np.float32).view(np.uint32) >> 16).astype(np.uint16)
    f32 = np.float32
    half = HD // 2
    freqs = (f32(1.0) / (f32(10000.0) ** (f32(2.0) * np.arange(half, dtype=f32) / f32(HD)))).astype(f32)
    ang = (np.arange(S, dtype=f32)[None, :] * freqs[:, None]).astype(f32)
    cos, sin = np.cos(ang).astype(f32) / f32(W_SCALE), np.sin(ang).astype(f32) / f32(W_SCALE)
    r = np.arange(64)[:, None]
    c = np.arange(64)[None, :]
    own, prev = np.where(c <= r, 0, MASKED), np.where(c >= r, 0, MASKED)
    even, odd = np.hstack([own, prev]), np.hstack([prev, own])
    first = np.hstack([own, np.full_like(prev, MASKED)])
    tile = lambda e, o: np.tile(np.hstack([e, e, o, o]), (2, 1))
    masks = bf16_bits(np.stack([tile(even, odd), tile(first, odd)], 1))
    p = np.arange(P)
    tokens = (np.arange(ALL)[None, None, :] * P + p[:, None, None] + np.arange(TOPK)[None, :, None] * TOKENS)
    wide = lambda v: np.ascontiguousarray(np.broadcast_to(np.asarray(v, f32), (P, len(v))))
    return dict(
        cos_t=np.vstack([cos, cos]), sin_t=np.vstack([-sin, sin]), mask_t=masks,
        ident=np.eye(P, dtype=f32), ident16=np.eye(P, dtype=np.float16), identb=bf16_bits(np.eye(P)),
        lower=np.triu(np.ones((P, P)), 1).astype(np.float16), tokens=tokens.astype(np.int32),
        bases=wide(np.arange(NX) * REGION), reverse=wide(NX - np.arange(NX)), slot_nos=wide(np.arange(SLOTS)))


def kernel(**inputs):
    import concourse.bacc as _bacc
    from concourse import mybir as _mybir
    from concourse.bass_utils import run_bass_kernel_spmd as _run

    a = {k: np.asarray(v) for k, v in inputs.items()}
    column = lambda v: v.reshape(-1, HD).T
    given = dict(
        x=a["L0_attn_x"].reshape(TOKENS, E),
        wq=_pairs_last(a["L0_attn_Wq"], NQ), bq=column(_pairs_last(a["L0_attn_bq"], NQ)),
        wk=_pairs_last(a["L0_attn_Wk"], NKV), bk=column(_pairs_last(a["L0_attn_bk"], NKV)),
        wv=a["L0_attn_Wv"], bv=column(a["L0_attn_bv"]), wo=a["L0_attn_Wo"], bo=a["L0_attn_bo"],
        w_gate=a["L0_ffn_w_gate"], w1=a["L0_ffn_w1"], w3=a["L0_ffn_w3"], w2=a["L0_ffn_w2"],
        c_t=a["L0_c"].reshape(B, EC, P).transpose(2, 1, 0), wmod=a["L0_wmod"])
    given.update(_constants())
    nc = _bacc.Bacc("TRN2", target_bir_lowering=False, num_devices=1)
    arrays, args = {}, {}
    for name, v in given.items():
        v = np.ascontiguousarray(v)
        arrays[f"in_{name}"] = v
        args[name] = nc.dram_tensor(f"in_{name}", v.shape, _mybir.dt.from_np(v.dtype), kind="ExternalInput").ap()
    out = nc.dram_tensor("out", (TOKENS, E), _mybir.dt.float32, kind="ExternalOutput").ap()
    layer_kernel(nc, out=out, **args)
    r = _run(nc, [arrays], core_ids=[0])
    return r.results[0]["out"].reshape(B, S, E)
```

```python
import math
from contextlib import ExitStack

import numpy as np

import concourse.bass as bass
from concourse import mybir
from concourse.alu_op_type import AluOpType as ALU

B, S, E = 2, 1024, 256
NQ, NKV, HD = 16, 4, 128
HG = NQ // NKV
WINDOW = 64
NX, TOPK, INNER = 8, 2, 512
SOFTCAP, EPS = 30.0, 1e-5
P = 128
EC = E // P
TILES = S // P
ALL = B * TILES
TOKENS = B * S
HALF = TILES // 2
W_SCALE = 64.0
P_SCALE = 64.0
K_SCALE = 1.0 / math.sqrt(HD)
MASKED = -1e30

REGION = TOKENS + P
ROWS = NX * REGION + P
UNUSED_ROW = NX * REGION
SLOTS = 40
ROW = 2 * E + 2
SKIP = TOPK * TOKENS

HALVES = ALL // HALF
PER_HALF = NKV * HALF
UNITS = HALVES * PER_HALF
FIRST_SLOT, LAST_SLOT = -11, (HALVES - 1) * PER_HALF + 32
Q_AHEAD = 6


def ring_entries():
    at = {}
    for i, pair in enumerate([[("ln", 0, 0), ("ln", 0, 1)]]
                             + [[("k", 0, 2 * i), ("k", 0, 2 * i + 1)] for i in range(2)]
                             + [[("v", 0, 2 * i), ("v", 0, 2 * i + 1)] for i in range(2)]
                             + [[("q", 2 * i, 0), ("q", 2 * i + 1, 0)] for i in range(3)]):
        at[i - 9 if i else -10] = pair
    for k in range(UNITS - Q_AHEAD):
        at[k] = [("q", k + Q_AHEAD, 0)]
    for H in range(1, HALVES):
        first = PER_HALF * H
        for kind, slots in (("ln", (-17, -16)), ("v", (-13, -12, -11, -10)), ("k", (-7, -5, -4, -2))):
            for j, d in enumerate(slots):
                at.setdefault(first + d, []).append((kind, H, j))
    for H in range(HALVES):
        for d, e in ((23, ("lt", H, 0)), (24, ("lt", H, 1)), (26, ("lg", H, 0)), (29, ("rk", H, 0))):
            at.setdefault(PER_HALF * H + d, []).append(e)
    return at


RING = ring_entries()
assert max(map(len, RING.values())) <= 2
ORDER = [e for k in sorted(RING) for e in RING[k]]
ENTRIES = len(ORDER)
NTH = {e: n for n, e in enumerate(ORDER)}
VAL_AT = {e: n for n, e in enumerate(e for e in ORDER if e[0] == "v")}
ROPED = [e for e in ORDER if e[0] in "qk"]
SPLIT = [e for e in ORDER if e[0] in ("q", "k", "ln")]
NZ, NA = 3, 4

NORMS = sorted([(FIRST_SLOT, "in", 0)] + [(PER_HALF * H - 19, "in", H) for H in range(1, HALVES)]
               + [(PER_HALF * H + 20, "out", H) for H in range(HALVES)])
NORM_AT = {slot: n for n, (slot, _, _) in enumerate(NORMS)}

EARLY_X = 2
SPLIT_X = {UNITS - 4 + m: [m] for m in range(3 * EARLY_X)}
for _m in range(3 * EARLY_X, 3 * NX):
    SPLIT_X.setdefault(UNITS + 3 + (_m - 3 * EARLY_X) // 2, []).append(_m)

ROPE_IN = 16 * 5
SMALL_IN = 16 * 11
POOL_READY = 7


def layer_kernel(nc, x, wq, bq, wk, bk, wv, bv, wo, bo, w_gate, w1, w3, w2, c_t, wmod,
                 cos_t, sin_t, mask_t, ident, ident16, identb, lower, tokens, bases, reverse, slot_nos, out):
    f32, f16, b16, i32, u32, u16 = (mybir.dt.float32, mybir.dt.float16, mybir.dt.bfloat16,
                                    mybir.dt.int32, mybir.dt.uint32, mybir.dt.uint16)
    ACT = mybir.ActivationFunctionType
    X = mybir.AxisListType.X
    routed = nc.dram_tensor("routed", [ROWS, ROW], f16).ap()
    results = nc.dram_tensor("results", [TOPK * TOKENS, E], f32).ap()

    with ExitStack() as ctx:
        def sb(name, shape, dt):
            return ctx.enter_context(nc.sbuf_tensor(name, shape, dt))

        def sem(name):
            return ctx.enter_context(nc.semaphore(name))

        PER_X = 6 * 1024
        region = sb("region", [P, NX * PER_X], f16)
        taken = [0]

        def carve(cols):
            at = taken[0]
            taken[0] += cols
            assert taken[0] <= NX * PER_X
            return region[:, at:at + cols]

        wq_s = carve(2 * EC * NQ * HD).rearrange("p (s c n) -> p s c n", s=2, c=EC)
        wk_s = carve(2 * EC * NKV * HD).rearrange("p (s c n) -> p s c n", s=2, c=EC)
        wv_s = carve(2 * EC * NKV * HD).rearrange("p (s c n) -> p s c n", s=2, c=EC)
        wo_s = carve(2 * NQ * E).rearrange("p (s h n) -> p s h n", s=2, h=NQ)
        KEYS = WINDOW + S
        keys_at = taken[0]
        keys = carve(NKV * 2 * KEYS).rearrange("p (g s n) -> p g s n", g=NKV, s=2)
        vals_flat = carve(2 * TILES * NKV * HD)
        vals = vals_flat.rearrange("p (s t n) -> p s t n", s=2, t=TILES)
        valx_flat = carve(2 * TILES * NKV * HD)
        valx = valx_flat.rearrange("p (s t n) -> p s t n", s=2, t=TILES)
        cos_s = carve(2 * S).bitcast(f32)
        masks = carve(2 * 512).bitcast(b16).rearrange("p (a n) -> p a n", a=2)
        wq_f = valx_flat.bitcast(f32).rearrange("p (c n) -> p c n", c=EC)
        wk_f = vals_flat[:, 0:2048].bitcast(f32).rearrange("p (c n) -> p c n", c=EC)
        wv_f = vals_flat[:, 2048:4096].bitcast(f32).rearrange("p (c n) -> p c n", c=EC)

        x_s = sb("x_s", [P, ALL, E], f32)
        hT = sb("hT", [P, 2, EC, S], f16)
        q_s = sb("q_s", [P, 2, 2, TILES, HG, 64], f16)
        att = sb("att", [P, 2, 2, HG, P], f16)
        exps = sb("exps", [P, 2, 4, P], f32)
        probs = sb("probs", [P, 2, 4, P], f32)
        pT = sb("pT", [P, 2, 2, 512], f16)
        zrot = sb("zrot", [P, NZ, 512], f32)
        arot = sb("arot", [P, NA, 512], f32)
        sin_s = sb("sin_s", [P, S], f32)
        ident_f = sb("ident_f", [P, P], f32)
        ident_b = sb("ident_b", [P, P], b16)
        ident_h = sb("ident_h", [P, P], f16)
        lower_h = sb("lower_h", [P, P], f16)
        ones_h = sb("ones_h", [P, P], f16)
        stage = sb("stage", [P, 2, 1024], f32)
        xn = sb("xn", [P, HALF, E], f32)
        h2T = sb("h2T", [P, 2, 512], f32)
        pay = sb("pay", [P, HALF, ROW], f16)
        pad = sb("pad", [P, ROW], f16)
        gates = sb("gates", [P, 4, B, E], f32)
        ga_bo = sb("ga_bo", [P, B, E], f32)
        mod_c = sb("mod_c", [P, 4, B], f32)
        bias_c = sb("bias_c", [P, NQ + 2 * NKV], f32)
        c_s = sb("c_s", [P, EC, B], f32)
        silu_c = sb("silu_c", [P, EC, B], f32)
        stats = sb("stats", [P, HALF, 6], f32)
        mean_var = sb("mean_var", [P, HALF, 2], f32)
        var_eps = sb("var_eps", [P, HALF], f32)
        power = sb("power", [P, HALF], f32)
        rstd = sb("rstd", [P, HALF], f32)
        neg_max = sb("neg_max", [P, 2, 4], f32)
        row_sum = sb("row_sum", [P, 2, 4], f32)
        inv_sum = sb("inv_sum", [P, 2, 4], f32)
        wg_s = sb("wg_s", [P, EC, NX], f32)
        G = [P, HALF, NX]
        logit, capped, shifted, eg, key, one1, one2, tmp, place = (
            sb(n, G, f32) for n in ("logit", "capped", "shifted", "eg", "key", "one1", "one2", "tmp", "place"))
        best, gsum, ginv, gw, gplace = (
            sb(n, [P, HALF], f32) for n in ("best", "gsum", "ginv", "gw", "gplace"))
        chosen = sb("chosen", [P, HALF + 1, NX], f16)
        used_rows = sb("used_rows", [P, NX], f32)
        base_s = sb("base_s", [P, NX], f32)
        rev_s = sb("rev_s", [P, NX], f32)
        weight = sb("weight", [P, TOPK, ALL], f32)
        rows_i = sb("rows_i", [P, TOPK, HALF], i32)
        tok_s = sb("tok_s", [P, TOPK, ALL], i32)

        x_rows = arot[:, :, :].rearrange("p a n -> p (a n)").bitcast(f16)[:, 0:4 * ROW].rearrange(
            "p (a n) -> p a n", a=4)
        q_flat = q_s[:, :, :, :, :, :].rearrange("p a s t h q -> p (a s t h q)")
        xT = q_flat[:, 0:1024].rearrange("p (a n) -> p a n", a=2)
        silu_g = q_flat[:, 1024:3072].bitcast(f32).rearrange("p (a n) -> p a n", a=2)
        inner = q_flat[:, 3072:5120].bitcast(f32).rearrange("p (a n) -> p a n", a=2)
        innerT = q_flat[:, 5120:7168].rearrange("p (a s n) -> p a s n", a=2, s=2)
        y_s = q_flat[:, 7168:8192].bitcast(f32).rearrange("p (a n) -> p a n", a=2)
        xstage = hT[:, :, :, :].rearrange("p s c n -> p (s c n)").bitcast(f32)[:, 0:2048].rearrange(
            "p (a n) -> p a n", a=2)
        NST = 4

        def xst(m):
            return stage[:, m % NST, :] if m % NST < 2 else xstage[:, m % NST - 2, :]

        counts = sb("counts", [P, NX], f32)
        counts_i = sb("counts_i", [P, NX], i32)
        xtiles = sb("xtiles", [P, NX], f32)
        scan = sb("scan", [P, 4, 2 * NX], f32)
        slot_no = sb("slot_no", [P, SLOTS], f32)
        slot_i = sb("slot_i", [P, SLOTS], i32)
        after = zrot[:, 0, 0:SLOTS * NX].rearrange("p (s x) -> p s x", x=NX)
        slot_x = sb("slot_x", [P, SLOTS], f32)
        slot_row = sb("slot_row", [P, SLOTS], f32)
        slot_t = sb("slot_t", [P, SLOTS], f32)
        slot_u = sb("slot_u", [P, SLOTS], f32)
        slot_xi = sb("slot_xi", [P, SLOTS], i32)
        slot_ri = sb("slot_ri", [P, SLOTS], i32)
        tiles_i = sb("tiles_i", [P, NX], i32)
        mix = region[:, 8192:8192 + 4 * E * 2].bitcast(f32).rearrange("p (a t n) -> p a t n", a=2, t=2)
        pair = region[:, 0:2 * 2 * 2 * E * 2].bitcast(f32).rearrange("p (a k t n) -> p a k t n", a=2, k=TOPK, t=2)

        def bank(name):
            return ctx.enter_context(nc.psum_tensor(name, [P, 512], f32))

        ring = [bank("ring0"), bank("ring1")]
        score = [bank("score0"), bank("score1")]
        t_ps = bank("t_ps")
        o_ps = bank("o_ps")
        y_ps = [bank("y0"), bank("y1")]

        wmod_s = q_flat[:, 0:6144].bitcast(f32).rearrange("p (c n) -> p c n", c=EC)
        wide_c = probs[:, :, :, :].rearrange("p a j n -> p (a j n)")[:, 0:EC * B * P].rearrange(
            "p (c b n) -> p c b n", c=EC, b=B)
        sign = exps[:, 0, :, :].rearrange("p j n -> p (j n)")
        absol = exps[:, 1, :, :].rearrange("p j n -> p (j n)")
        x_flat = x_s[:, :, :].rearrange("p t n -> p (t n)")
        gates_flat = gates[:, :, :, :].rearrange("p v b n -> p v (b n)")
        ga_bo_flat = ga_bo[:, :, :].rearrange("p b n -> p (b n)")
        pay_place = pay[:, :, 2 * E:ROW].bitcast(i32)
        vals_of = {0: valx, 1: vals}

        s_c_in = sem("c_in")
        s_cols_in = sem("cols_in")
        s_wmod_in = sem("wmod_in")
        s_ident_in = sem("ident_in")
        s_rope_in = sem("rope_in")
        s_small_in = sem("small_in")
        s_wkv_in = [sem("wk_in"), sem("wv_in")]
        s_wq_in = sem("wq_in")
        s_silu_done = sem("silu_done")
        s_wide_done = sem("wide_done")
        s_mod_cols = sem("mod_cols")
        s_mod_wide = sem("mod_wide")
        s_wide_taken = sem("wide_taken")
        s_gates_ready = sem("gates_ready")
        s_scaled_bias = sem("scaled_bias")
        s_wkv_hi = sem("wkv_hi")
        s_wkv_lo = sem("wkv_lo")
        s_wq_hi = sem("wq_hi")
        s_wq_lo = sem("wq_lo")
        s_wo_hi = sem("wo_hi")
        s_wo_lo = sem("wo_lo")
        s_pool_ready = sem("pool_ready")
        s_variance = sem("variance")
        s_rstd_done = sem("rstd_done")
        s_normed = sem("normed")
        s_tail_normed = sem("tail_normed")
        s_ring_filled = sem("ring_filled")
        s_ring_freed = sem("ring_freed")
        s_swapped = sem("swapped")
        s_turned = sem("turned")
        s_rotated = sem("rotated")
        s_split_hi = sem("split_hi")
        s_split_lo = sem("split_lo")
        s_val_hi = sem("val_hi")
        s_residual = sem("residual")
        s_scored = sem("scored")
        s_maxed = sem("maxed")
        s_exped = sem("exped")
        s_summed = sem("summed")
        s_normalized = sem("normalized")
        s_probs_t = sem("probs_t")
        s_pT_hi = sem("pT_hi")
        s_pT_lo = sem("pT_lo")
        s_att_ps = sem("att_ps")
        s_att_hi = sem("att_hi")
        s_att_lo = sem("att_lo")
        s_projected = sem("projected")
        s_y_taken = sem("y_taken")
        s_y_done = sem("y_done")
        s_h2_done = sem("h2_done")
        s_pay_hi = sem("pay_hi")
        s_pay_lo = sem("pay_lo")
        s_capped_s = sem("capped_s")
        s_shifted_s = sem("shifted_s")
        s_gate_exp = sem("gate_exp")
        s_placed = sem("placed")
        s_place_set = sem("place_set")
        s_routed_rows = sem("routed_rows")
        s_rows_ready = sem("rows_ready")
        s_slots_ready = sem("slots_ready")
        s_pads_written = sem("pads_written")
        s_vector_step = sem("vector_step")
        s_pool_step = sem("pool_step")
        s_pool_scaled = sem("pool_scaled")
        s_expert_hi = sem("expert_hi")
        s_expert_lo = sem("expert_lo")
        s_xT_ps = sem("xT_ps")
        s_xT_done = sem("xT_done")
        s_up_ps = sem("up_ps")
        s_gate_ps = sem("gate_ps")
        s_silu_g_done = sem("silu_g_done")
        s_inner_done = sem("inner_done")
        s_innerT_ps = sem("innerT_ps")
        s_innerT_hi = sem("innerT_hi")
        s_innerT_lo = sem("innerT_lo")
        s_down_ps = sem("down_ps")
        s_y_out = sem("y_out")
        s_first_done = sem("first_done")
        s_mixed = sem("mixed")
        s_summed_up = sem("summed_up")
        s_out_written = sem("out_written")
        s_x_in = [sem(f"x_in{i}") for i in range(4)]
        s_wo_in = [sem(f"wo_in{i}") for i in range(2)]
        s_stage_in = [sem(f"stage_in{i}") for i in range(4)]
        s_slot_in = [sem(f"slot_in{i}") for i in range(4)]
        s_y_written = [sem(f"y_written{i}") for i in range(2)]
        s_pair_in = [sem(f"pair_in{i}") for i in range(2)]
        s_vals_crossed = [sem(f"vals_crossed{i}") for i in range(2)]
        block = ctx.enter_context(nc.Block())

        def slot_list():
            return range(FIRST_SLOT, LAST_SLOT + 1)

        def norm_in(H):
            return xn if H == 0 else stage[:, 0, :].rearrange("p (t n) -> p t n", t=HALF)

        def tail_at(k, d):
            return next((H for H in range(HALVES) if k == PER_HALF * H + d), None)

        SPLIT_AT = {e: n for n, e in enumerate(SPLIT)}
        ROPED_AT = {e: n for n, e in enumerate(ROPED)}

        def bias_of(e):
            kind, i, j = e
            return (i % PER_HALF) // HALF * HG + i % HG if kind == "q" else NQ + j

        def dest(e, s):
            kind, i, j = e
            src = arot[:, SPLIT_AT[e] % NA, :]
            if kind == "q":
                return (q_s[:, i // 4 % 2, s, :, i % 4, :], src.rearrange("p (t q) -> p t q", q=64))
            if kind == "k":
                return keys[:, j, s, WINDOW + 512 * (i % 2):WINDOW + 512 * (i % 2 + 1)], src
            return hT[:, s, j, 512 * (i % 2):512 * (i % 2 + 1)], src

        @block.sync
        def _(sp):
            sp.dma_start(c_s[:, :, :], c_t).then_inc(s_c_in, 16)
            x_v = x.rearrange("(t p) n -> p t n", p=P)
            sp.dma_start(x_s[:, 0:HALF, :], x_v[:, 0:HALF, :]).then_inc(s_x_in[0], 16)
            wmod_v = wmod.rearrange("(c p) n -> p c n", p=P)
            sp.dma_start(wmod_s[:, :, 0:512], wmod_v[:, :, 0:512]).then_inc(s_cols_in, 16)
            sp.dma_start(ident_f[:, :], ident).then_inc(s_ident_in, 16)
            sp.dma_start(wk_f, wk.rearrange("(c p) n -> p c n", p=P)).then_inc(s_wkv_in[0], 16)
            for dst, src in ((bias_c[:, 0:NQ], bq), (bias_c[:, NQ:NQ + NKV], bk),
                             (bias_c[:, NQ + NKV:NQ + 2 * NKV], bv), (cos_s[:, :], cos_t), (sin_s[:, :], sin_t)):
                sp.dma_start(dst, src).then_inc(s_rope_in, 16)
            sp.dma_start(wv_f, wv.rearrange("(c p) n -> p c n", p=P)).then_inc(s_wkv_in[1], 16)
            sp.dma_start(wq_f, wq.rearrange("(c p) n -> p c n", p=P)).then_inc(s_wq_in, 16)
            sp.dma_start(wmod_s[:, :, 512:1536], wmod_v[:, :, 512:1536]).then_inc(s_wmod_in, 16)
            for dst, src in ((masks[:, :, :].bitcast(u16), mask_t), (ident_h[:, :], ident16),
                             (ident_b[:, :].bitcast(u16), identb),
                             (lower_h[:, :], lower), (tok_s[:, :, :], tokens), (base_s[:, :], bases),
                             (rev_s[:, :], reverse), (slot_no[:, :], slot_nos),
                             (wg_s[:, :, :], w_gate.rearrange("(c p) n -> p c n", p=P)),
                             (ga_bo[:, 0, :], bass.AP(bo.tensor, 0, [[0, P], [1, E]])),
                             (ga_bo[:, 1, :], bass.AP(bo.tensor, 0, [[0, P], [1, E]]))):
                sp.dma_start(dst, src).then_inc(s_small_in, 16)
            for t in range(1, ALL // HALF):
                sp.dma_start(x_s[:, t * HALF:(t + 1) * HALF, :],
                             x_v[:, t * HALF:(t + 1) * HALF, :]).then_inc(s_x_in[t], 16)
            for i in range(4):
                if i >= 2:
                    sp.wait_ge(s_wo_lo, i - 1)
                sp.dma_start(stage[:, i % 2, :].rearrange("p (h n) -> p h n", h=4),
                             wo[4 * i * HD:4 * (i + 1) * HD, :].rearrange("(h p) n -> p h n", p=P)
                             ).then_inc(s_wo_in[i % 2], 16)
            sp.wait_ge(s_pool_ready, POOL_READY)
            for H in range(HALVES):
                sp.wait_ge(s_ring_freed, NTH[("v", H, 3)] + 1)
                lo, hi = H % 2 * HALF, (H % 2 + 1) * HALF
                first = lo or 1
                for s in range(2):
                    sp.dma_start(valx[0:64, s, lo:hi, :], vals[0:64, s, lo:hi, :]
                                 ).then_inc(s_vals_crossed[H % 2], 16)
                    sp.dma_start(valx[64:P, s, first:hi, :], vals[64:P, s, first - 1:hi - 1, :]
                                 ).then_inc(s_vals_crossed[H % 2], 16)
            sp.wait_ge(s_ring_filled, NTH[("q", UNITS - 1, 0)] + 1)

            def load_expert(m):
                e, w = m // 3, m % 3
                if m >= NST:
                    sp.wait_ge(s_expert_lo, m - NST + 1)
                src = ((w1, w3)[w][e].rearrange("(c p) n -> p c n", p=P) if w < 2
                       else w2[e].rearrange("(c p) n -> p c n", p=P))
                sp.dma_start(xst(m).rearrange("p (c n) -> p c n", c=EC if w < 2 else INNER // P),
                             src).then_inc(s_stage_in[m % NST], 16)

            for m in range(3 * NX):
                load_expert(m)
            sp.dma_start(routed[UNUSED_ROW:UNUSED_ROW + P, :], pad[:, :]).then_inc(s_pads_written, 16)
            sp.wait_ge(s_rows_ready, 1)
            for e in range(NX):
                row = nc.sync.value_load(counts_i[0:1, e:e + 1], min_val=0, max_val=ROWS - P)
                sp.dma_start(routed[bass.ds(row, P), :], pad[:, :]).then_inc(s_pads_written, 16)
            sp.wait_ge(s_routed_rows, HALVES * TOPK * HALF * 16)
            sp.wait_ge(s_pads_written, 16 * (NX + 1))
            sp.wait_ge(s_slots_ready, 1)

            def load_slot(i, a, first):
                row = nc.sync.value_load(slot_ri[0:1, bass.ds(i * 4 + a, 1)] if not isinstance(i, int)
                                         else slot_ri[0:1, a:a + 1], min_val=0, max_val=ROWS - P)
                if not first:
                    sp.wait_ge(s_y_written[a % 2], (i * 2 + a // 2 - 1) * 16)
                sp.dma_start(x_rows[:, a, :], routed[bass.ds(row, P), :]).then_inc(s_slot_in[a], 16)

            for a in range(4):
                load_slot(0, a, True)
            with sp.Fori(1, SLOTS // 4) as i:
                for a in range(4):
                    load_slot(i, a, False)
            for a in range(2):
                sp.wait_ge(s_y_written[a], SLOTS // 2 * 16)
            res_v = results.rearrange("(k t p) n -> p k t n", k=TOPK, p=P)
            out_v = out.rearrange("(t p) n -> p t n", p=P)
            for n in range(ALL // 2):
                if n >= 2:
                    sp.wait_ge(s_mixed, n - 1)
                for k in range(TOPK):
                    sp.dma_start(pair[:, n % 2, k, :, :], res_v[:, k, 2 * n:2 * n + 2, :]
                                 ).then_inc(s_pair_in[n % 2], 16)
                if n >= 1:
                    sp.wait_ge(s_summed_up, n)
                    sp.dma_start(out_v[:, 2 * n - 2:2 * n, :], x_s[:, 2 * n - 2:2 * n, :]
                                 ).then_inc(s_out_written, 16)
            sp.wait_ge(s_summed_up, ALL // 2)
            sp.dma_start(out_v[:, ALL - 2:ALL, :], x_s[:, ALL - 2:ALL, :]).then_inc(s_out_written, 16)
            sp.wait_ge(s_out_written, 16 * (ALL // 2))

        @block.tensor
        def _(pe):
            mm = nc.tensor.matmul

            def three(out_ap, lhs, rhs, first, last):
                mm(out_ap, lhs(0), rhs(0), start=first, stop=False)
                mm(out_ap, lhs(0), rhs(1), start=False, stop=False)
                return mm(out_ap, lhs(1), rhs(0), start=False, stop=last)

            pe.wait_ge(s_cols_in, 16)
            pe.wait_ge(s_silu_done, 1)
            for v in range(4):
                for c in range(EC):
                    last = mm(score[0][:, B * v:B * (v + 1)], wmod_s[:, c, v * P:(v + 1) * P], silu_c[:, c, :],
                              start=(c == 0), stop=(c == EC - 1))
            last.then_inc(s_mod_cols, 1)

            def modulation():
                pe.wait_ge(s_wmod_in, 16)
                pe.wait_ge(s_wide_done, 1)
                for bb in range(B):
                    for half in range(2):
                        for c in range(EC):
                            last = mm((t_ps, o_ps, y_ps[0], y_ps[1])[2 * bb + half][:, :], wide_c[:, c, bb, :],
                                      wmod_s[:, c, 512 * (half + 1):512 * (half + 2)],
                                      start=(c == 0), stop=(c == EC - 1))
                        last.then_inc(s_mod_wide, 1)

            def entry(e):
                kind, i, j = e
                n = NTH[e]
                bank = ring[n % 2]
                if n >= 2:
                    pe.wait_ge(s_ring_freed, n - 1)
                if kind == "ln":
                    if i == 0:
                        pe.wait_ge(s_ident_in, 16)
                    pe.wait_ge(s_normed, i + 1)
                    for t in range(HALF):
                        last = nc.tensor.transpose(bank[:, t * P:(t + 1) * P], norm_in(i)[:, t, j * P:(j + 1) * P],
                                                   ident_f[:, :])
                elif kind in "kq":
                    half = i if kind == "k" else i // PER_HALF
                    cols = slice(half % 2 * 512, (half % 2 + 1) * 512)
                    if kind == "k":
                        w, at = wk_s, j * HD
                        if e == ("k", 0, 0):
                            pe.wait_ge(s_wkv_lo, 1)
                    else:
                        w, at = wq_s, bias_of(e) * HD
                        if i == 0:
                            pe.wait_ge(s_wq_lo, 2 * EC)
                    pe.wait_ge(s_split_lo, SPLIT_AT[("ln", half, 1)] + 1)
                    for c in range(EC):
                        last = three(bank[:, :], lambda s: w[:, s, c, at:at + HD],
                                     lambda s: hT[:, s, c, cols], c == 0, c == EC - 1)
                elif kind == "v":
                    at = (i % 2 * HALF + j) * P
                    rows = slice(at, at + P)
                    if e == ("v", 0, 0):
                        pe.wait_ge(s_wkv_lo, 2)
                    pe.wait_ge(s_split_lo, SPLIT_AT[("ln", i, 1)] + 1)
                    for c in range(EC):
                        last = three(bank[:, :], lambda s: hT[:, s, c, rows], lambda s: wv_s[:, s, c, :],
                                     c == 0, c == EC - 1)
                elif kind == "lt":
                    pe.wait_ge(s_h2_done, i + 1)
                    for t in range(2):
                        for c in range(EC):
                            last = nc.tensor.transpose(bank[:, (2 * t + c) * P:(2 * t + c + 1) * P],
                                                       xn[:, 2 * j + t, c * P:(c + 1) * P], ident_f[:, :])
                elif kind == "lg":
                    pe.wait_ge(s_ring_freed, NTH[("lt", i, 1)] + 1)
                    for t in range(HALF):
                        for c in range(EC):
                            at = (2 * (t % 2) + c) * P
                            last = mm(bank[:, t * NX:(t + 1) * NX], h2T[:, t // 2, at:at + P], wg_s[:, c, :],
                                      start=(c == 0), stop=(c == EC - 1))
                else:
                    pe.wait_ge(s_shifted_s, i + 1)
                    width = (HALF + 1) * NX
                    mm(bank[:, 0:width], lower_h[:, :], chosen[:, :, :].rearrange("p t n -> p (t n)"),
                       start=True, stop=False)
                    for t in range(HALF):
                        m = HALF - t
                        last = mm(bank[:, (t + 1) * NX:width].rearrange("p (t n) -> p t n", n=NX), ones_h[:, :],
                                  chosen[:, t:t + 1, :].to_broadcast([P, m, NX]), start=False, stop=(m == 1))
                last.then_inc(s_ring_filled, 1)

            def where(k):
                h = k // PER_HALF
                return h, k // HALF % NKV, HALF * (h % 2) + k % HALF

            def scores(k):
                h, g, t = where(k)
                if k >= 2:
                    pe.wait_ge(s_exped, k - 1)
                if k == 0:
                    pe.wait_ge(s_small_in, SMALL_IN)
                    pe.wait_ge(s_pool_ready, POOL_READY)
                if k % 4 == 0:
                    need = max(SPLIT_AT[("q", k + 3, 0)], SPLIT_AT[("k", h, g)])
                    pe.wait_ge(s_split_lo, need + 1)
                bank = score[k % 2]
                mm(bank[:, :], ident_b[:, :], masks[:, 1 if t == 0 else 0, :], start=True, stop=False)
                for blk in range(2):
                    for hp in range(2):
                        cols = bank[:, (2 * blk + hp) * P:(2 * blk + hp + 1) * P]

                        def kk(s):
                            if blk:
                                at = WINDOW + t * P
                                return keys[:, g, s, at:at + P]
                            v = keys[:, g, s, 0:P]
                            return bass.AP(v.tensor, v.offset + WINDOW + t * P,
                                           [list(v.ap[0]), [-WINDOW, 2], [1, WINDOW]])

                        def qq(s):
                            return q_s[:, k // 4 % 2, s, 2 * (t % HALF) + blk, 2 * hp:2 * hp + 2, :].rearrange(
                                "p h q -> p (h q)")
                        mm(cols, qq(0), kk(0), start=False, stop=False)
                        mm(cols, qq(0), kk(1), start=False, stop=False)
                        last = mm(cols, qq(1), kk(0), start=False, stop=(blk == 1 and hp == 1))
                last.then_inc(s_scored, 1)

            def transposed(k):
                pe.wait_ge(s_normalized, k + 1)
                if k == 0:
                    pe.wait_ge(s_wide_taken, 4)
                if k >= 1:
                    pe.wait_ge(s_pT_lo, k)
                for j in range(4):
                    last = nc.tensor.transpose(t_ps[:, j * P:(j + 1) * P], probs[:, k % 2, j, :], ident_f[:, :])
                last.then_inc(s_probs_t, 1)

            def attend(k):
                h, g, t = where(k)
                pe.wait_ge(s_pT_lo, k + 1)
                if k >= 1:
                    pe.wait_ge(s_att_lo, k)
                if k % PER_HALF == 0:
                    pe.wait_ge(s_vals_crossed[h % 2], (h // 2 + 1) * 64)
                o_v = o_ps[:, :].rearrange("p (h n) -> p h n", h=HG)
                for blk in range(2):
                    v = vals_of[blk]
                    last = three(o_v[:, :, blk * 64:(blk + 1) * 64],
                                 lambda s: v[:, s, t, g * HD:(g + 1) * HD],
                                 lambda s: pT[:, k % 2, s, blk * 256:(blk + 1) * 256].rearrange(
                                     "p (h n) -> p h n", h=HG), True, True)
                last.then_inc(s_att_ps, 1)

            def project(k):
                h, g, t = where(k)
                u = k % 4
                pe.wait_ge(s_att_lo, k + 1)
                if h >= 1 and g == 0 and u % 2 == 0:
                    pe.wait_ge(s_y_taken, 2 * h - 1 + u // 2)
                if k == 0:
                    pe.wait_ge(s_wo_lo, 4)
                cols = y_ps[u // 2][:, (u % 2) * E:(u % 2 + 1) * E]
                for n in range(HG):
                    for i, (sa, sw) in enumerate(((0, 0), (0, 1), (1, 0))):
                        last = mm(cols, att[:, k % 2, sa, n, :], wo_s[:, sw, g * HG + n, :],
                                  start=(g == 0 and n == 0 and i == 0 and u % 2 == 0),
                                  stop=(g == 3 and n == 3 and i == 2), skip_group_check=True)
                last.then_inc(s_projected, 1)

            for k in slot_list():
                if k == -5:
                    modulation()
                if 0 <= k < UNITS:
                    scores(k)
                for e in RING.get(k, ()):
                    entry(e)
                if 0 <= k - 1 < UNITS:
                    transposed(k - 1)
                if 0 <= k - 2 < UNITS:
                    attend(k - 2)
                if 0 <= k - 3 < UNITS:
                    project(k - 3)

            pe.wait_ge(s_expert_lo, 3 * NX)
            pe.wait_ge(s_slots_ready, 1)
            x_ps, it_ps, d_ps = ring[0], t_ps, o_ps
            x_ps_h = x_ps[:, :].bitcast(f16)

            def rows_t(s, i, a, first):
                pe.wait_ge(s_slot_in[a], (i + 1) * 16)
                if not first:
                    pe.wait_ge(s_xT_done, s)
                for q in range(4):
                    last = nc.tensor.transpose(x_ps_h[:, q * P:(q + 1) * P], x_rows[:, a, q * P:(q + 1) * P],
                                               ident_h[:, :])
                last.then_inc(s_xT_ps, 1)

            def up(s, a, early):
                e = nc.tensor.value_load(slot_xi[0:1, bass.ds(s, 1)] if not isinstance(s, int)
                                         else slot_xi[0:1, s:s + 1], min_val=0, max_val=NX - 1)
                pe.wait_ge(s_xT_done, s + 1)
                if not early:
                    pe.wait_ge(s_inner_done, s - 1)
                for w, (bank, done) in enumerate(((score[a % 2], s_up_ps), (y_ps[a % 2], s_gate_ps))):
                    for c in range(EC):
                        last = three(bank[:, :], lambda q: xT[:, a % 2, (2 * q + c) * P:(2 * q + c + 1) * P],
                                     lambda q: region[:, bass.ds(e * PER_X + ((2 * w + q) * EC + c) * INNER, INNER)],
                                     c == 0, c == EC - 1)
                    last.then_inc(done, 1)

            def inner_t(s, a, first):
                pe.wait_ge(s_inner_done, s + 1)
                if not first:
                    pe.wait_ge(s_innerT_lo, s)
                for q in range(4):
                    last = nc.tensor.transpose(it_ps[:, q * P:(q + 1) * P], inner[:, a % 2, q * P:(q + 1) * P],
                                               ident_f[:, :])
                last.then_inc(s_innerT_ps, 1)

            def down(s, a, first):
                e = nc.tensor.value_load(slot_xi[0:1, bass.ds(s, 1)] if not isinstance(s, int)
                                         else slot_xi[0:1, s:s + 1], min_val=0, max_val=NX - 1)
                pe.wait_ge(s_innerT_lo, s + 1)
                if not first:
                    pe.wait_ge(s_y_out, s)
                for c in range(INNER // P):
                    last = three(d_ps[:, 0:E], lambda q: innerT[:, a % 2, q, c * P:(c + 1) * P],
                                 lambda q: region[:, bass.ds(e * PER_X + 4 * 1024 + q * 1024 + c * E, E)],
                                 c == 0, c == INNER // P - 1)
                last.then_inc(s_down_ps, 1)

            def slot(i, a, head):
                s = i * 4 + a
                rows_t(s, i, a, head and a == 0)
                if not head or a >= 2:
                    down(s - 2, a - 2, head and a == 2)
                if not head or a >= 1:
                    inner_t(s - 1, a - 1, head and a == 1)
                up(s, a, head and a < 2)

            for a in range(4):
                slot(0, a, True)
            with pe.Fori(1, SLOTS // 4) as i:
                for a in range(4):
                    slot(i, a, False)
            down(SLOTS - 2, 0, False)
            inner_t(SLOTS - 1, 1, False)
            down(SLOTS - 1, 1, False)

        @block.scalar
        def _(act):
            A = nc.scalar.activation
            act.wait_ge(s_c_in, 16)
            A(silu_c[:, :, :], c_s[:, :, :], ACT.Silu).then_inc(s_silu_done, 1)
            def split_wkv(i):
                act.wait_ge(s_wkv_in[i], 16)
                A((wk_s, wv_s)[i][:, 0], (wk_f, wv_f)[i], ACT.Copy, scale=(W_SCALE * K_SCALE, W_SCALE)[i]
                  ).then_inc(s_wkv_hi, 1)

            def split_wq(c):
                if c == 0:
                    act.wait_ge(s_wq_in, 16)
                for n in range(2):
                    A(wq_s[:, 0, c, n * 1024:(n + 1) * 1024], wq_f[:, c, n * 1024:(n + 1) * 1024],
                      ACT.Copy, scale=W_SCALE).then_inc(s_wq_hi, 1)

            def split_wo(i):
                act.wait_ge(s_wo_in[i % 2], 16 * (i // 2 + 1))
                A(wo_s[:, 0, 4 * i:4 * (i + 1), :], stage[:, i % 2, :].rearrange("p (h n) -> p h n", h=4),
                  ACT.Copy, scale=W_SCALE).then_inc(s_wo_hi, 1)

            split_wkv(0)
            split_wkv(1)
            act.wait_ge(s_scaled_bias, 1)

            def swap(e):
                r, n = ROPED_AT[e], NTH[e]
                act.wait_ge(s_ring_filled, n + 1)
                if r >= NZ:
                    act.wait_ge(s_rotated, r - NZ + 1)
                col = bias_of(e)
                z = zrot[:, r % NZ, :]
                bank = ring[n % 2]
                A(z[0:64], bank[64:P, :], ACT.Identity, bias=bias_c[64:P, col:col + 1])
                A(z[64:P], bank[0:64, :], ACT.Identity, bias=bias_c[0:64, col:col + 1]).then_inc(s_swapped, 1)

            for k in slot_list():
                if k in (-9, -8):
                    split_wq(k + 9)
                if -7 <= k < -3:
                    split_wo(k + 7)
                if 0 <= k - 2 < UNITS:
                    u = k - 2
                    act.wait_ge(s_probs_t, u + 1)
                    if u >= 2:
                        act.wait_ge(s_att_ps, u - 1)
                    A(pT[:, u % 2, 0, :], t_ps[:, :], ACT.Copy, scale=P_SCALE).then_inc(s_pT_hi, 1)
                if 0 <= k - 3 < UNITS:
                    u = k - 3
                    g = u // HALF % NKV
                    act.wait_ge(s_att_ps, u + 1)
                    if u >= 2:
                        act.wait_ge(s_projected, u - 1)
                    A(att[:, u % 2, 0].rearrange("p h n -> p (h n)"), o_ps[:, :], ACT.Identity,
                      bias=bias_c[:, NQ + NKV + g:NQ + NKV + g + 1]).then_inc(s_att_hi, 1)
                if 0 <= k < UNITS:
                    act.wait_ge(s_maxed, k + 1)
                    if k == 0:
                        act.wait_ge(s_gates_ready, 1)
                    if k >= 2:
                        act.wait_ge(s_normalized, k - 1)
                    for j in range(4):
                        last = A(exps[:, k % 2, j, :], score[k % 2][:, j * P:(j + 1) * P], ACT.Exp,
                                 bias=neg_max[:, k % 2, j:j + 1], accum_out=row_sum[:, k % 2, j:j + 1])
                    last.then_inc(s_exped, 1)
                for e in RING.get(k, ()):
                    if e[0] in "qk":
                        swap(e)
                    elif e[0] == "v":
                        act.wait_ge(s_ring_filled, NTH[e] + 1)
                        if e[1] >= 2:
                            act.wait_ge(s_att_ps, PER_HALF * (e[1] - 1))
                            if e[1] % 2 == 0 and e[2] == 3:
                                act.wait_ge(s_att_ps, PER_HALF * (e[1] - 1) + 1)
                        A(vals[:, 0, e[1] % 2 * HALF + e[2], :], ring[NTH[e] % 2][:, :], ACT.Copy,
                          scale=1 / W_SCALE).then_inc(s_val_hi, 1)
                for e in RING.get(k - 1, ()):
                    if e in SPLIT_AT:
                        if e[0] == "ln":
                            act.wait_ge(s_ring_freed, NTH[e] + 1)
                        else:
                            act.wait_ge(s_rotated, ROPED_AT[e] + 1)
                        if e[0] == "q" and e[1] >= 8:
                            act.wait_ge(s_scored, e[1] // 4 * 4 - 4)
                        if e[0] == "k" and e[1] >= 2:
                            last_use = (PER_HALF * (e[1] - 1) + HALF * e[2] if e[1] % 2 == 0
                                        else PER_HALF * (e[1] - 2) + HALF * e[2] + 3)
                            act.wait_ge(s_scored, last_use + 1)
                        dst, src = dest(e, 0)
                        A(dst, src, ACT.Copy).then_inc(s_split_hi, 1)
                if k == -4:
                    for bb in range(B):
                        for v in range(2):
                            act.wait_ge(s_mod_wide, 2 * bb + v + 1)
                            A(gates[:, 2 * v:2 * v + 2, bb, :],
                              (t_ps, o_ps, y_ps[0], y_ps[1])[2 * bb + v][:, :].rearrange("p (v n) -> p v n", v=2),
                              ACT.Copy).then_inc(s_wide_taken, 1)
                h = tail_at(k, 23)
                if h is not None:
                    act.wait_ge(s_h2_done, h + 1)
                    if h:
                        act.wait_ge(s_routed_rows, h * 128)
                    A(pay[:, :, 0:E], xn[:, :, :], ACT.Copy).then_inc(s_pay_hi, 1)
                h = tail_at(k, 28)
                if h is not None:
                    act.wait_ge(s_ring_freed, NTH[("lg", h, 0)] + 1)
                    A(capped[:, :, :], logit[:, :, :], ACT.Tanh, scale=1 / SOFTCAP).then_inc(s_capped_s, 1)
                h = tail_at(k, 29)
                if h is not None:
                    act.wait_ge(s_shifted_s, h + 1)
                    A(eg[:, :, :], shifted[:, :, :], ACT.Exp, scale=SOFTCAP).then_inc(s_gate_exp, 1)
                for m in SPLIT_X.get(k, ()):
                    if m == 0:
                        act.wait_ge(s_ring_filled, NTH[("q", UNITS - 1, 0)] + 1)
                    if m == 3 * EARLY_X:
                        act.wait_ge(s_projected, UNITS)
                    act.wait_ge(s_stage_in[m % NST], 16 * (m // NST + 1))
                    at = m // 3 * PER_X + m % 3 * 2048
                    A(region[:, at:at + 1024], xst(m), ACT.Copy, scale=W_SCALE).then_inc(s_expert_hi, 1)

            def inner_hi(s, a, early):
                act.wait_ge(s_innerT_ps, s + 1)
                if not early:
                    act.wait_ge(s_down_ps, s - 1)
                A(innerT[:, a % 2, 0, :], t_ps[:, :], ACT.Copy).then_inc(s_innerT_hi, 1)

            def result(s, half, a, early):
                act.wait_ge(s_down_ps, s + 1)
                if not early:
                    act.wait_ge(s_y_written[a % 2], half * 16)
                A(y_s[:, a % 2, :], o_ps[:, 0:E], ACT.Copy, scale=1 / W_SCALE).then_inc(s_y_out, 1)

            def slot(i, a, head):
                s = i * 4 + a
                if not head or a >= 1:
                    inner_hi(s - 1, a - 1, head and a < 3)
                if not head or a >= 2:
                    result(s - 2, i * 2 + a // 2 - 1, a - 2, head)
                act.wait_ge(s_up_ps, s + 1)
                if not head or a >= 2:
                    act.wait_ge(s_inner_done, s - 1)
                A(silu_g[:, a % 2, :], score[a % 2][:, :], ACT.Silu, scale=1 / W_SCALE
                  ).then_inc(s_silu_g_done, 1)

            for a in range(4):
                slot(0, a, True)
            with act.Fori(1, SLOTS // 4) as i:
                for a in range(4):
                    slot(i, a, False)
            result(SLOTS - 2, SLOTS // 2 - 1, 0, False)
            inner_hi(SLOTS - 1, 1, False)
            result(SLOTS - 1, SLOTS // 2 - 1, 1, False)
            for n in range(ALL // 2):
                act.wait_ge(s_pair_in[n % 2], 32 * (n // 2 + 1))
                for t in range(2):
                    last = A(pair[:, n % 2, 0, t, :], pair[:, n % 2, 0, t, :], ACT.Copy,
                             scale=weight[:, 0, 2 * n + t:2 * n + t + 1])
                last.then_inc(s_first_done, 1)

        @block.vector
        def _(dve):
            V = nc.vector
            done = [0]

            def link(ins):
                done[0] += 1
                ins.then_inc(s_vector_step, 1)
                dve.wait_ge(s_vector_step, done[0])

            S_ = V.scalar_tensor_tensor

            dve.wait_ge(s_silu_done, 1)
            for c in range(EC):
                last = V.tensor_copy(wide_c[:, c], silu_c[:, c, :].unsqueeze(2).to_broadcast([P, B, P]))
            last.then_inc(s_wide_done, 1)

            def modulation_and_biases():
                dve.wait_ge(s_mod_cols, 1)
                V.tensor_copy(mod_c[:, 0:2, :], score[0][:, 0:4].rearrange("p (c b) -> p c b", b=B))
                V.tensor_scalar(mod_c[:, 2:4, :], score[0][:, 4:8].rearrange("p (c b) -> p c b", b=B), 1.0, None,
                                ALU.add)
                dve.wait_ge(s_rope_in, ROPE_IN)
                V.tensor_scalar(bias_c[:, 0:NQ], bias_c[:, 0:NQ], W_SCALE, None, ALU.mult)
                V.tensor_scalar(bias_c[:, NQ:NQ + NKV], bias_c[:, NQ:NQ + NKV], W_SCALE * K_SCALE, None, ALU.mult)
                V.tensor_scalar(bias_c[:, NQ + NKV:NQ + 2 * NKV], bias_c[:, NQ + NKV:NQ + 2 * NKV], P_SCALE,
                                None, ALU.mult).then_inc(s_scaled_bias, 1)
                dve.wait_ge(s_scaled_bias, 1)

            def split_wk():
                dve.wait_ge(s_wkv_hi, 1)
                S_(wk_s[:, 1], wk_f, W_SCALE * K_SCALE, wk_s[:, 0], ALU.mult, ALU.subtract).then_inc(s_wkv_lo, 1)

            def split_wv():
                dve.wait_ge(s_wkv_hi, 2)
                S_(wv_s[:, 1], wv_f, W_SCALE, wv_s[:, 0], ALU.mult, ALU.subtract).then_inc(s_wkv_lo, 1)

            def split_wq(c):
                for n in range(2):
                    dve.wait_ge(s_wq_hi, 2 * c + n + 1)
                    S_(wq_s[:, 1, c, n * 1024:(n + 1) * 1024], wq_f[:, c, n * 1024:(n + 1) * 1024], W_SCALE,
                       wq_s[:, 0, c, n * 1024:(n + 1) * 1024], ALU.mult, ALU.subtract).then_inc(s_wq_lo, 1)

            def split_wo(i):
                dve.wait_ge(s_wo_hi, i + 1)
                S_(wo_s[:, 1, 4 * i:4 * (i + 1), :], stage[:, i % 2, :].rearrange("p (h n) -> p h n", h=4), W_SCALE,
                   wo_s[:, 0, 4 * i:4 * (i + 1), :], ALU.mult, ALU.subtract).then_inc(s_wo_lo, 1)

            def xt(t, n=1):
                return x_flat[:, t * E:(t + n) * E]

            def statistics(n):
                _, which, H = NORMS[n]
                if which == "in":
                    dve.wait_ge(s_x_in[H], 16)
                else:
                    dve.wait_ge(s_y_done, 2 * H + 2)
                for i in range(HALF):
                    last = V.bn_stats(stats[:, i, :], xt(HALF * H + i))
                link(last)
                for i in range(HALF):
                    last = V.bn_aggr(mean_var[:, i, :], stats[:, i, :])
                link(last)
                V.tensor_scalar(var_eps[:, :], mean_var[:, :, 1], EPS, None, ALU.add).then_inc(s_variance, 1)

            def normalize(n):
                _, which, H = NORMS[n]
                dve.wait_ge(s_rstd_done, n + 1)
                to, done_ = (norm_in(H), s_normed) if which == "in" else (xn, s_tail_normed)
                for i in range(HALF):
                    last = V.tensor_scalar(to[:, i, :], xt(HALF * H + i), mean_var[:, i, 0:1], rstd[:, i:i + 1],
                                           ALU.subtract, ALU.mult)
                last.then_inc(done_, 1)

            def take(e):
                kind, i, j = e
                n = NTH[e]
                bank = ring[n % 2]
                if e in SPLIT_AT and SPLIT_AT[e] >= NA:
                    dve.wait_ge(s_split_lo, SPLIT_AT[e] - NA + 1)
                if kind in "kq":
                    col = bias_of(e)
                    half = (i if kind == "k" else i // PER_HALF) % 2
                    dve.wait_ge(s_swapped, ROPED_AT[e] + 1)
                    last = S_(arot[:, SPLIT_AT[e] % NA, :], bank[:, :], bias_c[:, col:col + 1],
                              cos_s[:, half * 512:(half + 1) * 512], ALU.add, ALU.mult)
                elif kind == "v":
                    dve.wait_ge(s_val_hi, VAL_AT[e] + 1)
                    t = i % 2 * HALF + j
                    last = S_(vals[:, 1, t, :], bank[:, :], 1 / W_SCALE, vals[:, 0, t, :],
                              ALU.mult, ALU.subtract)
                else:
                    dve.wait_ge(s_ring_filled, n + 1)
                    if kind == "ln":
                        last = V.tensor_scalar(arot[:, SPLIT_AT[e] % NA, :], bank[:, :],
                                               mod_c[:, 2 + j, i // 2:i // 2 + 1], mod_c[:, j, i // 2:i // 2 + 1],
                                               ALU.mult, ALU.add)
                    elif kind == "lt":
                        last = V.tensor_copy(h2T[:, j, :], bank[:, :])
                    elif kind == "lg":
                        last = V.tensor_copy(logit[:, :, :].rearrange("p t n -> p (t n)"), bank[:, 0:HALF * NX])
                    else:
                        link(V.tensor_tensor(place[:, :, :], bank[:, 0:HALF * NX].rearrange(
                            "p (t n) -> p t n", n=NX), used_rows[:, :].unsqueeze(1).to_broadcast(G), ALU.add))
                        last = V.tensor_tensor(used_rows[:, :], bank[:, HALF * NX:(HALF + 1) * NX],
                                               used_rows[:, :], ALU.add)
                last.then_inc(s_ring_freed, 1)

            def rotate(e):
                r, a = ROPED_AT[e], arot[:, SPLIT_AT[e] % NA, :]
                dve.wait_ge(s_turned, r + 1)
                dve.wait_ge(s_ring_freed, NTH[e] + 1)
                V.tensor_tensor(a, a, zrot[:, r % NZ, :], ALU.add).then_inc(s_rotated, 1)

            def low(e):
                dve.wait_ge(s_split_hi, SPLIT_AT[e] + 1)
                (hi, src), (lo, _) = dest(e, 0), dest(e, 1)
                V.tensor_tensor(lo, src, hi, ALU.subtract).then_inc(s_split_lo, 1)

            def residual(h, q):
                dve.wait_ge(s_projected, PER_HALF * h + 12 + 2 * q + 2)
                dve.wait_ge(s_residual, HALF * h + 2 * q + 2)
                ga2 = gates[:, 0, h // 2, :].unsqueeze(1).to_broadcast([P, 2, E])
                tmp2 = xn[:, 2 * q:2 * q + 2, :]
                V.tensor_tensor(tmp2, y_ps[q][:, :].rearrange("p (t n) -> p t n", t=2), ga2, ALU.mult
                                ).then_inc(s_y_taken, 1)
                dve.wait_ge(s_y_taken, 2 * h + q + 1)
                x2 = xt(HALF * h + 2 * q, 2).rearrange("p (t n) -> p t n", t=2)
                V.tensor_tensor(x2, x2, tmp2, ALU.add).then_inc(s_y_done, 1)

            def pick(one, score_ap):
                link(V.tensor_reduce(best[:, :], score_ap, X, ALU.max))
                link(V.tensor_tensor(key[:, :, :], score_ap, best[:, :].unsqueeze(2).to_broadcast(G),
                                      ALU.is_equal))
                link(V.tensor_tensor(key[:, :, :], key[:, :, :], rev_s[:, :].unsqueeze(1).to_broadcast(G),
                                      ALU.mult))
                link(V.tensor_reduce(gw[:, :], key[:, :, :], X, ALU.max))
                link(V.tensor_tensor(one[:, :, :], key[:, :, :], gw[:, :].unsqueeze(2).to_broadcast(G),
                                      ALU.is_equal))

            def gate_choice(h):
                dve.wait_ge(s_capped_s, h + 1)
                pick(one1, capped[:, :, :])
                V.tensor_tensor(shifted[:, :, :], capped[:, :, :], best[:, :].unsqueeze(2).to_broadcast(G),
                                ALU.subtract)
                link(S_(tmp[:, :, :], one1[:, :, :], -4.0, capped[:, :, :], ALU.mult, ALU.add))
                pick(one2, tmp[:, :, :])
                V.tensor_tensor(chosen[:, 0:HALF, :], one1[:, :, :], one2[:, :, :], ALU.add
                                ).then_inc(s_shifted_s, 1)

            def gate_weights(h):
                dve.wait_ge(s_gate_exp, h + 1)
                link(V.tensor_reduce(gsum[:, :], eg[:, :, :], X, ALU.add))
                link(V.reciprocal(ginv[:, :], gsum[:, :]))
                for k, one in enumerate((one1, one2)):
                    link(V.tensor_tensor(tmp[:, :, :], eg[:, :, :], one[:, :, :], ALU.mult))
                    link(V.tensor_reduce(gw[:, :], tmp[:, :, :], X, ALU.add))
                    link(V.tensor_tensor(weight[:, k, HALF * h:HALF * (h + 1)], gw[:, :], ginv[:, :],
                                          ALU.mult))

            def placing(h):
                if h:
                    dve.wait_ge(s_routed_rows, h * 128)
                for k, one in enumerate((one1, one2)):
                    link(V.tensor_tensor(tmp[:, :, :], place[:, :, :], one[:, :, :], ALU.mult))
                    link(V.tensor_reduce(gplace[:, :], tmp[:, :, :], X, ALU.add))
                    last = V.tensor_copy(rows_i[:, k, :], gplace[:, :])
                    if k == 0:
                        link(last)
                last.then_inc(s_placed, 1)

            for k in slot_list():
                if k == FIRST_SLOT + 1:
                    modulation_and_biases()
                    split_wk()
                if k == FIRST_SLOT + 1 + 1:
                    split_wv()
                if k in (-8, -7):
                    split_wq(k + 8)
                if -6 <= k < -2:
                    split_wo(k + 6)
                for e in RING.get(k - 1, ()):
                    take(e)
                if 0 <= k < UNITS:
                    dve.wait_ge(s_scored, k + 1)
                    V.tensor_reduce(neg_max[:, k % 2, :], score[k % 2][:, :].rearrange("p (j n) -> p j n", j=4),
                                    X, ALU.max, negate=True).then_inc(s_maxed, 1)
                if 0 <= k - 2 < UNITS:
                    u = k - 2
                    dve.wait_ge(s_pT_hi, u + 1)
                    S_(pT[:, u % 2, 1, :], t_ps[:, :], P_SCALE, pT[:, u % 2, 0, :], ALU.mult, ALU.subtract
                       ).then_inc(s_pT_lo, 1)
                if 0 <= k - 3 < UNITS:
                    u = k - 3
                    g = u // HALF % NKV
                    dve.wait_ge(s_att_hi, u + 1)
                    S_(att[:, u % 2, 1].rearrange("p h n -> p (h n)"), o_ps[:, :],
                       bias_c[:, NQ + NKV + g:NQ + NKV + g + 1],
                       att[:, u % 2, 0].rearrange("p h n -> p (h n)"), ALU.add, ALU.subtract
                       ).then_inc(s_att_lo, 1)
                if 0 <= k < UNITS:
                    dve.wait_ge(s_exped, k + 1)
                    V.reciprocal(inv_sum[:, k % 2, :], row_sum[:, k % 2, :]).then_inc(s_summed, 1)
                for e in RING.get(k - 1, ()):
                    if e in ROPED_AT:
                        rotate(e)
                for e in RING.get(k - 2, ()):
                    if e in SPLIT_AT:
                        low(e)
                if k == FIRST_SLOT:
                    statistics(0)
                    normalize(0)
                elif k in NORM_AT:
                    statistics(NORM_AT[k])
                elif k - 1 in NORM_AT and k - 1 != FIRST_SLOT:
                    normalize(NORM_AT[k - 1])
                if (h := tail_at(k, 17)) is not None:
                    residual(h, 0)
                if (h := tail_at(k, 19)) is not None:
                    residual(h, 1)
                if (h := tail_at(k, 24)) is not None:
                    dve.wait_ge(s_pay_hi, h + 1)
                    V.tensor_tensor(pay[:, :, E:2 * E], xn[:, :, :], pay[:, :, 0:E], ALU.subtract
                                    ).then_inc(s_pay_lo, 1)
                if (h := tail_at(k, 28)) is not None:
                    gate_choice(h)
                if (h := tail_at(k, 29)) is not None:
                    gate_weights(h)
                if (h := tail_at(k, 30)) is not None:
                    placing(h)
                for m in SPLIT_X.get(k, ()):
                    dve.wait_ge(s_expert_hi, m + 1)
                    at = m // 3 * PER_X + m % 3 * 2048
                    S_(region[:, at + 1024:at + 2048], xst(m), W_SCALE, region[:, at:at + 1024],
                       ALU.mult, ALU.subtract).then_inc(s_expert_lo, 1)

            V.tensor_copy(counts_i[:, :], used_rows[:, :]).then_inc(s_rows_ready, 1)
            link(V.tensor_tensor(counts[:, :], used_rows[:, :], base_s[:, :], ALU.subtract))
            link(V.tensor_scalar(counts[:, :], counts[:, :], float(P - 1), None, ALU.add))
            link(V.tensor_copy(tiles_i[:, :], counts[:, :]))
            link(V.tensor_scalar(tiles_i[:, :], tiles_i[:, :], 7, None, ALU.logical_shift_right))
            V.tensor_copy(xtiles[:, :], tiles_i[:, :])
            link(V.memset(scan[:, :, 0:NX], 0.0))
            link(V.tensor_copy(scan[:, 0, NX:], xtiles[:, :]))
            for j, d in enumerate((1, 2, 4)):
                link(V.tensor_tensor(scan[:, j + 1, NX:], scan[:, j, NX:], scan[:, j, NX - d:2 * NX - d], ALU.add))
            SG = [P, SLOTS, NX]
            no_b = slot_no[:, :].unsqueeze(2).to_broadcast(SG)
            link(V.tensor_tensor(after[:, :, :], no_b, scan[:, 3, NX:].unsqueeze(1).to_broadcast(SG), ALU.is_ge))
            link(V.tensor_reduce(slot_x[:, :], after[:, :, :], X, ALU.add))
            link(V.tensor_tensor(after[:, :, :], after[:, :, :], xtiles[:, :].unsqueeze(1).to_broadcast(SG),
                                  ALU.mult))
            link(V.tensor_reduce(slot_t[:, :], after[:, :, :], X, ALU.add))
            link(V.tensor_scalar(slot_u[:, :], slot_x[:, :], float(NX), None, ALU.is_lt))
            link(V.tensor_scalar(slot_x[:, :], slot_x[:, :], float(NX - 1), None, ALU.min))
            link(V.tensor_tensor(slot_t[:, :], slot_no[:, :], slot_t[:, :], ALU.subtract))
            link(V.tensor_scalar(slot_t[:, :], slot_t[:, :], float(P), float(-UNUSED_ROW), ALU.mult, ALU.add))
            link(S_(slot_row[:, :], slot_x[:, :], float(REGION), slot_t[:, :], ALU.mult, ALU.add))
            link(V.tensor_tensor(slot_row[:, :], slot_row[:, :], slot_u[:, :], ALU.mult))
            link(V.tensor_scalar(slot_row[:, :], slot_row[:, :], float(UNUSED_ROW), None, ALU.add))
            V.tensor_copy(slot_xi[:, :], slot_x[:, :])
            V.tensor_copy(slot_ri[:, :], slot_row[:, :]).then_inc(s_slots_ready, 1)
            x_ps_h = ring[0][:, :].bitcast(f16)

            def inner_lo(s, a):
                dve.wait_ge(s_innerT_hi, s + 1)
                V.tensor_tensor(innerT[:, a % 2, 1, :], t_ps[:, :], innerT[:, a % 2, 0, :], ALU.subtract
                                ).then_inc(s_innerT_lo, 1)

            def slot(i, a, head):
                s = i * 4 + a
                dve.wait_ge(s_xT_ps, s + 1)
                if not head or a >= 2:
                    dve.wait_ge(s_gate_ps, s - 1)
                V.tensor_copy(xT[:, a % 2, :], x_ps_h[:, 0:512]).then_inc(s_xT_done, 1)
                if not head or a >= 1:
                    inner_lo(s - 1, a - 1)
                dve.wait_ge(s_silu_g_done, s + 1)
                dve.wait_ge(s_gate_ps, s + 1)
                if not head or a >= 2:
                    dve.wait_ge(s_innerT_ps, s - 1)
                S_(inner[:, a % 2, :], y_ps[a % 2][:, :], 1 / W_SCALE, silu_g[:, a % 2, :], ALU.mult, ALU.mult
                   ).then_inc(s_inner_done, 1)

            for a in range(4):
                slot(0, a, True)
            with dve.Fori(1, SLOTS // 4) as i:
                for a in range(4):
                    slot(i, a, False)
            inner_lo(SLOTS - 1, 1)
            for n in range(ALL // 2):
                dve.wait_ge(s_first_done, n + 1)
                for t in range(2):
                    last = S_(pair[:, n % 2, 1, t, :], pair[:, n % 2, 1, t, :],
                              weight[:, 1, 2 * n + t:2 * n + t + 1], pair[:, n % 2, 0, t, :], ALU.mult, ALU.add)
                link(last)
                if n >= 2:
                    dve.wait_ge(s_summed_up, n - 1)
                V.tensor_tensor(mix[:, n % 2], pair[:, n % 2, 1, :, :],
                                gates[:, 3, 2 * n // TILES, :].unsqueeze(1).to_broadcast([P, 2, E]), ALU.mult
                                ).then_inc(s_mixed, 1)

        @block.gpsimd
        def _(pool):
            Q = nc.gpsimd
            Q.memset(power[:, :], -0.5).then_inc(s_pool_ready, 1)
            Q.memset(ones_h[:, :], 1.0).then_inc(s_pool_ready, 1)
            Q.memset(chosen[:, HALF, :], 0.0).then_inc(s_pool_ready, 1)
            Q.memset(keys[:, :, :, 0:WINDOW], 0.0).then_inc(s_pool_ready, 1)
            Q.memset(pad[:, :], 0.0).then_inc(s_pool_ready, 1)
            pool.wait_ge(s_pool_ready, 5)
            Q.memset(pad[:, 2 * E:ROW].bitcast(i32), SKIP).then_inc(s_pool_ready, 1)

            def rsqrt(n):
                pool.wait_ge(s_variance, n + 1)
                Q.tensor_tensor(rstd[:, :], var_eps[:, :], power[:, :], ALU.pow).then_inc(s_rstd_done, 1)

            def wide(v, b):
                return gates[:, v, b, :].unsqueeze(1).to_broadcast([P, HALF, E])

            steps = [0]

            def link(ins):
                steps[0] += 1
                ins.then_inc(s_pool_step, 1)
                pool.wait_ge(s_pool_step, steps[0])

            def form_gates():
                pool.wait_ge(s_wide_taken, 4)
                pool.wait_ge(s_small_in, SMALL_IN)
                for v in (0, 3):
                    gv = gates_flat[:, v, :]
                    link(Q.tensor_scalar(sign, gv, 0.0, 2.0, ALU.is_ge, ALU.mult))
                    link(Q.tensor_scalar(sign, sign, -1.0, None, ALU.add))
                    link(Q.tensor_tensor(absol, gv, sign, ALU.mult))
                    link(Q.tensor_scalar(absol, absol, 0.25, None, ALU.max))
                    link(Q.tensor_tensor(gv, absol, sign, ALU.mult))
                link(Q.tensor_tensor(ga_bo_flat, ga_bo_flat, gates_flat[:, 0, :], ALU.mult))
                Q.tensor_scalar(gates_flat[:, 0, :], gates_flat[:, 0, :], 1 / (W_SCALE * P_SCALE), None, ALU.mult)
                Q.tensor_copy(used_rows[:, :], base_s[:, :])
                Q.tensor_scalar(gates_flat[:, 2, :], gates_flat[:, 2, :], 1.0, None, ALU.add
                                ).then_inc(s_gates_ready, 1)

            for k in slot_list():
                if 0 <= k < UNITS:
                    pool.wait_ge(s_summed, k + 1)
                    if k >= 2:
                        pool.wait_ge(s_probs_t, k - 1)
                    Q.tensor_tensor(probs[:, k % 2], exps[:, k % 2],
                                    inv_sum[:, k % 2, :].unsqueeze(2).to_broadcast([P, 4, P]), ALU.mult
                                    ).then_inc(s_normalized, 1)
                for e in RING.get(k, ()):
                    if e in ROPED_AT:
                        r = ROPED_AT[e]
                        half = (e[1] if e[0] == "k" else e[1] // PER_HALF) % 2
                        z = zrot[:, r % NZ, :]
                        pool.wait_ge(s_swapped, r + 1)
                        Q.tensor_tensor(z, z, sin_s[:, half * 512:(half + 1) * 512], ALU.mult
                                        ).then_inc(s_turned, 1)
                if k == -6:
                    pool.wait_ge(s_wq_lo, 2 * EC)
                    Q.memset(valx[:, :, 0, :], 0.0).then_inc(s_pool_ready, 1)
                if k == -4:
                    form_gates()
                if k in NORM_AT:
                    rsqrt(NORM_AT[k])
                if 4 <= k % (2 * PER_HALF) < 4 + TILES and 0 <= k < UNITS:
                    b = k // (2 * PER_HALF)
                    t = b * TILES + k % (2 * PER_HALF) - 4
                    if t == b * TILES:
                        pool.wait_ge(s_gates_ready, 1)
                        pool.wait_ge(s_normed, 2 * b + 2)
                    Q.tensor_tensor(x_s[:, t, :], x_s[:, t, :], ga_bo[:, b, :], ALU.add).then_inc(s_residual, 1)
                if (h := tail_at(k, 21)) is not None:
                    pool.wait_ge(s_tail_normed, h + 1)
                    Q.tensor_tensor(xn[:, :, :], xn[:, :, :], wide(2, h // 2), ALU.mult).then_inc(s_pool_scaled, 1)
                if (h := tail_at(k, 22)) is not None:
                    pool.wait_ge(s_pool_scaled, h + 1)
                    Q.tensor_tensor(xn[:, :, :], xn[:, :, :], wide(1, h // 2), ALU.add).then_inc(s_h2_done, 1)
                if (h := tail_at(k, 31)) is not None:
                    for c in range(TOPK):
                        pool.wait_ge(s_pay_lo, h + 1)
                        pool.wait_ge(s_placed, h + 1)
                        if 2 * h + c:
                            pool.wait_ge(s_routed_rows, (2 * h + c) * 64)
                        Q.tensor_copy(pay_place, tok_s[:, c, HALF * h:HALF * (h + 1)].unsqueeze(2)
                                      ).then_inc(s_place_set, 1)
                        pool.wait_ge(s_place_set, 2 * h + c + 1)
                        for i in range(HALF):
                            Q.indirect_dma_start(
                                routed, bass.IndirectOffsetOnAxis(ap=rows_i[:, c, i:i + 1].bitcast(u32), axis=0),
                                pay[:, i, :], None).then_inc(s_routed_rows, 16)

            def scatter(s, a):
                pool.wait_ge(s_y_out, s + 1)
                Q.indirect_dma_start(results,
                                     bass.IndirectOffsetOnAxis(ap=x_rows[:, a, 2 * E:ROW].bitcast(u32), axis=0),
                                     y_s[:, a % 2, :], None, bounds_check=TOPK * TOKENS - 1, oob_is_err=False
                                     ).then_inc(s_y_written[s % 2], 16)

            for s in range(SLOTS):
                scatter(s, s % 4)
            for n in range(ALL // 2):
                pool.wait_ge(s_mixed, n + 1)
                x2 = x_s[:, 2 * n:2 * n + 2, :]
                Q.tensor_tensor(x2, x2, mix[:, n % 2], ALU.add).then_inc(s_summed_up, 1)


def _pairs_last(a, heads):
    n = a.shape[-1]
    return a.reshape(a.shape[:-1] + (heads, HD // 2, 2)).swapaxes(-1, -2).reshape(a.shape[:-1] + (n,))


def _constants():
    bf16_bits = lambda v: (np.ascontiguousarray(v, np.float32).view(np.uint32) >> 16).astype(np.uint16)
    f32 = np.float32
    half = HD // 2
    freqs = (f32(1.0) / (f32(10000.0) ** (f32(2.0) * np.arange(half, dtype=f32) / f32(HD)))).astype(f32)
    ang = (np.arange(S, dtype=f32)[None, :] * freqs[:, None]).astype(f32)
    cos, sin = np.cos(ang).astype(f32) / f32(W_SCALE), np.sin(ang).astype(f32) / f32(W_SCALE)
    r = np.arange(64)[:, None]
    c = np.arange(64)[None, :]
    own, prev = np.where(c <= r, 0, MASKED), np.where(c >= r, 0, MASKED)
    even, odd = np.hstack([own, prev]), np.hstack([prev, own])
    first = np.hstack([own, np.full_like(prev, MASKED)])
    tile = lambda e, o: np.tile(np.hstack([e, e, o, o]), (2, 1))
    masks = bf16_bits(np.stack([tile(even, odd), tile(first, odd)], 1))
    p = np.arange(P)
    tokens = (np.arange(ALL)[None, None, :] * P + p[:, None, None] + np.arange(TOPK)[None, :, None] * TOKENS)
    wide = lambda v: np.ascontiguousarray(np.broadcast_to(np.asarray(v, f32), (P, len(v))))
    return dict(
        cos_t=np.vstack([cos, cos]), sin_t=np.vstack([-sin, sin]), mask_t=masks,
        ident=np.eye(P, dtype=f32), ident16=np.eye(P, dtype=np.float16), identb=bf16_bits(np.eye(P)),
        lower=np.triu(np.ones((P, P)), 1).astype(np.float16), tokens=tokens.astype(np.int32),
        bases=wide(np.arange(NX) * REGION), reverse=wide(NX - np.arange(NX)), slot_nos=wide(np.arange(SLOTS)))


def kernel(**inputs):
    import concourse.bacc as _bacc
    from concourse import mybir as _mybir
    from concourse.bass_utils import run_bass_kernel_spmd as _run

    a = {k: np.asarray(v) for k, v in inputs.items()}
    column = lambda v: v.reshape(-1, HD).T
    given = dict(
        x=a["L0_attn_x"].reshape(TOKENS, E),
        wq=_pairs_last(a["L0_attn_Wq"], NQ), bq=column(_pairs_last(a["L0_attn_bq"], NQ)),
        wk=_pairs_last(a["L0_attn_Wk"], NKV), bk=column(_pairs_last(a["L0_attn_bk"], NKV)),
        wv=a["L0_attn_Wv"], bv=column(a["L0_attn_bv"]), wo=a["L0_attn_Wo"], bo=a["L0_attn_bo"],
        w_gate=a["L0_ffn_w_gate"], w1=a["L0_ffn_w1"], w3=a["L0_ffn_w3"], w2=a["L0_ffn_w2"],
        c_t=a["L0_c"].reshape(B, EC, P).transpose(2, 1, 0), wmod=a["L0_wmod"])
    given.update(_constants())
    nc = _bacc.Bacc("TRN2", target_bir_lowering=False, num_devices=1)
    arrays, args = {}, {}
    for name, v in given.items():
        v = np.ascontiguousarray(v)
        arrays[f"in_{name}"] = v
        args[name] = nc.dram_tensor(f"in_{name}", v.shape, _mybir.dt.from_np(v.dtype), kind="ExternalInput").ap()
    out = nc.dram_tensor("out", (TOKENS, E), _mybir.dt.float32, kind="ExternalOutput").ap()
    layer_kernel(nc, out=out, **args)
    r = _run(nc, [arrays], core_ids=[0])
    return r.results[0]["out"].reshape(B, S, E)
```

```python
import math
from contextlib import ExitStack

import numpy as np

import concourse.bass as bass
from concourse import mybir
from concourse.alu_op_type import AluOpType as ALU

B, S, E = 2, 1024, 256
NQ, NKV, HD = 16, 4, 128
HG = NQ // NKV
WINDOW = 64
NX, TOPK, INNER = 8, 2, 512
SOFTCAP, EPS = 30.0, 1e-5
P = 128
EC = E // P
TILES = S // P
ALL = B * TILES
TOKENS = B * S
HALF = TILES // 2
W_SCALE = 64.0
P_SCALE = 64.0
K_SCALE = 1.0 / math.sqrt(HD)
MASKED = -1e30

REGION = TOKENS + P
ROWS = NX * REGION + P
UNUSED_ROW = NX * REGION
SLOTS = TOPK * TOKENS // P + NX - 1
ROW = 2 * E + 2
SKIP = TOPK * TOKENS

HALVES = ALL // HALF
PER_HALF = NKV * HALF
UNITS = HALVES * PER_HALF
FIRST_SLOT, LAST_SLOT = -10, (HALVES - 1) * PER_HALF + 33
Q_AHEAD = 6


def ring_entries():
    at = {}
    for i, pair in enumerate([[("ln", 0, 0), ("ln", 0, 1)], [], [("k", 0, 0), ("v", 0, 0)],
                              [("v", 0, 1), ("v", 0, 2)], [("v", 0, 3), ("q", 0, 0)], [("q", 1, 0), ("q", 2, 0)],
                              [("q", 3, 0), ("q", 4, 0)], [("q", 5, 0)]]):
        at[FIRST_SLOT + 1 + i] = pair
    for k in range(UNITS - Q_AHEAD):
        at[k] = [("q", k + Q_AHEAD, 0)]
    for j, k in enumerate((1, 2, 7)):
        at[k].append(("k", 0, j + 1))
    for H in range(1, HALVES):
        first = PER_HALF * H
        for kind, slots in (("ln", (-17, -16)), ("v", (-13, -12, -11, -10)), ("k", (-7, -5, -4, -3))):
            for j, d in enumerate(slots):
                at.setdefault(first + d, []).append((kind, H, j))
    for H in range(HALVES):
        for d, e in ((23, ("lt", H, 0)), (24, ("lt", H, 1)), (26, ("lg", H, 0)), (30, ("rk", H, 0))):
            at.setdefault(PER_HALF * H + d, []).append(e)
    return at


RING = ring_entries()
assert max(map(len, RING.values())) <= 2
ORDER = [e for k in sorted(RING) for e in RING[k]]
ENTRIES = len(ORDER)
NTH = {e: n for n, e in enumerate(ORDER)}
VAL_AT = {e: n for n, e in enumerate(e for e in ORDER if e[0] == "v")}
ROPED = [e for e in ORDER if e[0] in "qk"]
SPLIT = [e for e in ORDER if e[0] in ("q", "k", "ln")]
NSPLIT = len(SPLIT)


def rotated_by_pool(k, e):
    return k < 0 or e[0] == "k" or all(other[0] != "k" for other in RING[k])


ON_POOL = [e for k in sorted(RING) for e in RING[k] if e in ROPED and rotated_by_pool(k, e)]
ON_VECTOR = [e for e in ROPED if e not in ON_POOL]
NZ, NA = 3, 4

NORMS = sorted([(FIRST_SLOT, "in", 0), (PER_HALF - 19, "in", 1)]
               + [(PER_HALF * H - 22, "in", H) for H in range(2, HALVES)]
               + [(PER_HALF * H + 20, "out", H) for H in range(HALVES)])
NORM_AT = {slot: n for n, (slot, _, _) in enumerate(NORMS)}

X_ORDER = [0, 1, 2, 3, 4, 5, 6, 8, 10, 11, 12, 7, 9] + list(range(13, 3 * NX))
SPLIT_X = {59: [0], 60: [1], 61: [2], 62: [3], 63: [4], 64: [5, 6], 65: [7, 8], 66: [9, 10], 68: [11],
           69: [12], 70: [13, 14], 73: [15, 16, 17, 18]}
SPLIT_HI = {**SPLIT_X, 68: [11, 12], 69: [13, 14], 70: [15, 16], 73: [17, 18]}
LATE_X = 19
POOL_X = [12, 14, 17]
VECTOR_X = [n for n in range(3 * NX) if n not in POOL_X]
assert sorted(X_ORDER) == list(range(3 * NX)) and sum(SPLIT_X.values(), []) == list(range(LATE_X))

ROPE_IN = 16 * 5
SMALL_IN = 16 * 11
POOL_READY = 7


def layer_kernel(nc, x, wq, bq, wk, bk, wv, bv, wo, bo, w_gate, w1, w3, w2, c_t, wmod,
                 cos_t, sin_t, mask_t, ident, ident16, identb, lower, tokens, bases, reverse, slot_nos, out):
    f32, f16, b16, i32, u32, u16 = (mybir.dt.float32, mybir.dt.float16, mybir.dt.bfloat16,
                                    mybir.dt.int32, mybir.dt.uint32, mybir.dt.uint16)
    ACT = mybir.ActivationFunctionType
    X = mybir.AxisListType.X
    routed = nc.dram_tensor("routed", [ROWS, ROW], f16).ap()
    results = nc.dram_tensor("results", [TOPK * TOKENS, E], f32).ap()

    with ExitStack() as ctx:
        def sb(name, shape, dt):
            return ctx.enter_context(nc.sbuf_tensor(name, shape, dt))

        def sem(name):
            return ctx.enter_context(nc.semaphore(name))

        PER_X = 6 * 1024
        region = sb("region", [P, NX * PER_X], f16)
        taken = [0]

        def carve(cols):
            at = taken[0]
            taken[0] += cols
            assert taken[0] <= NX * PER_X
            return region[:, at:at + cols]

        wq_s = carve(2 * EC * NQ * HD).rearrange("p (s c n) -> p s c n", s=2, c=EC)
        wk_s = carve(2 * EC * NKV * HD).rearrange("p (s c n) -> p s c n", s=2, c=EC)
        wv_s = carve(2 * EC * NKV * HD).rearrange("p (s c n) -> p s c n", s=2, c=EC)
        wo_s = carve(2 * NQ * E).rearrange("p (s h n) -> p s h n", s=2, h=NQ)
        KEYS = WINDOW + S
        keys = carve(NKV * 2 * KEYS).rearrange("p (g s n) -> p g s n", g=NKV, s=2)
        vals_flat = carve(2 * TILES * NKV * HD)
        vals = vals_flat.rearrange("p (s t n) -> p s t n", s=2, t=TILES)
        valx_flat = carve(2 * TILES * NKV * HD)
        valx = valx_flat.rearrange("p (s t n) -> p s t n", s=2, t=TILES)
        cos_s = carve(2 * S).bitcast(f32)
        masks = carve(2 * 512).bitcast(b16).rearrange("p (a n) -> p a n", a=2)
        wq_f = valx_flat.bitcast(f32).rearrange("p (c n) -> p c n", c=EC)
        wk_f = vals_flat[:, 0:2048].bitcast(f32).rearrange("p (c n) -> p c n", c=EC)
        wv_f = vals_flat[:, 2048:4096].bitcast(f32).rearrange("p (c n) -> p c n", c=EC)

        x_s = sb("x_s", [P, ALL, E], f32)
        hT = sb("hT", [P, 2, EC, S], f16)
        q_s = sb("q_s", [P, 2, 2, TILES, HG, 64], f16)
        att = sb("att", [P, 2, 2, HG, P], f16)
        exps = sb("exps", [P, 2, 4, P], f32)
        probs = sb("probs", [P, 2, 4, P], f32)
        pT = sb("pT", [P, 2, 2, 512], f16)
        zrot = sb("zrot", [P, NZ, 512], f32)
        arot = sb("arot", [P, NA, 512], f32)
        sin_s = sb("sin_s", [P, S], f32)
        ident_f = sb("ident_f", [P, P], f32)
        ident_b = sb("ident_b", [P, P], b16)
        ident_h = sb("ident_h", [P, P], f16)
        lower_h = sb("lower_h", [P, P], f16)
        ones_h = sb("ones_h", [P, P], f16)
        stage = sb("stage", [P, 2, 1024], f32)
        xn = sb("xn", [P, HALF, E], f32)
        h2T = sb("h2T", [P, 2, 512], f32)
        pay = sb("pay", [P, HALF, ROW], f16)
        pad = sb("pad", [P, ROW], f16)
        gates = sb("gates", [P, 4, B, E], f32)
        ga_bo = sb("ga_bo", [P, B, E], f32)
        mod_c = sb("mod_c", [P, 4, B], f32)
        bias_c = sb("bias_c", [P, NQ + 2 * NKV], f32)
        c_s = sb("c_s", [P, EC, B], f32)
        silu_c = sb("silu_c", [P, EC, B], f32)
        stats = sb("stats", [P, HALF, 6], f32)
        mean_var = sb("mean_var", [P, HALF, 2], f32)
        var_eps = sb("var_eps", [P, HALF], f32)
        power = sb("power", [P, HALF], f32)
        rstd = sb("rstd", [P, HALF], f32)
        neg_max = sb("neg_max", [P, 2, 4], f32)
        row_sum = sb("row_sum", [P, 2, 4], f32)
        inv_sum = sb("inv_sum", [P, 2, 4], f32)
        wg_s = sb("wg_s", [P, EC, NX], f32)
        G = [P, HALF, NX]
        logit, capped, shifted, eg, key, one1, one2, tmp, place = (
            sb(n, G, f32) for n in ("logit", "capped", "shifted", "eg", "key", "one1", "one2", "tmp", "place"))
        best, gsum, ginv, gw, gplace = (
            sb(n, [P, HALF], f32) for n in ("best", "gsum", "ginv", "gw", "gplace"))
        chosen = sb("chosen", [P, HALF + 1, NX], f16)
        used_rows = sb("used_rows", [P, NX], f32)
        base_s = sb("base_s", [P, NX], f32)
        rev_s = sb("rev_s", [P, NX], f32)
        weight = sb("weight", [P, TOPK, ALL], f32)
        rows_i = sb("rows_i", [P, TOPK, HALF], i32)
        tok_s = sb("tok_s", [P, TOPK, ALL], i32)

        x_rows = hT[:, :, :, :].rearrange("p s c n -> p (s c n)")[:, 0:4 * ROW].rearrange(
            "p (a n) -> p a n", a=4)
        q_flat = q_s[:, :, :, :, :, :].rearrange("p a s t h q -> p (a s t h q)")
        xT = q_flat[:, 0:1024].rearrange("p (a n) -> p a n", a=2)
        silu_g = q_flat[:, 1024:3072].bitcast(f32).rearrange("p (a n) -> p a n", a=2)
        inner = q_flat[:, 3072:5120].bitcast(f32).rearrange("p (a n) -> p a n", a=2)
        innerT = q_flat[:, 5120:7168].rearrange("p (a s n) -> p a s n", a=2, s=2)
        y_s = q_flat[:, 7168:8192].bitcast(f32).rearrange("p (a n) -> p a n", a=2)
        xstage = hT[:, :, :, :].rearrange("p s c n -> p (s c n)").bitcast(f32)[:, 0:2048].rearrange(
            "p (a n) -> p a n", a=2)
        arot_stage = arot[:, :, :].rearrange("p a n -> p (a n)").rearrange("p (a n) -> p a n", a=2)
        q_stage = q_flat[:, 0:4096].bitcast(f32).rearrange("p (a n) -> p a n", a=2)
        NST = 8

        def xst(n):
            return (stage, xstage, arot_stage, q_stage)[n % NST // 2][:, n % 2, :]

        counts = sb("counts", [P, NX], f32)
        counts_i = sb("counts_i", [P, NX], i32)
        xtiles = sb("xtiles", [P, NX], f32)
        scan = sb("scan", [P, 4, 2 * NX], f32)
        slot_no = sb("slot_no", [P, SLOTS], f32)
        after = exps[:, 0, :, :].rearrange("p j n -> p (j n)")[:, 0:SLOTS * NX].rearrange(
            "p (s x) -> p s x", x=NX)
        slot_x = sb("slot_x", [P, SLOTS], f32)
        slot_row = sb("slot_row", [P, SLOTS], f32)
        slot_t = sb("slot_t", [P, SLOTS], f32)
        slot_u = sb("slot_u", [P, SLOTS], f32)
        slot_xi = sb("slot_xi", [P, SLOTS], i32)
        slot_ri = sb("slot_ri", [P, SLOTS], i32)
        tiles_i = sb("tiles_i", [P, NX], i32)
        PAIRS = ALL // 2
        pair = region[:, 0:PAIRS * TOPK * 2 * E * 2].bitcast(f32).rearrange(
            "p (a k t n) -> p a k t n", a=PAIRS, k=TOPK, t=2)

        def bank(name):
            return ctx.enter_context(nc.psum_tensor(name, [P, 512], f32))

        ring = [bank("ring0"), bank("ring1")]
        score = [bank("score0"), bank("score1")]
        t_ps = bank("t_ps")
        o_ps = bank("o_ps")
        y_ps = [bank("y0"), bank("y1")]

        wmod_s = q_flat[:, 0:6144].bitcast(f32).rearrange("p (c n) -> p c n", c=EC)
        wide_c = probs[:, :, :, :].rearrange("p a j n -> p (a j n)")[:, 0:EC * B * P].rearrange(
            "p (c b n) -> p c b n", c=EC, b=B)
        sign = xn[:, 0:2, :].rearrange("p t n -> p (t n)")
        absol = xn[:, 2:4, :].rearrange("p t n -> p (t n)")
        x_flat = x_s[:, :, :].rearrange("p t n -> p (t n)")
        gates_flat = gates[:, :, :, :].rearrange("p v b n -> p v (b n)")
        ga_bo_flat = ga_bo[:, :, :].rearrange("p b n -> p (b n)")
        pay_again = zrot[:, :, :].rearrange("p a n -> p (a n)").bitcast(f16)[
            :, 0:HALF * ROW].rearrange("p (t n) -> p t n", t=HALF)
        vals_of = {0: valx, 1: vals}

        s_c_in = sem("c_in")
        s_cols_in = sem("cols_in")
        s_wmod_in = sem("wmod_in")
        s_ident_in = sem("ident_in")
        s_rope_in = sem("rope_in")
        s_small_in = sem("small_in")
        s_wkv_in = [sem("wk_in"), sem("wv_in")]
        s_wq_in = sem("wq_in")
        s_silu_done = sem("silu_done")
        s_wide_done = sem("wide_done")
        s_mod_cols = sem("mod_cols")
        s_mod_wide = sem("mod_wide")
        s_wide_taken = sem("wide_taken")
        s_gates_ready = sem("gates_ready")
        s_scaled_bias = sem("scaled_bias")
        s_wkv_hi = sem("wkv_hi")
        s_wkv_lo = sem("wkv_lo")
        s_wq_hi = sem("wq_hi")
        s_wq_lo = sem("wq_lo")
        s_wo_hi = sem("wo_hi")
        s_wo_lo = sem("wo_lo")
        s_pool_ready = sem("pool_ready")
        s_variance = sem("variance")
        s_rstd_done = sem("rstd_done")
        s_normed = sem("normed")
        s_ring_filled = sem("ring_filled")
        s_ring_freed = sem("ring_freed")
        s_swapped = sem("swapped")
        s_turned = sem("turned")
        s_rotated = sem("rotated")
        s_rotated_pool = sem("rotated_pool")
        s_split_hi = sem("split_hi")
        s_split_lo = sem("split_lo")
        s_val_hi = sem("val_hi")
        s_residual = sem("residual")
        s_scored = sem("scored")
        s_maxed = sem("maxed")
        s_exped = sem("exped")
        s_summed = sem("summed")
        s_normalized = sem("normalized")
        s_probs_t = sem("probs_t")
        s_pT_hi = sem("pT_hi")
        s_pT_lo = sem("pT_lo")
        s_att_ps = sem("att_ps")
        s_att_hi = sem("att_hi")
        s_att_lo = sem("att_lo")
        s_projected = sem("projected")
        s_y_taken = sem("y_taken")
        s_y_done = sem("y_done")
        s_scaled = sem("scaled")
        s_h2_done = sem("h2_done")
        s_pay_hi = sem("pay_hi")
        s_pay_lo = sem("pay_lo")
        s_capped_s = sem("capped_s")
        s_shifted_s = sem("shifted_s")
        s_gate_exp = sem("gate_exp")
        s_placed = sem("placed")
        s_place_set = sem("place_set")
        s_routed_rows = sem("routed_rows")
        s_rows_ready = sem("rows_ready")
        s_slots_ready = sem("slots_ready")
        s_pads_written = sem("pads_written")
        s_vector_step = sem("vector_step")
        s_expert_hi = sem("expert_hi")
        s_expert_scaled = sem("expert_scaled")
        s_expert_lo = sem("expert_lo")
        s_expert_lo_pool = sem("expert_lo_pool")
        s_xT_ps = sem("xT_ps")
        s_xT_done = sem("xT_done")
        s_up_ps = sem("up_ps")
        s_gate_ps = sem("gate_ps")
        s_silu_g_done = sem("silu_g_done")
        s_inner_done = sem("inner_done")
        s_innerT_ps = sem("innerT_ps")
        s_innerT_hi = sem("innerT_hi")
        s_innerT_lo = sem("innerT_lo")
        s_down_ps = sem("down_ps")
        s_y_out = sem("y_out")
        s_first_done = sem("first_done")
        s_mixed = sem("mixed")
        s_summed_up = sem("summed_up")
        s_out_written = sem("out_written")
        s_x_in = [sem(f"x_in{i}") for i in range(4)]
        s_wo_in = [sem(f"wo_in{i}") for i in range(2)]
        s_stage_in = [sem(f"stage_in{i}") for i in range(NST)]
        s_slot_in = [sem(f"slot_in{i}") for i in range(4)]
        s_y_written = [sem(f"y_written{i}") for i in range(2)]
        s_pair_in = [sem(f"pair_in{i}") for i in range(PAIRS)]
        s_vals_crossed = [sem(f"vals_crossed{i}") for i in range(2)]
        block = ctx.enter_context(nc.Block())

        def slot_list():
            return range(FIRST_SLOT, LAST_SLOT + 1)

        def norm_in(H):
            return xn if H == 0 else stage[:, 0, :].rearrange("p (t n) -> p t n", t=HALF)

        def tail_at(k, d):
            return next((H for H in range(HALVES) if k == PER_HALF * H + d), None)

        SPLIT_AT = {e: n for n, e in enumerate(SPLIT)}
        ROPED_AT = {e: n for n, e in enumerate(ROPED)}

        def rotated(e):
            return (s_rotated_pool, ON_POOL.index(e) + 1) if e in ON_POOL else (s_rotated, ON_VECTOR.index(e) + 1)

        def split_done(n):
            return ((s_expert_lo_pool, POOL_X.index(n) + 1) if n in POOL_X
                    else (s_expert_lo, VECTOR_X.index(n) + 1))

        def bias_of(e):
            kind, i, j = e
            return (i % PER_HALF) // HALF * HG + i % HG if kind == "q" else NQ + j

        def dest(e, s):
            kind, i, j = e
            src = arot[:, SPLIT_AT[e] % NA, :]
            if kind == "q":
                return (q_s[:, i // 4 % 2, s, :, i % 4, :], src.rearrange("p (t q) -> p t q", q=64))
            if kind == "k":
                return keys[:, j, s, WINDOW + 512 * (i % 2):WINDOW + 512 * (i % 2 + 1)], src
            return hT[:, s, j, 512 * (i % 2):512 * (i % 2 + 1)], src

        @block.sync
        def _(sp):
            sp.dma_start(c_s[:, :, :], c_t).then_inc(s_c_in, 16)
            x_v = x.rearrange("(t p) n -> p t n", p=P)
            sp.dma_start(x_s[:, 0:HALF, :], x_v[:, 0:HALF, :]).then_inc(s_x_in[0], 16)
            wmod_v = wmod.rearrange("(c p) n -> p c n", p=P)
            sp.dma_start(wmod_s[:, :, 0:512], wmod_v[:, :, 0:512]).then_inc(s_cols_in, 16)
            sp.dma_start(ident_f[:, :], ident).then_inc(s_ident_in, 16)
            sp.dma_start(wk_f, wk.rearrange("(c p) n -> p c n", p=P)).then_inc(s_wkv_in[0], 16)
            for dst, src in ((bias_c[:, 0:NQ], bq), (bias_c[:, NQ:NQ + NKV], bk),
                             (bias_c[:, NQ + NKV:NQ + 2 * NKV], bv), (cos_s[:, :], cos_t), (sin_s[:, :], sin_t)):
                sp.dma_start(dst, src).then_inc(s_rope_in, 16)
            sp.dma_start(wv_f, wv.rearrange("(c p) n -> p c n", p=P)).then_inc(s_wkv_in[1], 16)
            sp.dma_start(wq_f, wq.rearrange("(c p) n -> p c n", p=P)).then_inc(s_wq_in, 16)
            sp.dma_start(wmod_s[:, :, 512:1536], wmod_v[:, :, 512:1536]).then_inc(s_wmod_in, 16)
            for dst, src in ((masks[:, :, :].bitcast(u16), mask_t), (ident_h[:, :], ident16),
                             (ident_b[:, :].bitcast(u16), identb),
                             (lower_h[:, :], lower), (tok_s[:, :, :], tokens), (base_s[:, :], bases),
                             (rev_s[:, :], reverse), (slot_no[:, :], slot_nos),
                             (wg_s[:, :, :], w_gate.rearrange("(c p) n -> p c n", p=P)),
                             (ga_bo[:, 0, :], bass.AP(bo.tensor, 0, [[0, P], [1, E]])),
                             (ga_bo[:, 1, :], bass.AP(bo.tensor, 0, [[0, P], [1, E]]))):
                sp.dma_start(dst, src).then_inc(s_small_in, 16)
            for t in range(1, ALL // HALF):
                sp.dma_start(x_s[:, t * HALF:(t + 1) * HALF, :],
                             x_v[:, t * HALF:(t + 1) * HALF, :]).then_inc(s_x_in[t], 16)
            for i in range(4):
                if i >= 2:
                    sp.wait_ge(s_wo_lo, i - 1)
                sp.dma_start(stage[:, i % 2, :].rearrange("p (h n) -> p h n", h=4),
                             wo[4 * i * HD:4 * (i + 1) * HD, :].rearrange("(h p) n -> p h n", p=P)
                             ).then_inc(s_wo_in[i % 2], 16)
            sp.wait_ge(s_pool_ready, POOL_READY)
            for H in range(HALVES):
                sp.wait_ge(s_ring_freed, NTH[("v", H, 3)] + 1)
                lo, hi = H % 2 * HALF, (H % 2 + 1) * HALF
                first = lo or 1
                for s in range(2):
                    sp.dma_start(valx[0:64, s, lo:hi, :], vals[0:64, s, lo:hi, :]
                                 ).then_inc(s_vals_crossed[H % 2], 16)
                    sp.dma_start(valx[64:P, s, first:hi, :], vals[64:P, s, first - 1:hi - 1, :]
                                 ).then_inc(s_vals_crossed[H % 2], 16)
            sp.wait_ge(s_ring_filled, NTH[("q", UNITS - 1, 0)] + 1)

            def load_expert(n):
                m = X_ORDER[n]
                e, w = m // 3, m % 3
                if n >= NST:
                    before, value = split_done(n - NST)
                    sp.wait_ge(before, value)
                elif n == 4:
                    sp.wait_ge(s_split_lo, NSPLIT)
                elif n == 6:
                    sp.wait_ge(s_scored, UNITS - HALF)
                src = ((w1, w3)[w][e].rearrange("(c p) n -> p c n", p=P) if w < 2
                       else w2[e].rearrange("(c p) n -> p c n", p=P))
                sp.dma_start(xst(n).rearrange("p (c n) -> p c n", c=EC if w < 2 else INNER // P),
                             src).then_inc(s_stage_in[n % NST], 16)

            for n in range(3 * NX):
                load_expert(n)
            sp.dma_start(routed[UNUSED_ROW:UNUSED_ROW + P, :], pad[:, :]).then_inc(s_pads_written, 16)
            sp.wait_ge(s_rows_ready, 1)
            for e in range(NX):
                row = nc.sync.value_load(counts_i[0:1, e:e + 1], min_val=0, max_val=ROWS - P)
                sp.dma_start(routed[bass.ds(row, P), :], pad[:, :]).then_inc(s_pads_written, 16)
            sp.wait_ge(s_routed_rows, HALVES * TOPK * HALF * 16)
            sp.wait_ge(s_pads_written, 16 * (NX + 1))
            sp.wait_ge(s_slots_ready, 1)
            sp.wait_ge(s_expert_lo, len(VECTOR_X) - 4)

            def load_slot(i, a, first):
                row = nc.sync.value_load(slot_ri[0:1, bass.ds(i * 4 + a, 1)] if not isinstance(i, int)
                                         else slot_ri[0:1, i * 4 + a:i * 4 + a + 1], min_val=0, max_val=ROWS - P)
                if not first:
                    sp.wait_ge(s_y_written[a % 2], (i * 2 + a // 2 - 1) * 16)
                sp.dma_start(x_rows[:, a, :], routed[bass.ds(row, P), :]).then_inc(s_slot_in[a], 16)

            for a in range(4):
                load_slot(0, a, True)
            with sp.Fori(1, SLOTS // 4) as i:
                for a in range(4):
                    load_slot(i, a, False)
            for a in range(SLOTS % 4):
                load_slot(SLOTS // 4, a, False)
            for a in range(2):
                sp.wait_ge(s_y_written[a], (SLOTS + 1 - a) // 2 * 16)
            res_v = results.rearrange("(k t p) n -> p k t n", k=TOPK, p=P)
            out_v = out.rearrange("(t p) n -> p t n", p=P)
            for n in range(PAIRS):
                for k in range(TOPK):
                    sp.dma_start(pair[:, n, k, :, :], res_v[:, k, 2 * n:2 * n + 2, :]).then_inc(s_pair_in[n], 16)
            for n in range(PAIRS):
                sp.wait_ge(s_summed_up, n + 1)
                sp.dma_start(out_v[:, 2 * n:2 * n + 2, :], x_s[:, 2 * n:2 * n + 2, :]).then_inc(s_out_written, 16)
            sp.wait_ge(s_out_written, 16 * PAIRS)

        @block.tensor
        def _(pe):
            mm = nc.tensor.matmul

            def three(out_ap, lhs, rhs, first, last):
                mm(out_ap, lhs(0), rhs(0), start=first, stop=False)
                mm(out_ap, lhs(0), rhs(1), start=False, stop=False)
                return mm(out_ap, lhs(1), rhs(0), start=False, stop=last)

            pe.wait_ge(s_cols_in, 16)
            pe.wait_ge(s_silu_done, 1)
            for v in range(4):
                for c in range(EC):
                    last = mm(score[0][:, B * v:B * (v + 1)], wmod_s[:, c, v * P:(v + 1) * P], silu_c[:, c, :],
                              start=(c == 0), stop=(c == EC - 1))
            last.then_inc(s_mod_cols, 1)

            def modulation(i):
                if i == 0:
                    pe.wait_ge(s_wmod_in, 16)
                    pe.wait_ge(s_wide_done, 1)
                for c in range(EC):
                    last = mm((t_ps, o_ps, y_ps[0], y_ps[1])[i][:, :], wide_c[:, c, i // 2, :],
                              wmod_s[:, c, 512 * (i % 2 + 1):512 * (i % 2 + 2)], start=(c == 0), stop=(c == EC - 1))
                last.then_inc(s_mod_wide, 1)

            def entry(e):
                kind, i, j = e
                n = NTH[e]
                bank = ring[n % 2]
                if n >= 2:
                    pe.wait_ge(s_ring_freed, n - 1)
                if kind == "ln":
                    if i == 0:
                        pe.wait_ge(s_ident_in, 16)
                    pe.wait_ge(s_normed, i + 1)
                    for t in range(HALF):
                        last = nc.tensor.transpose(bank[:, t * P:(t + 1) * P], norm_in(i)[:, t, j * P:(j + 1) * P],
                                                   ident_f[:, :])
                elif kind in "kq":
                    half = i if kind == "k" else i // PER_HALF
                    cols = slice(half % 2 * 512, (half % 2 + 1) * 512)
                    if kind == "k":
                        w, at = wk_s, j * HD
                        if e == ("k", 0, 0):
                            pe.wait_ge(s_wkv_lo, 1)
                    else:
                        w, at = wq_s, bias_of(e) * HD
                        if i == 0:
                            pe.wait_ge(s_wq_lo, 2 * EC)
                    pe.wait_ge(s_split_lo, SPLIT_AT[("ln", half, 1)] + 1)
                    for c in range(EC):
                        last = three(bank[:, :], lambda s: w[:, s, c, at:at + HD],
                                     lambda s: hT[:, s, c, cols], c == 0, c == EC - 1)
                elif kind == "v":
                    at = (i % 2 * HALF + j) * P
                    rows = slice(at, at + P)
                    if e == ("v", 0, 0):
                        pe.wait_ge(s_wkv_lo, 2)
                    pe.wait_ge(s_split_lo, SPLIT_AT[("ln", i, 1)] + 1)
                    for c in range(EC):
                        last = three(bank[:, :], lambda s: hT[:, s, c, rows], lambda s: wv_s[:, s, c, :],
                                     c == 0, c == EC - 1)
                elif kind == "lt":
                    pe.wait_ge(s_h2_done, i + 1)
                    for t in range(2):
                        for c in range(EC):
                            last = nc.tensor.transpose(bank[:, (2 * t + c) * P:(2 * t + c + 1) * P],
                                                       xn[:, 2 * j + t, c * P:(c + 1) * P], ident_f[:, :])
                elif kind == "lg":
                    pe.wait_ge(s_ring_freed, NTH[("lt", i, 1)] + 1)
                    for t in range(HALF):
                        for c in range(EC):
                            at = (2 * (t % 2) + c) * P
                            last = mm(bank[:, t * NX:(t + 1) * NX], h2T[:, t // 2, at:at + P], wg_s[:, c, :],
                                      start=(c == 0), stop=(c == EC - 1))
                else:
                    pe.wait_ge(s_shifted_s, i + 1)
                    width = (HALF + 1) * NX
                    mm(bank[:, 0:width], lower_h[:, :], chosen[:, :, :].rearrange("p t n -> p (t n)"),
                       start=True, stop=False)
                    for t in range(HALF):
                        m = HALF - t
                        last = mm(bank[:, (t + 1) * NX:width].rearrange("p (t n) -> p t n", n=NX), ones_h[:, :],
                                  chosen[:, t:t + 1, :].to_broadcast([P, m, NX]), start=False, stop=(m == 1))
                last.then_inc(s_ring_filled, 1)

            def where(k):
                h = k // PER_HALF
                return h, k // HALF % NKV, HALF * (h % 2) + k % HALF

            def scores(k):
                h, g, t = where(k)
                if k >= 2:
                    pe.wait_ge(s_exped, k - 1)
                if k == 0:
                    pe.wait_ge(s_small_in, SMALL_IN)
                    pe.wait_ge(s_pool_ready, POOL_READY)
                if k % 4 == 0:
                    need = max(SPLIT_AT[("q", k + 3, 0)], SPLIT_AT[("k", h, g)])
                    pe.wait_ge(s_split_lo, need + 1)
                bank = score[k % 2]
                mm(bank[:, :], ident_b[:, :], masks[:, 1 if t == 0 else 0, :], start=True, stop=False)
                for blk in range(2):
                    for hp in range(2):
                        cols = bank[:, (2 * blk + hp) * P:(2 * blk + hp + 1) * P]

                        def kk(s):
                            if blk:
                                at = WINDOW + t * P
                                return keys[:, g, s, at:at + P]
                            v = keys[:, g, s, 0:P]
                            return bass.AP(v.tensor, v.offset + WINDOW + t * P,
                                           [list(v.ap[0]), [-WINDOW, 2], [1, WINDOW]])

                        def qq(s):
                            return q_s[:, k // 4 % 2, s, 2 * (t % HALF) + blk, 2 * hp:2 * hp + 2, :].rearrange(
                                "p h q -> p (h q)")
                        mm(cols, qq(0), kk(0), start=False, stop=False)
                        mm(cols, qq(0), kk(1), start=False, stop=False)
                        last = mm(cols, qq(1), kk(0), start=False, stop=(blk == 1 and hp == 1))
                last.then_inc(s_scored, 1)

            def transposed(k):
                pe.wait_ge(s_normalized, k + 1)
                if k == 0:
                    pe.wait_ge(s_wide_taken, 4)
                if k >= 1:
                    pe.wait_ge(s_pT_lo, k)
                for j in range(4):
                    last = nc.tensor.transpose(t_ps[:, j * P:(j + 1) * P], probs[:, k % 2, j, :], ident_f[:, :])
                last.then_inc(s_probs_t, 1)

            def attend(k):
                h, g, t = where(k)
                pe.wait_ge(s_pT_lo, k + 1)
                if k >= 1:
                    pe.wait_ge(s_att_lo, k)
                if k % PER_HALF == 0:
                    pe.wait_ge(s_vals_crossed[h % 2], (h // 2 + 1) * 64)
                o_v = o_ps[:, :].rearrange("p (h n) -> p h n", h=HG)
                for blk in range(2):
                    v = vals_of[blk]
                    last = three(o_v[:, :, blk * 64:(blk + 1) * 64],
                                 lambda s: v[:, s, t, g * HD:(g + 1) * HD],
                                 lambda s: pT[:, k % 2, s, blk * 256:(blk + 1) * 256].rearrange(
                                     "p (h n) -> p h n", h=HG), True, True)
                last.then_inc(s_att_ps, 1)

            def project(k):
                h, g, t = where(k)
                u = k % 4
                pe.wait_ge(s_att_lo, k + 1)
                if h >= 1 and g == 0 and u % 2 == 0:
                    pe.wait_ge(s_y_taken, 2 * h - 1 + u // 2)
                if k == 0:
                    pe.wait_ge(s_wo_lo, 4)
                cols = y_ps[u // 2][:, (u % 2) * E:(u % 2 + 1) * E]
                for n in range(HG):
                    for i, (sa, sw) in enumerate(((0, 0), (0, 1), (1, 0))):
                        last = mm(cols, att[:, k % 2, sa, n, :], wo_s[:, sw, g * HG + n, :],
                                  start=(g == 0 and n == 0 and i == 0 and u % 2 == 0),
                                  stop=(g == 3 and n == 3 and i == 2), skip_group_check=True)
                last.then_inc(s_projected, 1)

            for k in slot_list():
                if 0 <= k < UNITS:
                    scores(k)
                for e in RING.get(k, ()):
                    entry(e)
                if -7 <= k < -3:
                    modulation(k + 7)
                if 0 <= k - 1 < UNITS:
                    transposed(k - 1)
                if 0 <= k - 2 < UNITS:
                    attend(k - 2)
                if 0 <= k - 3 < UNITS:
                    project(k - 3)

            pe.wait_ge(s_expert_lo, len(VECTOR_X))
            pe.wait_ge(s_expert_lo_pool, len(POOL_X))
            pe.wait_ge(s_slots_ready, 1)
            x_ps, it_ps, d_ps = ring[0], t_ps, o_ps
            x_ps_h = x_ps[:, :].bitcast(f16)

            def rows_t(s, i, a, first):
                pe.wait_ge(s_slot_in[a], (i + 1) * 16)
                if not first:
                    pe.wait_ge(s_xT_done, s)
                for q in range(4):
                    last = nc.tensor.transpose(x_ps_h[:, q * P:(q + 1) * P], x_rows[:, a, q * P:(q + 1) * P],
                                               ident_h[:, :])
                last.then_inc(s_xT_ps, 1)

            def up(s, a, early):
                e = nc.tensor.value_load(slot_xi[0:1, bass.ds(s, 1)] if not isinstance(s, int)
                                         else slot_xi[0:1, s:s + 1], min_val=0, max_val=NX - 1)
                pe.wait_ge(s_xT_done, s + 1)
                if not early:
                    pe.wait_ge(s_inner_done, s - 1)
                for w, (bank, done) in enumerate(((score[a % 2], s_up_ps), (y_ps[a % 2], s_gate_ps))):
                    for c in range(EC):
                        last = three(bank[:, :], lambda q: xT[:, a % 2, (2 * q + c) * P:(2 * q + c + 1) * P],
                                     lambda q: region[:, bass.ds(e * PER_X + ((2 * w + q) * EC + c) * INNER, INNER)],
                                     c == 0, c == EC - 1)
                    last.then_inc(done, 1)

            def inner_t(s, a, first):
                pe.wait_ge(s_inner_done, s + 1)
                if not first:
                    pe.wait_ge(s_innerT_lo, s)
                for q in range(4):
                    last = nc.tensor.transpose(it_ps[:, q * P:(q + 1) * P], inner[:, a % 2, q * P:(q + 1) * P],
                                               ident_f[:, :])
                last.then_inc(s_innerT_ps, 1)

            def down(s, a, first):
                e = nc.tensor.value_load(slot_xi[0:1, bass.ds(s, 1)] if not isinstance(s, int)
                                         else slot_xi[0:1, s:s + 1], min_val=0, max_val=NX - 1)
                pe.wait_ge(s_innerT_lo, s + 1)
                if not first:
                    pe.wait_ge(s_y_out, s)
                for c in range(INNER // P):
                    last = three(d_ps[:, 0:E], lambda q: innerT[:, a % 2, q, c * P:(c + 1) * P],
                                 lambda q: region[:, bass.ds(e * PER_X + 4 * 1024 + q * 1024 + c * E, E)],
                                 c == 0, c == INNER // P - 1)
                last.then_inc(s_down_ps, 1)

            def slot(i, a, head):
                s = i * 4 + a
                rows_t(s, i, a, head and a == 0)
                if not head or a >= 2:
                    down(s - 2, a - 2, head and a == 2)
                if not head or a >= 1:
                    inner_t(s - 1, a - 1, head and a == 1)
                up(s, a, head and a < 2)

            for a in range(4):
                slot(0, a, True)
            with pe.Fori(1, SLOTS // 4) as i:
                for a in range(4):
                    slot(i, a, False)
            for a in range(SLOTS % 4):
                slot(SLOTS // 4, a, False)
            down(SLOTS - 2, SLOTS - 2, False)
            inner_t(SLOTS - 1, SLOTS - 1, False)
            down(SLOTS - 1, SLOTS - 1, False)

        @block.scalar
        def _(act):
            A = nc.scalar.activation
            act.wait_ge(s_c_in, 16)
            A(silu_c[:, :, :], c_s[:, :, :], ACT.Silu).then_inc(s_silu_done, 1)
            def split_wkv(i):
                act.wait_ge(s_wkv_in[i], 16)
                A((wk_s, wv_s)[i][:, 0], (wk_f, wv_f)[i], ACT.Copy, scale=(W_SCALE * K_SCALE, W_SCALE)[i]
                  ).then_inc(s_wkv_hi, 1)

            def split_wq(c):
                if c == 0:
                    act.wait_ge(s_wq_in, 16)
                for n in range(2):
                    A(wq_s[:, 0, c, n * 1024:(n + 1) * 1024], wq_f[:, c, n * 1024:(n + 1) * 1024],
                      ACT.Copy, scale=W_SCALE).then_inc(s_wq_hi, 1)

            def split_wo(i):
                act.wait_ge(s_wo_in[i % 2], 16 * (i // 2 + 1))
                A(wo_s[:, 0, 4 * i:4 * (i + 1), :], stage[:, i % 2, :].rearrange("p (h n) -> p h n", h=4),
                  ACT.Copy, scale=W_SCALE).then_inc(s_wo_hi, 1)

            split_wkv(0)
            split_wkv(1)
            act.wait_ge(s_scaled_bias, 1)

            def split_expert(n):
                m = X_ORDER[n]
                if n == 0:
                    act.wait_ge(s_ring_filled, NTH[("q", UNITS - 1, 0)] + 1)
                elif m in (6, 8):
                    act.wait_ge(s_projected, UNITS - 2 * HALF)
                elif m in (10, 11, 12):
                    act.wait_ge(s_scored, UNITS - HALF * (12 - m) - HALF)
                elif m in (7, 13):
                    act.wait_ge(s_projected, UNITS)
                act.wait_ge(s_stage_in[n % NST], 16 * (n // NST + 1))
                at = m // 3 * PER_X + m % 3 * 2048
                A(region[:, at:at + 1024], xst(n), ACT.Copy, scale=W_SCALE).then_inc(s_expert_hi, 1)
                if n in POOL_X:
                    act.wait_ge(s_expert_hi, n + 1)
                    A(xst(n), xst(n), ACT.Copy, scale=W_SCALE).then_inc(s_expert_scaled, 1)

            def swap(e):
                r, n = ROPED_AT[e], NTH[e]
                act.wait_ge(s_ring_filled, n + 1)
                if r >= NZ:
                    before, value = rotated(ROPED[r - NZ])
                    act.wait_ge(before, value)
                col = bias_of(e)
                z = zrot[:, r % NZ, :]
                bank = ring[n % 2]
                A(z[0:64], bank[64:P, :], ACT.Identity, bias=bias_c[64:P, col:col + 1])
                A(z[64:P], bank[0:64, :], ACT.Identity, bias=bias_c[0:64, col:col + 1]).then_inc(s_swapped, 1)

            for k in slot_list():
                if 0 <= k - 2 < UNITS:
                    u = k - 2
                    act.wait_ge(s_probs_t, u + 1)
                    if u >= 2:
                        act.wait_ge(s_att_ps, u - 1)
                    A(pT[:, u % 2, 0, :], t_ps[:, :], ACT.Copy, scale=P_SCALE).then_inc(s_pT_hi, 1)
                if 0 <= k - 3 < UNITS:
                    u = k - 3
                    g = u // HALF % NKV
                    act.wait_ge(s_att_ps, u + 1)
                    if u >= 2:
                        act.wait_ge(s_projected, u - 1)
                    A(att[:, u % 2, 0].rearrange("p h n -> p (h n)"), o_ps[:, :], ACT.Identity,
                      bias=bias_c[:, NQ + NKV + g:NQ + NKV + g + 1]).then_inc(s_att_hi, 1)
                if 0 <= k < UNITS:
                    act.wait_ge(s_maxed, k + 1)
                    if k >= 2:
                        act.wait_ge(s_normalized, k - 1)
                    for j in range(4):
                        last = A(exps[:, k % 2, j, :], score[k % 2][:, j * P:(j + 1) * P], ACT.Exp,
                                 bias=neg_max[:, k % 2, j:j + 1], accum_out=row_sum[:, k % 2, j:j + 1])
                    last.then_inc(s_exped, 1)
                for e in RING.get(k, ()):
                    if e[0] in "qk":
                        swap(e)
                    elif e[0] == "v":
                        act.wait_ge(s_ring_filled, NTH[e] + 1)
                        if e[1] >= 2:
                            act.wait_ge(s_att_ps, PER_HALF * (e[1] - 1))
                            if e[1] % 2 == 0 and e[2] == 3:
                                act.wait_ge(s_att_ps, PER_HALF * (e[1] - 1) + 1)
                        A(vals[:, 0, e[1] % 2 * HALF + e[2], :], ring[NTH[e] % 2][:, :], ACT.Copy,
                          scale=1 / W_SCALE).then_inc(s_val_hi, 1)
                for e in RING.get(k - 1, ()):
                    if e in SPLIT_AT:
                        if e[0] == "ln":
                            act.wait_ge(s_ring_freed, NTH[e] + 1)
                        else:
                            turned_sum, value = rotated(e)
                            act.wait_ge(turned_sum, value)
                        if e == ("q", 0, 0):
                            act.wait_ge(s_mod_wide, 4)
                        if e[0] == "q" and e[1] >= 8:
                            act.wait_ge(s_scored, e[1] // 4 * 4 - 4)
                        if e[0] == "k" and e[1] >= 2:
                            last_use = (PER_HALF * (e[1] - 1) + HALF * e[2] if e[1] % 2 == 0
                                        else PER_HALF * (e[1] - 2) + HALF * e[2] + 3)
                            act.wait_ge(s_scored, last_use + 1)
                        dst, src = dest(e, 0)
                        A(dst, src, ACT.Copy).then_inc(s_split_hi, 1)
                if k in (-8, -7):
                    split_wq(k + 8)
                if -6 <= k < -2:
                    split_wo(k + 6)
                if -7 <= k < -3:
                    bb, v = divmod(k + 7, 2)
                    act.wait_ge(s_mod_wide, k + 8)
                    A(gates[:, 2 * v:2 * v + 2, bb, :],
                      (t_ps, o_ps, y_ps[0], y_ps[1])[k + 7][:, :].rearrange("p (v n) -> p v n", v=2),
                      ACT.Copy).then_inc(s_wide_taken, 1)
                h = tail_at(k, 23)
                if h is not None:
                    act.wait_ge(s_h2_done, h + 1)
                    if h:
                        act.wait_ge(s_routed_rows, h * 128)
                    A(pay[:, :, 0:E], xn[:, :, :], ACT.Copy).then_inc(s_pay_hi, 1)
                    if h == HALVES - 1:
                        A(pay_again[:, :, 0:E], xn[:, :, :], ACT.Copy).then_inc(s_pay_hi, 1)
                h = tail_at(k, 27)
                if h is not None:
                    act.wait_ge(s_ring_freed, NTH[("lg", h, 0)] + 1)
                    A(capped[:, :, :], logit[:, :, :], ACT.Tanh, scale=1 / SOFTCAP).then_inc(s_capped_s, 1)
                h = tail_at(k, 30)
                if h is not None:
                    act.wait_ge(s_shifted_s, h + 1)
                    A(eg[:, :, :], shifted[:, :, :], ACT.Exp, scale=SOFTCAP).then_inc(s_gate_exp, 1)
                for n in SPLIT_HI.get(k, ()):
                    split_expert(n)

            for n in range(LATE_X, 3 * NX):
                split_expert(n)

            def inner_hi(s, a, early):
                act.wait_ge(s_innerT_ps, s + 1)
                if not early:
                    act.wait_ge(s_down_ps, s - 1)
                A(innerT[:, a % 2, 0, :], t_ps[:, :], ACT.Copy).then_inc(s_innerT_hi, 1)

            def result(s, half, a, early):
                act.wait_ge(s_down_ps, s + 1)
                if not early:
                    act.wait_ge(s_y_written[a % 2], half * 16)
                A(y_s[:, a % 2, :], o_ps[:, 0:E], ACT.Copy, scale=1 / W_SCALE).then_inc(s_y_out, 1)

            def slot(i, a, head):
                s = i * 4 + a
                if not head or a >= 1:
                    inner_hi(s - 1, a - 1, head and a < 3)
                if not head or a >= 2:
                    result(s - 2, i * 2 + a // 2 - 1, a - 2, head)
                act.wait_ge(s_up_ps, s + 1)
                if not head or a >= 2:
                    act.wait_ge(s_inner_done, s - 1)
                A(silu_g[:, a % 2, :], score[a % 2][:, :], ACT.Silu, scale=1 / W_SCALE
                  ).then_inc(s_silu_g_done, 1)

            for a in range(4):
                slot(0, a, True)
            with act.Fori(1, SLOTS // 4) as i:
                for a in range(4):
                    slot(i, a, False)
            for a in range(SLOTS % 4):
                slot(SLOTS // 4, a, False)
            result(SLOTS - 2, (SLOTS - 2) // 2, SLOTS - 2, False)
            inner_hi(SLOTS - 1, SLOTS - 1, False)
            result(SLOTS - 1, (SLOTS - 1) // 2, SLOTS - 1, False)
            for n in range(PAIRS):
                act.wait_ge(s_pair_in[n], 32)
                for t in range(2):
                    last = A(pair[:, n, 0, t, :], pair[:, n, 0, t, :], ACT.Copy,
                             scale=weight[:, 0, 2 * n + t:2 * n + t + 1])
                last.then_inc(s_first_done, 1)

        @block.vector
        def _(dve):
            V = nc.vector
            done = [0]

            def link(ins):
                done[0] += 1
                ins.then_inc(s_vector_step, 1)
                dve.wait_ge(s_vector_step, done[0])

            S_ = V.scalar_tensor_tensor

            dve.wait_ge(s_silu_done, 1)
            for c in range(EC):
                last = V.tensor_copy(wide_c[:, c], silu_c[:, c, :].unsqueeze(2).to_broadcast([P, B, P]))
            last.then_inc(s_wide_done, 1)

            def modulation_and_biases():
                dve.wait_ge(s_mod_cols, 1)
                V.tensor_copy(mod_c[:, 0:2, :], score[0][:, 0:4].rearrange("p (c b) -> p c b", b=B))
                V.tensor_scalar(mod_c[:, 2:4, :], score[0][:, 4:8].rearrange("p (c b) -> p c b", b=B), 1.0, None,
                                ALU.add)
                dve.wait_ge(s_rope_in, ROPE_IN)
                V.tensor_scalar(bias_c[:, 0:NQ], bias_c[:, 0:NQ], W_SCALE, None, ALU.mult)
                V.tensor_scalar(bias_c[:, NQ:NQ + NKV], bias_c[:, NQ:NQ + NKV], W_SCALE * K_SCALE, None, ALU.mult)
                V.tensor_scalar(bias_c[:, NQ + NKV:NQ + 2 * NKV], bias_c[:, NQ + NKV:NQ + 2 * NKV], P_SCALE,
                                None, ALU.mult).then_inc(s_scaled_bias, 1)
                dve.wait_ge(s_scaled_bias, 1)

            def split_wk():
                dve.wait_ge(s_wkv_hi, 1)
                S_(wk_s[:, 1], wk_f, W_SCALE * K_SCALE, wk_s[:, 0], ALU.mult, ALU.subtract).then_inc(s_wkv_lo, 1)

            def split_wv():
                dve.wait_ge(s_wkv_hi, 2)
                S_(wv_s[:, 1], wv_f, W_SCALE, wv_s[:, 0], ALU.mult, ALU.subtract).then_inc(s_wkv_lo, 1)

            def split_wq(c):
                for n in range(2):
                    dve.wait_ge(s_wq_hi, 2 * c + n + 1)
                    S_(wq_s[:, 1, c, n * 1024:(n + 1) * 1024], wq_f[:, c, n * 1024:(n + 1) * 1024], W_SCALE,
                       wq_s[:, 0, c, n * 1024:(n + 1) * 1024], ALU.mult, ALU.subtract).then_inc(s_wq_lo, 1)

            def split_wo(i):
                dve.wait_ge(s_wo_hi, i + 1)
                S_(wo_s[:, 1, 4 * i:4 * (i + 1), :], stage[:, i % 2, :].rearrange("p (h n) -> p h n", h=4), W_SCALE,
                   wo_s[:, 0, 4 * i:4 * (i + 1), :], ALU.mult, ALU.subtract).then_inc(s_wo_lo, 1)

            def form_gates(i):
                gv = gates_flat[:, (0, 3)[i // 4 % 2], :]
                if i == 8:
                    link(V.tensor_tensor(ga_bo_flat, ga_bo_flat, gates_flat[:, 0, :], ALU.mult))
                elif i == 9:
                    V.tensor_scalar(gates_flat[:, 0, :], gates_flat[:, 0, :], 1 / (W_SCALE * P_SCALE), None,
                                    ALU.mult)
                    V.tensor_copy(used_rows[:, :], base_s[:, :])
                    V.tensor_scalar(gates_flat[:, 2, :], gates_flat[:, 2, :], 1.0, None, ALU.add
                                    ).then_inc(s_gates_ready, 1)
                elif i % 4 == 0:
                    link(V.tensor_scalar(sign, gv, 0.0, 2.0, ALU.is_ge, ALU.mult))
                elif i % 4 == 1:
                    link(V.tensor_scalar(sign, sign, -1.0, None, ALU.add))
                elif i % 4 == 2:
                    link(S_(absol, gv, -1.0, gv, ALU.mult, ALU.max))
                else:
                    link(S_(gv, absol, 0.25, sign, ALU.max, ALU.mult))

            def split_expert(n):
                dve.wait_ge(s_expert_hi, n + 1)
                at = X_ORDER[n] // 3 * PER_X + X_ORDER[n] % 3 * 2048
                S_(region[:, at + 1024:at + 2048], xst(n), W_SCALE, region[:, at:at + 1024],
                   ALU.mult, ALU.subtract).then_inc(s_expert_lo, 1)

            def xt(t, n=1):
                return x_flat[:, t * E:(t + n) * E]

            def statistics(n):
                _, which, H = NORMS[n]
                if which == "in":
                    dve.wait_ge(s_x_in[H], 16)
                else:
                    dve.wait_ge(s_y_done, 2 * H + 2)
                for i in range(HALF):
                    last = V.bn_stats(stats[:, i, :], xt(HALF * H + i))
                link(last)
                for i in range(HALF):
                    last = V.bn_aggr(mean_var[:, i, :], stats[:, i, :])
                link(last)
                V.tensor_scalar(var_eps[:, :], mean_var[:, :, 1], EPS, None, ALU.add).then_inc(s_variance, 1)

            def normalize(n):
                _, which, H = NORMS[n]
                dve.wait_ge(s_rstd_done, n + 1)
                if which == "in":
                    if H == 1:
                        dve.wait_ge(s_wo_lo, 3)
                    for i in range(HALF):
                        last = V.tensor_scalar(norm_in(H)[:, i, :], xt(HALF * H + i), mean_var[:, i, 0:1],
                                               rstd[:, i:i + 1], ALU.subtract, ALU.mult)
                    last.then_inc(s_normed, 1)
                else:
                    for i in range(HALF):
                        last = S_(xn[:, i, :], xt(HALF * H + i), mean_var[:, i, 0:1], gates[:, 2, H // 2, :],
                                  ALU.subtract, ALU.mult)
                    last.then_inc(s_scaled, 1)

            def modulate(H):
                dve.wait_ge(s_scaled, H + 1)
                for i in range(HALF):
                    last = S_(xn[:, i, :], xn[:, i, :], rstd[:, i:i + 1], gates[:, 1, H // 2, :], ALU.mult, ALU.add)
                last.then_inc(s_h2_done, 1)

            def take(e):
                kind, i, j = e
                n = NTH[e]
                bank = ring[n % 2]
                if e in SPLIT_AT and SPLIT_AT[e] >= NA:
                    dve.wait_ge(s_split_lo, SPLIT_AT[e] - NA + 1)
                if kind in "kq":
                    col = bias_of(e)
                    half = (i if kind == "k" else i // PER_HALF) % 2
                    dve.wait_ge(s_swapped, ROPED_AT[e] + 1)
                    last = S_(arot[:, SPLIT_AT[e] % NA, :], bank[:, :], bias_c[:, col:col + 1],
                              cos_s[:, half * 512:(half + 1) * 512], ALU.add, ALU.mult)
                elif kind == "v":
                    dve.wait_ge(s_val_hi, VAL_AT[e] + 1)
                    t = i % 2 * HALF + j
                    last = S_(vals[:, 1, t, :], bank[:, :], 1 / W_SCALE, vals[:, 0, t, :],
                              ALU.mult, ALU.subtract)
                else:
                    dve.wait_ge(s_ring_filled, n + 1)
                    if kind == "ln":
                        last = V.tensor_scalar(arot[:, SPLIT_AT[e] % NA, :], bank[:, :],
                                               mod_c[:, 2 + j, i // 2:i // 2 + 1], mod_c[:, j, i // 2:i // 2 + 1],
                                               ALU.mult, ALU.add)
                    elif kind == "lt":
                        last = V.tensor_copy(h2T[:, j, :], bank[:, :])
                    elif kind == "lg":
                        last = V.tensor_copy(logit[:, :, :].rearrange("p t n -> p (t n)"), bank[:, 0:HALF * NX])
                    else:
                        link(V.tensor_tensor(place[:, :, :], bank[:, 0:HALF * NX].rearrange(
                            "p (t n) -> p t n", n=NX), used_rows[:, :].unsqueeze(1).to_broadcast(G), ALU.add))
                        last = V.tensor_tensor(used_rows[:, :], bank[:, HALF * NX:(HALF + 1) * NX],
                                               used_rows[:, :], ALU.add)
                last.then_inc(s_ring_freed, 1)

            def rotate(e):
                r, a = ROPED_AT[e], arot[:, SPLIT_AT[e] % NA, :]
                dve.wait_ge(s_turned, r + 1)
                dve.wait_ge(s_ring_freed, NTH[e] + 1)
                V.tensor_tensor(a, a, zrot[:, r % NZ, :], ALU.add).then_inc(s_rotated, 1)

            def low(e):
                dve.wait_ge(s_split_hi, SPLIT_AT[e] + 1)
                (hi, src), (lo, _) = dest(e, 0), dest(e, 1)
                V.tensor_tensor(lo, src, hi, ALU.subtract).then_inc(s_split_lo, 1)

            def residual(h, q):
                dve.wait_ge(s_projected, PER_HALF * h + 12 + 2 * q + 2)
                dve.wait_ge(s_residual, HALF * h + 2 * q + 2)
                ga2 = gates[:, 0, h // 2, :].unsqueeze(1).to_broadcast([P, 2, E])
                tmp2 = xn[:, 2 * q:2 * q + 2, :]
                V.tensor_tensor(tmp2, y_ps[q][:, :].rearrange("p (t n) -> p t n", t=2), ga2, ALU.mult
                                ).then_inc(s_y_taken, 1)
                dve.wait_ge(s_y_taken, 2 * h + q + 1)
                x2 = xt(HALF * h + 2 * q, 2).rearrange("p (t n) -> p t n", t=2)
                V.tensor_tensor(x2, x2, tmp2, ALU.add).then_inc(s_y_done, 1)

            def pick(one, score_ap):
                link(V.tensor_reduce(best[:, :], score_ap, X, ALU.max))
                link(V.tensor_tensor(key[:, :, :], score_ap, best[:, :].unsqueeze(2).to_broadcast(G),
                                      ALU.is_equal))
                link(V.tensor_tensor(key[:, :, :], key[:, :, :], rev_s[:, :].unsqueeze(1).to_broadcast(G),
                                      ALU.mult))
                link(V.tensor_reduce(gw[:, :], key[:, :, :], X, ALU.max))
                link(V.tensor_tensor(one[:, :, :], key[:, :, :], gw[:, :].unsqueeze(2).to_broadcast(G),
                                      ALU.is_equal))

            def gate_choice(h):
                dve.wait_ge(s_capped_s, h + 1)
                pick(one1, capped[:, :, :])
                V.tensor_tensor(shifted[:, :, :], capped[:, :, :], best[:, :].unsqueeze(2).to_broadcast(G),
                                ALU.subtract)
                link(S_(tmp[:, :, :], one1[:, :, :], -4.0, capped[:, :, :], ALU.mult, ALU.add))

            def second_choice(h):
                pick(one2, tmp[:, :, :])
                V.tensor_tensor(chosen[:, 0:HALF, :], one1[:, :, :], one2[:, :, :], ALU.add
                                ).then_inc(s_shifted_s, 1)

            def gate_weights(h):
                dve.wait_ge(s_gate_exp, h + 1)
                link(V.tensor_reduce(gsum[:, :], eg[:, :, :], X, ALU.add))
                link(V.reciprocal(ginv[:, :], gsum[:, :]))
                for k, one in enumerate((one1, one2)):
                    link(V.tensor_tensor(tmp[:, :, :], eg[:, :, :], one[:, :, :], ALU.mult))
                    link(V.tensor_reduce(gw[:, :], tmp[:, :, :], X, ALU.add))
                    link(V.tensor_tensor(weight[:, k, HALF * h:HALF * (h + 1)], gw[:, :], ginv[:, :],
                                          ALU.mult))

            def placing(h):
                if h:
                    dve.wait_ge(s_routed_rows, h * 128)
                for k, one in enumerate((one1, one2)):
                    link(V.tensor_tensor(tmp[:, :, :], place[:, :, :], one[:, :, :], ALU.mult))
                    link(V.tensor_reduce(gplace[:, :], tmp[:, :, :], X, ALU.add))
                    last = V.tensor_copy(rows_i[:, k, :], gplace[:, :])
                    if k == 0:
                        link(last)
                last.then_inc(s_placed, 1)

            def row_max(k):
                if 0 <= k < UNITS:
                    dve.wait_ge(s_scored, k + 1)
                    V.tensor_reduce(neg_max[:, k % 2, :], score[k % 2][:, :].rearrange("p (j n) -> p j n", j=4),
                                    X, ALU.max, negate=True).then_inc(s_maxed, 1)

            for k in slot_list():
                if k == FIRST_SLOT + 1:
                    modulation_and_biases()
                    split_wk()
                crowded = max(len(RING.get(k, ())), len(RING.get(k - 1, ()))) > 1
                if crowded:
                    for e in RING.get(k - 1, ()):
                        take(e)
                    row_max(k)
                if 0 <= k - 2 < UNITS:
                    u = k - 2
                    dve.wait_ge(s_pT_hi, u + 1)
                    S_(pT[:, u % 2, 1, :], t_ps[:, :], P_SCALE, pT[:, u % 2, 0, :], ALU.mult, ALU.subtract
                       ).then_inc(s_pT_lo, 1)
                if not crowded:
                    row_max(k)
                if 0 <= k - 3 < UNITS:
                    u = k - 3
                    g = u // HALF % NKV
                    dve.wait_ge(s_att_hi, u + 1)
                    S_(att[:, u % 2, 1].rearrange("p h n -> p (h n)"), o_ps[:, :],
                       bias_c[:, NQ + NKV + g:NQ + NKV + g + 1],
                       att[:, u % 2, 0].rearrange("p h n -> p (h n)"), ALU.add, ALU.subtract
                       ).then_inc(s_att_lo, 1)
                if not crowded:
                    for e in RING.get(k - 1, ()):
                        take(e)
                if 0 <= k < UNITS:
                    dve.wait_ge(s_exped, k + 1)
                    V.reciprocal(inv_sum[:, k % 2, :], row_sum[:, k % 2, :]).then_inc(s_summed, 1)
                for e in RING.get(k - 1, ()):
                    if e in ON_VECTOR:
                        rotate(e)
                for e in RING.get(k - 2, ()):
                    if e in SPLIT_AT:
                        low(e)
                if k == -8:
                    split_wv()
                if k in (-7, -6):
                    split_wq(k + 7)
                if -5 <= k < -1:
                    split_wo(k + 5)
                if k == FIRST_SLOT:
                    statistics(0)
                    normalize(0)
                elif k in NORM_AT:
                    statistics(NORM_AT[k])
                elif k - 1 in NORM_AT and k - 1 != FIRST_SLOT:
                    normalize(NORM_AT[k - 1])
                if -1 <= k < 9:
                    if k == -1:
                        dve.wait_ge(s_wide_taken, 4)
                        dve.wait_ge(s_small_in, SMALL_IN)
                    form_gates(k + 1)
                if (h := tail_at(k, 17)) is not None:
                    residual(h, 0)
                if (h := tail_at(k, 19)) is not None:
                    residual(h, 1)
                if (h := tail_at(k, 22)) is not None:
                    modulate(h)
                if (h := tail_at(k, 25)) is not None and h < HALVES - 1:
                    dve.wait_ge(s_pay_hi, h + 1)
                    V.tensor_tensor(pay[:, :, E:2 * E], xn[:, :, :], pay[:, :, 0:E], ALU.subtract
                                    ).then_inc(s_pay_lo, 1)
                if (h := tail_at(k, 28)) is not None:
                    gate_choice(h)
                if (h := tail_at(k, 29)) is not None:
                    second_choice(h)
                if (h := tail_at(k, 31)) is not None:
                    placing(h)
                if (h := tail_at(k, 32)) is not None:
                    gate_weights(h)
                for n in SPLIT_X.get(k, ()):
                    if n in VECTOR_X:
                        split_expert(n)

            V.tensor_copy(counts_i[:, :], used_rows[:, :]).then_inc(s_rows_ready, 1)
            link(V.tensor_tensor(counts[:, :], used_rows[:, :], base_s[:, :], ALU.subtract))
            link(V.tensor_scalar(counts[:, :], counts[:, :], float(P - 1), None, ALU.add))
            link(V.tensor_copy(tiles_i[:, :], counts[:, :]))
            link(V.tensor_scalar(tiles_i[:, :], tiles_i[:, :], 7, None, ALU.logical_shift_right))
            V.tensor_copy(xtiles[:, :], tiles_i[:, :])
            link(V.memset(scan[:, :, 0:NX], 0.0))
            link(V.tensor_copy(scan[:, 0, NX:], xtiles[:, :]))
            for j, d in enumerate((1, 2, 4)):
                link(V.tensor_tensor(scan[:, j + 1, NX:], scan[:, j, NX:], scan[:, j, NX - d:2 * NX - d], ALU.add))
            SG = [P, SLOTS, NX]
            no_b = slot_no[:, :].unsqueeze(2).to_broadcast(SG)
            link(V.tensor_tensor(after[:, :, :], no_b, scan[:, 3, NX:].unsqueeze(1).to_broadcast(SG), ALU.is_ge))
            link(V.tensor_reduce(slot_x[:, :], after[:, :, :], X, ALU.add))
            link(V.tensor_tensor(after[:, :, :], after[:, :, :], xtiles[:, :].unsqueeze(1).to_broadcast(SG),
                                  ALU.mult))
            link(V.tensor_reduce(slot_t[:, :], after[:, :, :], X, ALU.add))
            link(V.tensor_scalar(slot_u[:, :], slot_x[:, :], float(NX), None, ALU.is_lt))
            link(V.tensor_scalar(slot_x[:, :], slot_x[:, :], float(NX - 1), None, ALU.min))
            link(V.tensor_tensor(slot_t[:, :], slot_no[:, :], slot_t[:, :], ALU.subtract))
            link(V.tensor_scalar(slot_t[:, :], slot_t[:, :], float(P), float(-UNUSED_ROW), ALU.mult, ALU.add))
            link(S_(slot_row[:, :], slot_x[:, :], float(REGION), slot_t[:, :], ALU.mult, ALU.add))
            link(V.tensor_tensor(slot_row[:, :], slot_row[:, :], slot_u[:, :], ALU.mult))
            link(V.tensor_scalar(slot_row[:, :], slot_row[:, :], float(UNUSED_ROW), None, ALU.add))
            V.tensor_copy(slot_xi[:, :], slot_x[:, :])
            V.tensor_copy(slot_ri[:, :], slot_row[:, :]).then_inc(s_slots_ready, 1)
            for n in range(LATE_X, 3 * NX):
                split_expert(n)
            x_ps_h = ring[0][:, :].bitcast(f16)

            def inner_lo(s, a):
                dve.wait_ge(s_innerT_hi, s + 1)
                V.tensor_tensor(innerT[:, a % 2, 1, :], t_ps[:, :], innerT[:, a % 2, 0, :], ALU.subtract
                                ).then_inc(s_innerT_lo, 1)

            def slot(i, a, head):
                s = i * 4 + a
                dve.wait_ge(s_xT_ps, s + 1)
                if not head or a >= 2:
                    dve.wait_ge(s_gate_ps, s - 1)
                V.tensor_copy(xT[:, a % 2, :], x_ps_h[:, 0:512]).then_inc(s_xT_done, 1)
                if not head or a >= 1:
                    inner_lo(s - 1, a - 1)
                dve.wait_ge(s_silu_g_done, s + 1)
                dve.wait_ge(s_gate_ps, s + 1)
                if not head or a >= 2:
                    dve.wait_ge(s_innerT_ps, s - 1)
                S_(inner[:, a % 2, :], y_ps[a % 2][:, :], 1 / W_SCALE, silu_g[:, a % 2, :], ALU.mult, ALU.mult
                   ).then_inc(s_inner_done, 1)

            for a in range(4):
                slot(0, a, True)
            with dve.Fori(1, SLOTS // 4) as i:
                for a in range(4):
                    slot(i, a, False)
            for a in range(SLOTS % 4):
                slot(SLOTS // 4, a, False)
            inner_lo(SLOTS - 1, SLOTS - 1)
            for n in range(PAIRS):
                dve.wait_ge(s_first_done, n + 1)
                for t in range(2):
                    last = S_(pair[:, n, 1, t, :], pair[:, n, 1, t, :],
                              weight[:, 1, 2 * n + t:2 * n + t + 1], pair[:, n, 0, t, :], ALU.mult, ALU.add)
                link(last)
                V.tensor_tensor(pair[:, n, 0], pair[:, n, 1],
                                gates[:, 3, 2 * n // TILES, :].unsqueeze(1).to_broadcast([P, 2, E]), ALU.mult
                                ).then_inc(s_mixed, 1)

        @block.gpsimd
        def _(pool):
            Q = nc.gpsimd
            Q.memset(power[:, :], -0.5).then_inc(s_pool_ready, 1)
            Q.memset(ones_h[:, :], 1.0).then_inc(s_pool_ready, 1)
            Q.memset(chosen[:, HALF, :], 0.0).then_inc(s_pool_ready, 1)
            Q.memset(keys[:, :, :, 0:WINDOW], 0.0).then_inc(s_pool_ready, 1)
            Q.memset(pad[:, :], 0.0).then_inc(s_pool_ready, 1)
            pool.wait_ge(s_pool_ready, 5)
            Q.memset(pad[:, 2 * E:ROW].bitcast(i32), SKIP).then_inc(s_pool_ready, 1)

            def rsqrt(n):
                pool.wait_ge(s_variance, n + 1)
                Q.tensor_tensor(rstd[:, :], var_eps[:, :], power[:, :], ALU.pow).then_inc(s_rstd_done, 1)

            def set_places(h, c, rows):
                pool.wait_ge(s_pay_lo, h + 1 + (rows is pay_again))
                pool.wait_ge(s_placed, h + 1)
                if h + c and rows is pay:
                    pool.wait_ge(s_routed_rows, (2 * h + c) * 64)
                Q.tensor_copy(rows[:, :, 2 * E:ROW].bitcast(i32),
                              tok_s[:, c, HALF * h:HALF * (h + 1)].unsqueeze(2)).then_inc(s_place_set, 1)

            def route(h, c, rows, tiles):
                pool.wait_ge(s_place_set, 2 * h + c + 1)
                for i in tiles:
                    Q.indirect_dma_start(
                        routed, bass.IndirectOffsetOnAxis(ap=rows_i[:, c, i:i + 1].bitcast(u32), axis=0),
                        rows[:, i, :], None).then_inc(s_routed_rows, 16)

            for k in slot_list():
                for e in RING.get(k - 1, ()):
                    if e in ON_POOL:
                        a, r = arot[:, SPLIT_AT[e] % NA, :], ROPED_AT[e]
                        pool.wait_ge(s_turned, r + 1)
                        pool.wait_ge(s_ring_freed, NTH[e] + 1)
                        Q.tensor_tensor(a, a, zrot[:, r % NZ, :], ALU.add).then_inc(s_rotated_pool, 1)
                if 0 <= k < UNITS:
                    pool.wait_ge(s_summed, k + 1)
                    if k >= 2:
                        pool.wait_ge(s_probs_t, k - 1)
                    Q.tensor_tensor(probs[:, k % 2], exps[:, k % 2],
                                    inv_sum[:, k % 2, :].unsqueeze(2).to_broadcast([P, 4, P]), ALU.mult
                                    ).then_inc(s_normalized, 1)
                for e in RING.get(k, ()):
                    if e in ROPED_AT:
                        r = ROPED_AT[e]
                        half = (e[1] if e[0] == "k" else e[1] // PER_HALF) % 2
                        z = zrot[:, r % NZ, :]
                        pool.wait_ge(s_swapped, r + 1)
                        Q.tensor_tensor(z, z, sin_s[:, half * 512:(half + 1) * 512], ALU.mult
                                        ).then_inc(s_turned, 1)
                if k == -5:
                    pool.wait_ge(s_wq_lo, 2 * EC)
                    Q.memset(valx[:, :, 0, :], 0.0).then_inc(s_pool_ready, 1)
                if k in NORM_AT:
                    rsqrt(NORM_AT[k])
                if 9 <= k % (2 * PER_HALF) < 9 + TILES and 0 <= k < UNITS:
                    b = k // (2 * PER_HALF)
                    t = b * TILES + k % (2 * PER_HALF) - 9
                    if t == b * TILES:
                        pool.wait_ge(s_gates_ready, 1)
                        pool.wait_ge(s_normed, 2 * b + 2)
                    Q.tensor_tensor(x_s[:, t, :], x_s[:, t, :], ga_bo[:, b, :], ALU.add).then_inc(s_residual, 1)
                if k == PER_HALF * (HALVES - 1) + 24:
                    for i, rows in enumerate((pay, pay_again)):
                        pool.wait_ge(s_pay_hi, HALVES + i)
                        Q.tensor_tensor(rows[:, :, E:2 * E], xn[:, :, :], rows[:, :, 0:E], ALU.subtract
                                        ).then_inc(s_pay_lo, 1)
                for n in SPLIT_X.get(k, ()):
                    if n in POOL_X:
                        at = X_ORDER[n] // 3 * PER_X + X_ORDER[n] % 3 * 2048
                        pool.wait_ge(s_expert_scaled, POOL_X.index(n) + 1)
                        Q.tensor_tensor(region[:, at + 1024:at + 2048], xst(n), region[:, at:at + 1024],
                                        ALU.subtract).then_inc(s_expert_lo_pool, 1)
                for d, c, tiles in ((32, 0, (0, 1)), (33, 0, (2, 3)), (34, 1, (0, 1)), (35, 1, (2, 3))):
                    if (h := tail_at(k, d)) is not None and h < HALVES - 1:
                        if tiles[0] == 0:
                            set_places(h, c, pay)
                        route(h, c, pay, tiles)
                if k == PER_HALF * (HALVES - 1) + 32:
                    set_places(HALVES - 1, 0, pay)
                    set_places(HALVES - 1, 1, pay_again)
                    route(HALVES - 1, 0, pay, range(HALF))
                    route(HALVES - 1, 1, pay_again, range(HALF))

            def scatter(s, a):
                pool.wait_ge(s_y_out, s + 1)
                Q.indirect_dma_start(results,
                                     bass.IndirectOffsetOnAxis(ap=x_rows[:, a, 2 * E:ROW].bitcast(u32), axis=0),
                                     y_s[:, a % 2, :], None, bounds_check=TOPK * TOKENS - 1, oob_is_err=False
                                     ).then_inc(s_y_written[s % 2], 16)

            for s in range(SLOTS):
                scatter(s, s % 4)
            for n in range(PAIRS):
                pool.wait_ge(s_mixed, n + 1)
                x2 = x_s[:, 2 * n:2 * n + 2, :]
                Q.tensor_tensor(x2, x2, pair[:, n, 0], ALU.add).then_inc(s_summed_up, 1)


def _pairs_last(a, heads):
    n = a.shape[-1]
    return a.reshape(a.shape[:-1] + (heads, HD // 2, 2)).swapaxes(-1, -2).reshape(a.shape[:-1] + (n,))


def _constants():
    bf16_bits = lambda v: (np.ascontiguousarray(v, np.float32).view(np.uint32) >> 16).astype(np.uint16)
    f32 = np.float32
    half = HD // 2
    freqs = (f32(1.0) / (f32(10000.0) ** (f32(2.0) * np.arange(half, dtype=f32) / f32(HD)))).astype(f32)
    ang = (np.arange(S, dtype=f32)[None, :] * freqs[:, None]).astype(f32)
    cos, sin = np.cos(ang).astype(f32) / f32(W_SCALE), np.sin(ang).astype(f32) / f32(W_SCALE)
    r = np.arange(64)[:, None]
    c = np.arange(64)[None, :]
    own, prev = np.where(c <= r, 0, MASKED), np.where(c >= r, 0, MASKED)
    even, odd = np.hstack([own, prev]), np.hstack([prev, own])
    first = np.hstack([own, np.full_like(prev, MASKED)])
    tile = lambda e, o: np.tile(np.hstack([e, e, o, o]), (2, 1))
    masks = bf16_bits(np.stack([tile(even, odd), tile(first, odd)], 1))
    p = np.arange(P)
    tokens = (np.arange(ALL)[None, None, :] * P + p[:, None, None] + np.arange(TOPK)[None, :, None] * TOKENS)
    wide = lambda v: np.ascontiguousarray(np.broadcast_to(np.asarray(v, f32), (P, len(v))))
    return dict(
        cos_t=np.vstack([cos, cos]), sin_t=np.vstack([-sin, sin]), mask_t=masks,
        ident=np.eye(P, dtype=f32), ident16=np.eye(P, dtype=np.float16), identb=bf16_bits(np.eye(P)),
        lower=np.triu(np.ones((P, P)), 1).astype(np.float16), tokens=tokens.astype(np.int32),
        bases=wide(np.arange(NX) * REGION), reverse=wide(NX - np.arange(NX)), slot_nos=wide(np.arange(SLOTS)))


def kernel(**inputs):
    import concourse.bacc as _bacc
    from concourse import mybir as _mybir
    from concourse.bass_utils import run_bass_kernel_spmd as _run

    a = {k: np.asarray(v) for k, v in inputs.items()}
    column = lambda v: v.reshape(-1, HD).T
    given = dict(
        x=a["L0_attn_x"].reshape(TOKENS, E),
        wq=_pairs_last(a["L0_attn_Wq"], NQ), bq=column(_pairs_last(a["L0_attn_bq"], NQ)),
        wk=_pairs_last(a["L0_attn_Wk"], NKV), bk=column(_pairs_last(a["L0_attn_bk"], NKV)),
        wv=a["L0_attn_Wv"], bv=column(a["L0_attn_bv"]), wo=a["L0_attn_Wo"], bo=a["L0_attn_bo"],
        w_gate=a["L0_ffn_w_gate"], w1=a["L0_ffn_w1"], w3=a["L0_ffn_w3"], w2=a["L0_ffn_w2"],
        c_t=a["L0_c"].reshape(B, EC, P).transpose(2, 1, 0), wmod=a["L0_wmod"])
    given.update(_constants())
    nc = _bacc.Bacc("TRN2", target_bir_lowering=False, num_devices=1)
    arrays, args = {}, {}
    for name, v in given.items():
        v = np.ascontiguousarray(v)
        arrays[f"in_{name}"] = v
        args[name] = nc.dram_tensor(f"in_{name}", v.shape, _mybir.dt.from_np(v.dtype), kind="ExternalInput").ap()
    out = nc.dram_tensor("out", (TOKENS, E), _mybir.dt.float32, kind="ExternalOutput").ap()
    layer_kernel(nc, out=out, **args)
    r = _run(nc, [arrays], core_ids=[0])
    return r.results[0]["out"].reshape(B, S, E)
```
